# Optimizing a Trainium2 kernel written in Bass

```python
import numpy as np
import jax
import jax.numpy as jnp

def _softmax(x, axis=-1):
    return jax.nn.softmax(x, axis=axis)

def _gelu(x):
    return jax.nn.gelu(x, approximate=True)

def _silu(x):
    return jax.nn.silu(x)

def _sigmoid(x):
    return jax.nn.sigmoid(x)

def _layernorm(x, axis=-1, eps=1e-05):
    m = jnp.mean(x, axis=axis, keepdims=True)
    v = jnp.var(x, axis=axis, keepdims=True)
    return (x - m) / jnp.sqrt(v + eps)

def _scatter_add(tgt, idx, src, axis=0):
    return tgt.at[idx].add(src)

def _segment_sum(src, seg, n):
    return jax.ops.segment_sum(src, seg, n)
kernel_name = 'mk_seq_postln_d2_jaxref_r4_8a5948'

def setup_inputs(seed: int=0):
    np.random.seed(seed)
    _w = jnp.asarray

    def _L0_attn_setup():
        import jax, jax.numpy as jnp
        import numpy as np
        D_MODEL = 256
        HEADS = 4
        DK = 256
        DV = 512
        HDK = DK // HEADS
        HDV = DV // HEADS
        LOW_RANK = 16
        CHUNK = 64
        GATE_NORM = 16.0
        EPS = 1e-05

        def _gla_chunked(q, k, v, g):
            B, H, T, _ = q.shape
            NC = T // CHUNK
            scale = HDK ** (-0.5)

            def to_chunks(t, d):
                return t.reshape(B, H, NC, CHUNK, d).transpose(2, 0, 1, 3, 4)
            qc = to_chunks(q, HDK)
            kc = to_chunks(k, HDK)
            vc = to_chunks(v, HDV)
            bc = jnp.cumsum(to_chunks(g, HDK), axis=-2)
            mask = jnp.tril(jnp.ones((CHUNK, CHUNK), bool))

            def step(S, inp):
                qb, kb, vb, bb = inp
                qg = qb * jnp.exp(bb) * scale
                kd = kb * jnp.exp(-bb)
                A = jnp.einsum('bhtd,bhsd->bhts', qg, kd)
                A = jnp.where(mask, A, 0.0)
                o = jnp.einsum('bhts,bhsv->bhtv', A, vb) + jnp.einsum('bhtd,bhdv->bhtv', qg, S)
                b_last = bb[:, :, -1:, :]
                kg = kb * jnp.exp(b_last - bb)
                S = S * jnp.exp(b_last[:, :, 0, :])[..., None] + jnp.einsum('bhtd,bhtv->bhdv', kg, vb)
                return (S, o)
            S0 = jnp.zeros((B, H, HDK, HDV), q.dtype)
            _, o = jax.lax.scan(step, S0, (qc, kc, vc, bc))
            return o.transpose(1, 2, 0, 3, 4).reshape(B, H, T, HDV)
        key = jax.random.key(seed)
        ks = jax.random.split(key, 10)
        gain = 2.0 ** (-2.5)

        def xavier(k, shape):
            lim = gain * np.sqrt(6.0 / (shape[0] + shape[1]))
            return jax.random.uniform(k, shape, jnp.float32, -lim, lim)
        return {'x': jax.random.normal(ks[0], (2, 512, D_MODEL), jnp.float32), 'Wq': xavier(ks[1], (D_MODEL, DK)), 'Wk': xavier(ks[2], (D_MODEL, DK)), 'Wv': xavier(ks[3], (D_MODEL, DV)), 'Wg': xavier(ks[4], (D_MODEL, DV)), 'Wgk1': xavier(ks[5], (D_MODEL, LOW_RANK)), 'Wgk2': xavier(ks[6], (LOW_RANK, DK)), 'bgk2': jnp.zeros((DK,), jnp.float32), 'Wo': xavier(ks[7], (DV, D_MODEL)), 'rms_w': jnp.ones((HDV,), jnp.float32)}
    _L0_attn_in = _L0_attn_setup()

    def _L0_ffn_setup():
        import jax, jax.numpy as jnp
        import numpy as np
        LN_EPS = 1e-05

        def _swiglu(h, w_gate_up, w_down):
            gu = h @ w_gate_up.T
            gate, up = jnp.split(gu, 2, axis=-1)
            return jax.nn.silu(gate) * up @ w_down.T
        key = jax.random.key(seed)
        ks = jax.random.split(key, 6)
        d_model, d_ff, E = (256, 1024, 8)
        shared_d_ff = d_ff // 4
        routed_d_ff = d_ff - shared_d_ff
        B, S = (4, 512)
        x = jax.random.normal(ks[0], (B, S, d_model), dtype=jnp.float32)
        ln_gamma = jnp.ones((d_model,), jnp.float32)
        ln_beta = jnp.zeros((d_model,), jnp.float32)
        router_w = jax.random.normal(ks[1], (E, d_model), jnp.float32) * 0.02
        gate_up_w = jax.random.normal(ks[2], (E, 2 * routed_d_ff, d_model), jnp.float32) * (1.0 / np.sqrt(d_model))
        down_w = jax.random.normal(ks[3], (E, d_model, routed_d_ff), jnp.float32) * (1.0 / np.sqrt(routed_d_ff))
        shared_gate_up_w = jax.random.normal(ks[4], (2 * shared_d_ff, d_model), jnp.float32) * (1.0 / np.sqrt(d_model))
        shared_down_w = jax.random.normal(ks[5], (d_model, shared_d_ff), jnp.float32) * (1.0 / np.sqrt(shared_d_ff))
        return dict(x=x, ln_gamma=ln_gamma, ln_beta=ln_beta, router_w=router_w, gate_up_w=gate_up_w, down_w=down_w, shared_gate_up_w=shared_gate_up_w, shared_down_w=shared_down_w)
    _L0_ffn_in = _L0_ffn_setup()

    def _L1_attn_setup():
        import jax, jax.numpy as jnp
        import numpy as np
        import math
        D_MODEL = 256
        N_HEADS = 16
        HEAD_DIM = D_MODEL // N_HEADS
        LAMBDA_INIT = 0.8 - 0.6 * math.exp(-0.3 * 0)
        EPS = 1e-06

        def _rope_cache(seq_len, head_dim, dtype):
            half = head_dim // 2
            inv_freq = 1.0 / 10000.0 ** (jnp.arange(half, dtype=jnp.float32) / max(half, 1))
            ang = jnp.arange(seq_len, dtype=jnp.float32)[:, None] * inv_freq[None, :]
            return (jnp.cos(ang).astype(dtype)[None, None], jnp.sin(ang).astype(dtype)[None, None])

        def _apply_rope(x, cos, sin):
            half = x.shape[-1] // 2
            x1, x2 = (x[..., :half], x[..., half:])
            return jnp.concatenate([x1 * cos - x2 * sin, x1 * sin + x2 * cos], axis=-1)
        key = jax.random.key(seed)
        ks = jax.random.split(key, 16)
        B, S, D = (2, 512, D_MODEL)
        s = 0.02
        return {'x': jax.random.normal(ks[0], (B, S, D), jnp.float32), 'Wq': jax.random.normal(ks[1], (2 * D, D), jnp.float32) * s, 'bq': jnp.zeros((2 * D,), jnp.float32), 'Wk': jax.random.normal(ks[2], (2 * D, D), jnp.float32) * s, 'bk': jnp.zeros((2 * D,), jnp.float32), 'Wv': jax.random.normal(ks[3], (D, D), jnp.float32) * s, 'bv': jnp.zeros((D,), jnp.float32), 'Wo': jax.random.normal(ks[4], (D, D), jnp.float32) * s, 'bo': jnp.zeros((D,), jnp.float32), 'head_norm_w': jnp.ones((N_HEADS, HEAD_DIM), jnp.float32), 'lq1': jax.random.normal(ks[5], (N_HEADS, HEAD_DIM), jnp.float32) * 0.1, 'lk1': jax.random.normal(ks[6], (N_HEADS, HEAD_DIM), jnp.float32) * 0.1, 'lq2': jax.random.normal(ks[7], (N_HEADS, HEAD_DIM), jnp.float32) * 0.1, 'lk2': jax.random.normal(ks[8], (N_HEADS, HEAD_DIM), jnp.float32) * 0.1}
    _L1_attn_in = _L1_attn_setup()

    def _L1_ffn_setup():
        import jax, jax.numpy as jnp
        import numpy as np
        B, S, D, H, DOUT, E, K = (4, 512, 256, 256, 256, 8, 2)
        key = jax.random.key(seed)
        k1, k2, k3, k4 = jax.random.split(key, 4)
        x = jax.random.normal(k1, (B, S, D), dtype=jnp.float32)
        Wr = jax.random.normal(k2, (D, E), dtype=jnp.float32) * 0.02
        Wi = jax.random.normal(k3, (E, D, H), dtype=jnp.float32) * 0.02
        Wo = jax.random.normal(k4, (E, H, DOUT), dtype=jnp.float32) * 0.02
        return {'x': x, 'Wr': Wr, 'Wi': Wi, 'Wo': Wo}
    _L1_ffn_in = _L1_ffn_setup()
    _d = {'L0_attn_x': _L0_attn_in['x'], 'L0_attn_Wq': _L0_attn_in['Wq'], 'L0_attn_Wk': _L0_attn_in['Wk'], 'L0_attn_Wv': _L0_attn_in['Wv'], 'L0_attn_Wg': _L0_attn_in['Wg'], 'L0_attn_Wgk1': _L0_attn_in['Wgk1'], 'L0_attn_Wgk2': _L0_attn_in['Wgk2'], 'L0_attn_bgk2': _L0_attn_in['bgk2'], 'L0_attn_Wo': _L0_attn_in['Wo'], 'L0_attn_rms_w': _L0_attn_in['rms_w'], 'L0_ffn_ln_gamma': _L0_ffn_in['ln_gamma'], 'L0_ffn_ln_beta': _L0_ffn_in['ln_beta'], 'L0_ffn_router_w': _L0_ffn_in['router_w'], 'L0_ffn_gate_up_w': _L0_ffn_in['gate_up_w'], 'L0_ffn_down_w': _L0_ffn_in['down_w'], 'L0_ffn_shared_gate_up_w': _L0_ffn_in['shared_gate_up_w'], 'L0_ffn_shared_down_w': _L0_ffn_in['shared_down_w'], 'L1_attn_Wq': _L1_attn_in['Wq'], 'L1_attn_bq': _L1_attn_in['bq'], 'L1_attn_Wk': _L1_attn_in['Wk'], 'L1_attn_bk': _L1_attn_in['bk'], 'L1_attn_Wv': _L1_attn_in['Wv'], 'L1_attn_bv': _L1_attn_in['bv'], 'L1_attn_Wo': _L1_attn_in['Wo'], 'L1_attn_bo': _L1_attn_in['bo'], 'L1_attn_head_norm_w': _L1_attn_in['head_norm_w'], 'L1_attn_lq1': _L1_attn_in['lq1'], 'L1_attn_lk1': _L1_attn_in['lk1'], 'L1_attn_lq2': _L1_attn_in['lq2'], 'L1_attn_lk2': _L1_attn_in['lk2'], 'L1_ffn_Wr': _L1_ffn_in['Wr'], 'L1_ffn_Wi': _L1_ffn_in['Wi'], 'L1_ffn_Wo': _L1_ffn_in['Wo']}
    _x0 = _d['L0_attn_x']
    _d['L0_attn_x'] = jax.random.normal(jax.random.fold_in(jax.random.key(seed), 1), (4, 1024, 256), dtype=_x0.dtype)
    del _x0
    return _d

def reference(L0_attn_x, L0_attn_Wq, L0_attn_Wk, L0_attn_Wv, L0_attn_Wg, L0_attn_Wgk1, L0_attn_Wgk2, L0_attn_bgk2, L0_attn_Wo, L0_attn_rms_w, L0_ffn_ln_gamma, L0_ffn_ln_beta, L0_ffn_router_w, L0_ffn_gate_up_w, L0_ffn_down_w, L0_ffn_shared_gate_up_w, L0_ffn_shared_down_w, L1_attn_Wq, L1_attn_bq, L1_attn_Wk, L1_attn_bk, L1_attn_Wv, L1_attn_bv, L1_attn_Wo, L1_attn_bo, L1_attn_head_norm_w, L1_attn_lq1, L1_attn_lk1, L1_attn_lq2, L1_attn_lk2, L1_ffn_Wr, L1_ffn_Wi, L1_ffn_Wo):

    def _L0_attn_ref(x, Wq, Wk, Wv, Wg, Wgk1, Wgk2, bgk2, Wo, rms_w):
        import jax, jax.numpy as jnp
        import numpy as np
        D_MODEL = 256
        HEADS = 4
        DK = 256
        DV = 512
        HDK = DK // HEADS
        HDV = DV // HEADS
        LOW_RANK = 16
        CHUNK = 64
        GATE_NORM = 16.0
        EPS = 1e-05

        def _gla_chunked(q, k, v, g):
            B, H, T, _ = q.shape
            NC = T // CHUNK
            scale = HDK ** (-0.5)

            def to_chunks(t, d):
                return t.reshape(B, H, NC, CHUNK, d).transpose(2, 0, 1, 3, 4)
            qc = to_chunks(q, HDK)
            kc = to_chunks(k, HDK)
            vc = to_chunks(v, HDV)
            bc = jnp.cumsum(to_chunks(g, HDK), axis=-2)
            mask = jnp.tril(jnp.ones((CHUNK, CHUNK), bool))

            def step(S, inp):
                qb, kb, vb, bb = inp
                qg = qb * jnp.exp(bb) * scale
                kd = kb * jnp.exp(-bb)
                A = jnp.einsum('bhtd,bhsd->bhts', qg, kd)
                A = jnp.where(mask, A, 0.0)
                o = jnp.einsum('bhts,bhsv->bhtv', A, vb) + jnp.einsum('bhtd,bhdv->bhtv', qg, S)
                b_last = bb[:, :, -1:, :]
                kg = kb * jnp.exp(b_last - bb)
                S = S * jnp.exp(b_last[:, :, 0, :])[..., None] + jnp.einsum('bhtd,bhtv->bhdv', kg, vb)
                return (S, o)
            S0 = jnp.zeros((B, H, HDK, HDV), q.dtype)
            _, o = jax.lax.scan(step, S0, (qc, kc, vc, bc))
            return o.transpose(1, 2, 0, 3, 4).reshape(B, H, T, HDV)
        B, T, _ = x.shape
        q = (x @ Wq).reshape(B, T, HEADS, HDK).transpose(0, 2, 1, 3)
        k = (x @ Wk).reshape(B, T, HEADS, HDK).transpose(0, 2, 1, 3)
        v = (x @ Wv).reshape(B, T, HEADS, HDV).transpose(0, 2, 1, 3)
        gk = x @ Wgk1 @ Wgk2 + bgk2
        g = jax.nn.log_sigmoid(gk.astype(jnp.float32)) / GATE_NORM
        g = g.reshape(B, T, HEADS, HDK).transpose(0, 2, 1, 3)
        o = _gla_chunked(q, k, v, g)
        o = o.transpose(0, 2, 1, 3)
        o = o * jax.lax.rsqrt(jnp.mean(o * o, axis=-1, keepdims=True) + EPS) * rms_w
        o = o.reshape(B, T, HEADS * HDV)
        o = o * jax.nn.silu(x @ Wg)
        return o @ Wo

    def _L0_ffn_ref(x, ln_gamma, ln_beta, router_w, gate_up_w, down_w, shared_gate_up_w, shared_down_w):
        import jax, jax.numpy as jnp
        import numpy as np
        LN_EPS = 1e-05

        def _swiglu(h, w_gate_up, w_down):
            gu = h @ w_gate_up.T
            gate, up = jnp.split(gu, 2, axis=-1)
            return jax.nn.silu(gate) * up @ w_down.T
        B, S, D = x.shape
        E = router_w.shape[0]
        top_k = 2
        xt = x.reshape(-1, D)
        mu = jnp.mean(xt, axis=-1, keepdims=True)
        var = jnp.mean(jnp.square(xt - mu), axis=-1, keepdims=True)
        normed = (xt - mu) * jax.lax.rsqrt(var + LN_EPS) * ln_gamma + ln_beta
        logits = normed.astype(jnp.float32) @ router_w.T
        probs = jax.nn.softmax(logits, axis=-1)
        top_v, top_i = jax.lax.top_k(probs, top_k)
        gates = jax.nn.softmax(top_v, axis=-1)
        comb = jnp.sum(jax.nn.one_hot(top_i, E, dtype=gates.dtype) * gates[..., None], axis=1)
        out = jnp.zeros_like(normed)
        for e in range(E):
            y = _swiglu(normed, gate_up_w[e], down_w[e])
            out = out + comb[:, e, None] * y
        out = out + _swiglu(normed, shared_gate_up_w, shared_down_w)
        return out.reshape(B, S, D)

    def _L1_attn_ref(x, Wq, bq, Wk, bk, Wv, bv, Wo, bo, head_norm_w, lq1, lk1, lq2, lk2):
        import jax, jax.numpy as jnp
        import numpy as np
        import math
        D_MODEL = 256
        N_HEADS = 16
        HEAD_DIM = D_MODEL // N_HEADS
        LAMBDA_INIT = 0.8 - 0.6 * math.exp(-0.3 * 0)
        EPS = 1e-06

        def _rope_cache(seq_len, head_dim, dtype):
            half = head_dim // 2
            inv_freq = 1.0 / 10000.0 ** (jnp.arange(half, dtype=jnp.float32) / max(half, 1))
            ang = jnp.arange(seq_len, dtype=jnp.float32)[:, None] * inv_freq[None, :]
            return (jnp.cos(ang).astype(dtype)[None, None], jnp.sin(ang).astype(dtype)[None, None])

        def _apply_rope(x, cos, sin):
            half = x.shape[-1] // 2
            x1, x2 = (x[..., :half], x[..., half:])
            return jnp.concatenate([x1 * cos - x2 * sin, x1 * sin + x2 * cos], axis=-1)
        B, S, D = x.shape
        H, hd = (N_HEADS, HEAD_DIM)
        dtype = x.dtype
        q = (x @ Wq.T + bq).reshape(B, S, H, 2 * hd).transpose(0, 2, 1, 3)
        k = (x @ Wk.T + bk).reshape(B, S, H, 2 * hd).transpose(0, 2, 1, 3)
        v = (x @ Wv.T + bv).reshape(B, S, H, hd).transpose(0, 2, 1, 3)
        q1, q2 = (q[..., :hd], q[..., hd:])
        k1, k2 = (k[..., :hd], k[..., hd:])
        cos, sin = _rope_cache(S, hd, dtype)
        q1, q2 = (_apply_rope(q1, cos, sin), _apply_rope(q2, cos, sin))
        k1, k2 = (_apply_rope(k1, cos, sin), _apply_rope(k2, cos, sin))
        scale = 1.0 / math.sqrt(hd)
        s1 = jnp.einsum('bhqd,bhkd->bhqk', q1, k1) * scale
        s2 = jnp.einsum('bhqd,bhkd->bhqk', q2, k2) * scale
        causal = jnp.triu(jnp.ones((S, S), bool), k=1)
        neg = jnp.finfo(dtype).min
        s1 = jnp.where(causal, neg, s1)
        s2 = jnp.where(causal, neg, s2)
        a1 = jax.nn.softmax(s1, axis=-1)
        a2 = jax.nn.softmax(s2, axis=-1)
        lam = LAMBDA_INIT + jnp.exp(jnp.sum(lq1 * lk1, -1)) - jnp.exp(jnp.sum(lq2 * lk2, -1))
        attn = a1 - lam.astype(dtype)[None, :, None, None] * a2
        out = jnp.einsum('bhqk,bhkd->bhqd', attn, v)
        rms = jnp.mean(out * out, axis=-1, keepdims=True)
        out = out * jax.lax.rsqrt(rms + EPS)
        out = out * head_norm_w[None, :, None, :]
        out = out * (1.0 - LAMBDA_INIT)
        out = out.transpose(0, 2, 1, 3).reshape(B, S, D)
        return out @ Wo.T + bo

    def _L1_ffn_ref(x, Wr, Wi, Wo):
        import jax, jax.numpy as jnp
        import numpy as np
        B, S, D, H, DOUT, E, K = (4, 512, 256, 256, 256, 8, 2)
        b, s, d = x.shape
        e_cnt, _, h = Wi.shape
        dout = Wo.shape[2]
        xf = x.reshape(-1, d)
        T = xf.shape[0]
        probs = jax.nn.softmax(xf @ Wr, axis=-1)
        topk_p, topk_i = jax.lax.top_k(probs, K)
        mask = topk_i[:, :, None] == jnp.arange(e_cnt)[None, None, :]
        hmix = jnp.zeros((T, K, h), dtype=xf.dtype)
        for e in range(e_cnt):
            he = xf @ Wi[e]
            hmix = hmix + jnp.where(mask[:, :, e][:, :, None], he[:, None, :], 0.0)
        o = jnp.zeros((T, K, dout), dtype=xf.dtype)
        for e in range(e_cnt):
            oe = jnp.einsum('tkh,hd->tkd', hmix, Wo[e])
            o = o + jnp.where(mask[:, :, e][:, :, None], oe, 0.0)
        out = jnp.sum(o * topk_p[:, :, None], axis=1)
        return out.reshape(b, s, dout)
    x = L0_attn_x
    x = _layernorm(x + _L0_attn_ref(x, L0_attn_Wq, L0_attn_Wk, L0_attn_Wv, L0_attn_Wg, L0_attn_Wgk1, L0_attn_Wgk2, L0_attn_bgk2, L0_attn_Wo, L0_attn_rms_w), axis=-1)
    x = _layernorm(x + _L0_ffn_ref(x, L0_ffn_ln_gamma, L0_ffn_ln_beta, L0_ffn_router_w, L0_ffn_gate_up_w, L0_ffn_down_w, L0_ffn_shared_gate_up_w, L0_ffn_shared_down_w), axis=-1)
    x = _layernorm(x + _L1_attn_ref(x, L1_attn_Wq, L1_attn_bq, L1_attn_Wk, L1_attn_bk, L1_attn_Wv, L1_attn_bv, L1_attn_Wo, L1_attn_bo, L1_attn_head_norm_w, L1_attn_lq1, L1_attn_lk1, L1_attn_lq2, L1_attn_lk2), axis=-1)
    x = _layernorm(x + _L1_ffn_ref(x, L1_ffn_Wr, L1_ffn_Wi, L1_ffn_Wo), axis=-1)
    return x

_drawn_inputs = setup_inputs


def setup_inputs(seed=0):
    import zlib

    import numpy as np

    out = dict(_drawn_inputs(seed))
    spreads = {'L0_attn_bgk2': (0.0, 0.717),
     'L0_attn_rms_w': (1.0, 0.6),
     'L0_ffn_ln_gamma': (1.0, 0.2),
     'L0_ffn_ln_beta': (0.0, 0.1),
     'L1_attn_bq': (0.0, 0.8),
     'L1_attn_bk': (0.0, 0.8),
     'L1_attn_bv': (0.0, 0.1),
     'L1_attn_bo': (0.0, 0.1),
     'L1_attn_head_norm_w': (1.0, 0.2)}
    factors = {'L0_attn_Wgk1': 30.267,
     'L0_attn_Wgk2': 28.132,
     'L1_attn_Wq': 6.992,
     'L1_attn_Wk': 6.592,
     'L1_attn_lq1': 8.0,
     'L1_attn_lk1': 8.0,
     'L1_attn_lq2': 8.0,
     'L1_attn_lk2': 8.0}
    for name, (base, spread) in spreads.items():
        noise = np.random.default_rng([zlib.crc32(name.encode()), seed]).standard_normal(out[name].shape)
        drawn = base * np.exp(spread * noise) if base else spread * noise
        out[name] = jnp.asarray(drawn.astype(out[name].dtype))
    for name, factor in factors.items():
        out[name] = (out[name] * factor).astype(out[name].dtype)
    return out
```

```python
from contextlib import ExitStack

import numpy as np
import concourse.bass as bass
from concourse import mybir

F32 = mybir.dt.float32
BF16 = mybir.dt.bfloat16
I32 = mybir.dt.int32
ALU = mybir.AluOpType
ACT = mybir.ActivationFunctionType
AX = mybir.AxisListType.X


class Op:

    def __init__(self, eng, fn, waits, step=1):
        self.eng, self.fn, self.waits, self.step = eng, fn, waits, step
        self.sem, self.value, self.marked = None, 0, False


def flat(x):
    out = []
    for y in x:
        if isinstance(y, (list, tuple)):
            out += flat(y)
        elif y is not None:
            out.append(y)
    return out


class Queues:

    ENGINES = ("pe", "dve", "act", "pool", "sp")

    def __init__(self, nc, ctx, ndma):
        self.q = {e: [] for e in self.ENGINES}
        self.sem = {e: ctx.enter_context(nc.semaphore(f"done_{e}")) for e in self.ENGINES}
        self.dsem = [ctx.enter_context(nc.semaphore(f"dma{i}")) for i in range(ndma)]
        self.dlast = [None] * ndma
        self.n = 0

    def add(self, eng, fn, *waits):
        op = Op(eng, fn, flat(waits))
        op.sem = self.sem[eng]
        for w in op.waits:
            w.marked = True
        self.q[eng].append(op)
        return op

    def dma(self, eng, out, in_, *waits):
        k = self.n % len(self.dsem)
        self.n += 1
        waits = flat(waits) + ([self.dlast[k]] if self.dlast[k] else [])
        op = Op(eng, lambda e: e.dma_start(out, in_), waits, 16)
        op.sem, op.marked = self.dsem[k], True
        op.value = 16 + (self.dlast[k].value if self.dlast[k] else 0)
        for w in waits:
            w.marked = True
        self.dlast[k] = op
        self.q[eng].append(op)
        return op

    def last(self):
        out = [d for d in self.dlast if d]
        for e in self.ENGINES:
            own = [o for o in self.q[e] if o.step == 1]
            if own:
                out.append(own[-1])
        return out

    def barrier(self):
        end = self.last()
        for e in self.ENGINES:
            self.q[e].append(Op(e, None, [o for o in end]))
        for o in end:
            o.marked = True

    def emit(self, nc, ctx):
        for e in self.ENGINES:
            n = 0
            for o in self.q[e]:
                if o.step == 1 and o.fn and o.marked:
                    n += 1
                    o.value = n
        block = ctx.enter_context(nc.Block())
        heads = dict(pe=block.tensor, dve=block.vector, act=block.scalar, pool=block.gpsimd, sp=block.sync)
        for name in self.ENGINES:
            ops = self.q[name]

            def body(e, ops=ops):
                seen = {}
                for o in ops:
                    for w in o.waits:
                        k = id(w.sem)
                        if seen.get(k, 0) < w.value:
                            e.wait_ge(w.sem, w.value)
                            seen[k] = w.value
                    if o.fn:
                        ins = o.fn(e)
                        if o.marked:
                            ins.then_inc(o.sem, o.step)

            heads[name](body)


def program(nc, A, out, stages=9, dbg=None):
    with ExitStack() as ctx:
        def sb(name, shape, dt=F32, c=ctx):
            return c.enter_context(nc.sbuf_tensor(name, shape, dt))

        Q = Queues(nc, ctx, 40)
        PS = ctx.enter_context(nc.psum_tensor("PS", [128, 8, 512], F32))

        def pe(fn, *w): return Q.add("pe", fn, *w)
        def dve(fn, *w): return Q.add("dve", fn, *w)
        def act(fn, *w): return Q.add("act", fn, *w)
        def pool(fn, *w): return Q.add("pool", fn, *w)

        def mm(o, l, r, start=True, stop=True, w=(), skip=False):
            return pe(lambda e: e.matmul(o, l, r, start=start, stop=stop, skip_group_check=skip), *w)

        def tr(o, i, w=()):
            n = i.shape[0]
            return pe(lambda e: e.transpose(o, i, IDN[0:n, 0:n]), *w)

        def load(name, dst, src, *w, eng="sp"):
            return Q.dma(eng, dst, src, *w)

        banks = [(k, []) for k in range(8)]

        def take():
            return banks.pop(0)

        def give(k, *ops):
            banks.append((k, flat(ops)))

        X = sb("X", [128, 32, 256])
        XT = sb("XT", [128, 2, 4096])
        IDN = sb("IDN", [128, 128])
        COMB = sb("COMB", [128, 32, 8])
        EPS = sb("EPS", [128, 4])
        ST = sb("ST", [128, 4, 6])
        MV = sb("MV", [128, 4, 2])
        LV = sb("LV", [128, 4])
        RS = sb("RS", [128, 4])
        IREV = sb("IREV", [128, 8])
        l_eps = Q.dma("sp", EPS[:], A["c_eps"])
        l_idn = Q.dma("sp", IDN[:], A["c_idn"])
        l_irev = Q.dma("sp", IREV[:], A["c_irev"])

        def rsqrt(dst, src, tmp, scale, epscol, *w):
            a = act(lambda e: e.activation(tmp, src, ACT.Ln, bias=EPS[:, epscol:epscol + 1], scale=scale), l_eps, *w)
            return act(lambda e: e.activation(dst, tmp, ACT.Exp, scale=-0.5), a)

        ln_state = {"free": []}

        def layernorm(tiles, outs, *w):
            ops = []
            for i, t in enumerate(tiles):
                a = dve(lambda e, i=i, t=t: e.bn_stats(ST[:, i, :], t), *w, ln_state["free"])
                ops.append(a)
            for i in range(len(tiles)):
                a = dve(lambda e, i=i: e.bn_aggr(MV[:, i, :], ST[:, i, :]), ops[i])
            n = len(tiles)
            r = rsqrt(RS[:, 0:n], MV[:, 0:n, 1], LV[:, 0:n], 1.0, 0, a)
            res = []
            for i, (t, o) in enumerate(zip(tiles, outs)):
                res.append(dve(lambda e, i=i, t=t, o=o: e.tensor_scalar(
                    o, t, MV[:, i, 0:1], RS[:, i:i + 1], ALU.subtract, ALU.mult), r))
            ln_state["free"] = [res[-1]]
            return res

        xv = X[:].rearrange("p (b t) d -> p b t d", b=4)
        xtv = XT[:].rearrange("p k (b s) -> p k b s", b=4)
        with ExitStack() as c1:
            s1 = lambda n, s, d=F32: sb(n, s, d, c1)
            WQ, WK = s1("WQ", [128, 2, 256]), s1("WK", [128, 2, 256])
            WV, WG = s1("WV", [128, 2, 512]), s1("WG", [128, 2, 512])
            W1 = s1("W1", [128, 2, 16])
            W2 = s1("W2", [17, 256])
            WO = s1("WO", [128, 4, 256])
            RMS = s1("RMS", [128, 512])
            GAM, BET = s1("GAM", [128, 256]), s1("BET", [128, 256])
            TRI = s1("TRI", [128, 128])
            MSK = s1("MSK", [128, 128], I32)
            XG = s1("XG", [32, 512])
            GA, GE, GG = s1("GA", [128, 1024]), s1("GE", [128, 1024]), s1("GG", [128, 1024])
            EP, EM = s1("EP", [128, 2, 512]), s1("EM", [128, 2, 512])
            QG = s1("QG", [128, 2, 2, 512])
            KD, KG = s1("KD", [128, 2, 512]), s1("KG", [128, 2, 512])
            KZ = s1("KZ", [128, 2, 4, 256])
            V = s1("V", [128, 4, 512])
            AT = s1("AT", [128, 16, 128])
            SG = s1("SG", [128, 4, 512])
            Y = s1("Y", [128, 4, 512])
            YT = s1("YT", [128, 16, 128])
            S = s1("S", [128, 2, 2, 4, 128])
            SQ = s1("SQ", [128, 128])
            SS, SL, SR = s1("SS", [128, 16]), s1("SL", [128, 16]), s1("SR", [128, 16])
            NR = s1("NR", [128, 4, 256])

            lx = []
            for t in range(8):
                lx.append(Q.dma("sp", xtv[:, :, :, 128 * t:128 * t + 128].rearrange("p k b s -> p (k b) s"), A["xt"][t]))
                if t == 0:
                    l_w1 = Q.dma("sp", W1[:], A["wgk1"])
                    l_w2 = [Q.dma("sp", W2[0:16, :], A["wgk2"]), Q.dma("sp", W2[16:17, :], A["bgk2"])]
                    l_q = Q.dma("sp", WQ[:], A["wq0"])
                    l_k = Q.dma("sp", WK[:], A["wk0"])
                    l_v = Q.dma("sp", WV[:], A["wv0"])
                    l_g = Q.dma("sp", WG[:], A["wg0"])
                    l_tri = Q.dma("sp", TRI[:], A["c_tri"])
                    l_msk = Q.dma("sp", MSK[:], A["c_msk"])
                    l_o = Q.dma("sp", WO[:], A["wo0"])
                    l_rms = Q.dma("sp", RMS[:], A["rms"])
                    l_gam = Q.dma("sp", GAM[:], A["gam"])
                    l_bet = Q.dma("sp", BET[:], A["bet"])
                    l_X = Q.dma("sp", X[:], A["x"])

            z_xg = pool(lambda e: e.memset(XG[:], 1.0))
            z_qg = pool(lambda e: e.memset(QG[:], 0.0))
            z_kz = pool(lambda e: e.memset(KZ[:], 0.0))
            z_at = pool(lambda e: e.memset(AT[:], 0.0))
            z_s = pool(lambda e: e.memset(S[:], 0.0))

            f = {k: [] for k in "xg ga ge gg ep em qg kd kg kz v at sg y yt sr nr".split()}
            s_ready = [z_s] * 8
            s_read = [[] for _ in range(8)]
            for t in range(8):
                xt = [xtv[:, k, :, 128 * t:128 * t + 128] for k in range(2)]
                bt = lambda k: PS[:, k, :].rearrange("p (b s) -> p b s", b=4)
                kb, fr = take()
                mm(PS[0:16, kb, :].rearrange("p (b s) -> p b s", b=4), W1[:, 0, :], xt[0], True, False, [fr, lx[t], l_w1])
                a = mm(PS[0:16, kb, :].rearrange("p (b s) -> p b s", b=4), W1[:, 1, :], xt[1], False, True)
                xg = act(lambda e, kb=kb: e.activation(XG[0:16, :], PS[0:16, kb, :], ACT.Copy), a, z_xg, f["xg"])
                give(kb, xg)
                qk = []
                for W, l in ((WQ, l_q), (WK, l_k)):
                    for h in range(2):
                        kb, fr = take()
                        mm(bt(kb), W[:, 0, 128 * h:128 * h + 128], xt[0], True, False, [fr, l])
                        qk.append((kb, mm(bt(kb), W[:, 1, 128 * h:128 * h + 128], xt[1], False, True)))
                g2 = []
                for p in range(2):
                    kb, fr = take()
                    for j in range(2):
                        b = 2 * p + j
                        a = mm(PS[:, kb, 256 * j:256 * j + 256], XG[0:17, 128 * b:128 * b + 128], W2[:],
                               True, True, [fr, xg, l_w2])
                    f["xg"] = [a]
                    c0 = 512 * p
                    z1 = act(lambda e, kb=kb, c0=c0: e.activation(GA[:, c0:c0 + 512], PS[:, kb, :], ACT.Abs), a, f["ga"])
                    z2 = act(lambda e, c0=c0: e.activation(GE[:, c0:c0 + 512], GA[:, c0:c0 + 512], ACT.Exp, scale=-1.0), z1, f["ge"])
                    z3 = act(lambda e, c0=c0: e.activation(GA[:, c0:c0 + 512], GE[:, c0:c0 + 512], ACT.Ln, bias=EPS[:, 2:3]), z2, l_eps)
                    z4 = dve(lambda e, kb=kb, c0=c0: e.scalar_tensor_tensor(
                        out=GG[:, c0:c0 + 512], in0=PS[:, kb, :], scalar=0.0, in1=GA[:, c0:c0 + 512],
                        op0=ALU.min, op1=ALU.subtract), z3, f["gg"])
                    give(kb, z4)
                    g2.append(z4)
                f["ga"], f["ge"] = g2, [z3]
                vr = []
                for b in range(4):
                    kb, fr = take()
                    mm(PS[:, kb, :], xt[0][:, b, :], WV[:, 0, :], True, False, [fr, l_v])
                    a = mm(PS[:, kb, :], xt[1][:, b, :], WV[:, 1, :], False, True)
                    a = act(lambda e, kb=kb, b=b: e.activation(V[:, b, :], PS[:, kb, :], ACT.Copy), a, f["v"])
                    give(kb, a)
                    vr.append(a)
                qgr, kdr, kgr = [], [], []
                for h in range(2):
                    kb, fr = take()
                    for b in range(4):
                        a = mm(PS[:, kb, 128 * b:128 * b + 128], GG[:, 256 * b + 128 * h:256 * b + 128 * h + 128], TRI[:],
                               True, True, [fr, g2, l_tri])
                    e1 = act(lambda e, kb=kb, h=h: e.activation(EP[:, h, :], PS[:, kb, :], ACT.Exp), a, f["ep"])
                    e2 = act(lambda e, kb=kb, h=h: e.activation(EM[:, h, :], PS[:, kb, :], ACT.Exp, scale=-1.0), a, f["em"])
                    give(kb, e2)
                    f["gg"] = [a]
                    kq, mq = qk[h]
                    for hh in range(2):
                        r = slice(64 * hh, 64 * hh + 64)
                        a = dve(lambda e, r=r, h=h, hh=hh, kq=kq: e.scalar_tensor_tensor(
                            out=QG[r, h, hh, :], in0=PS[r, kq, :], scalar=0.125, in1=EP[r, h, :],
                            op0=ALU.mult, op1=ALU.mult), e1, mq, z_qg, f["qg"])
                    give(kq, a)
                    qgr.append(a)
                    kk, mk = qk[2 + h]
                    a = dve(lambda e, h=h, kk=kk: e.tensor_tensor(KD[:, h, :], PS[:, kk, :], EM[:, h, :], ALU.mult), e2, mk, f["kd"])
                    give(kk, a)
                    kdr.append(a)
                    lastc = EP[:, h, :].rearrange("p (c s) -> p c s", s=64)[:, :, 63:64].to_broadcast([128, 8, 64])
                    a = pool(lambda e, h=h, lastc=lastc: e.tensor_tensor(
                        KG[:, h, :].rearrange("p (c s) -> p c s", s=64), KD[:, h, :].rearrange("p (c s) -> p c s", s=64),
                        lastc, ALU.mult), a, e1, f["kg"])
                    kgr.append(a)
                f["em"] = kdr
                atr = []
                for h in range(2):
                    for p in range(2):
                        kb, fr = take()
                        for j in range(2):
                            b = 2 * p + j
                            a = mm(PS[:, kb, 256 * j:256 * j + 256].rearrange("p (h s) -> p h s", h=2),
                                   KD[:, h, 128 * b:128 * b + 128], QG[:, h, :, 128 * b:128 * b + 128],
                                   True, True, [fr, qgr, kdr])
                        dst = AT[:].rearrange("p (b g) s -> p b g s", b=4)[:, 2 * p:2 * p + 2, 2 * h:2 * h + 2, :]
                        for j in range(2):
                            a2 = dve(lambda e, kb=kb, j=j, dst=dst: e.copy_predicated(
                                dst[:, j], MSK[:].unsqueeze(1).to_broadcast([128, 2, 128]),
                                PS[:, kb, 256 * j:256 * j + 256].rearrange("p (h s) -> p h s", h=2)),
                                a, z_at, l_msk, f["at"])
                        give(kb, a2)
                        atr.append(a2)
                f["kd"] = [a, kgr]
                kzr = []
                for p in range(2):
                    kb, fr = take()
                    for j in range(2):
                        for h in range(2):
                            b = 2 * p + j
                            a = tr(PS[:, kb, 256 * j + 128 * h:256 * j + 128 * h + 128], KG[:, h, 128 * b:128 * b + 128],
                                   [fr, kgr, l_idn])
                    for c in range(2):
                        r = slice(64 * c, 64 * c + 64)
                        a2 = act(lambda e, r=r, c=c, p=p, kb=kb: e.activation(
                            KZ[r, c, 2 * p:2 * p + 2, :], PS[r, kb, :].rearrange("p (b s) -> p b s", b=2), ACT.Copy), a, z_kz, f["kz"])
                    give(kb, a2)
                    kzr.append(a2)
                f["kg"] = [a]
                ob = []
                for b in range(4):
                    kb, fr = take()
                    for hd in range(4):
                        a = mm(PS[:, kb, 128 * hd:128 * hd + 128], AT[:, 4 * b + hd, :], V[:, b, 128 * hd:128 * hd + 128],
                               hd == 0, False, [fr, atr, vr], skip=True)
                    ob.append(kb)
                f["at"] = [a]
                for c in range(2):
                    cur, nxt = c, 1 - c
                    for b in range(4):
                        for h in range(2):
                            for hh in range(2):
                                hd = 2 * h + hh
                                a = mm(PS[64 * c:64 * c + 64, ob[b], 128 * hd:128 * hd + 128],
                                       QG[:, h, hh, 128 * b + 64 * c:128 * b + 64 * c + 64], S[:, cur, h, b, :],
                                       False, c == 1, [s_ready[4 * h + b]], skip=True)
                            s_read[4 * h + b] = [a]
                    oend = a
                    for h in range(2):
                        kb, fr = take()
                        for b in range(4):
                            for hh in range(2):
                                hd = 2 * h + hh
                                a = mm(PS[64 * hh:64 * hh + 64, kb, 128 * b:128 * b + 128],
                                       KZ[:, c, b, 64 * hd:64 * hd + 64], V[:, b, 128 * hd:128 * hd + 128],
                                       True, True, [fr, kzr])
                        for b in range(4):
                            ecol = EP[:, h, 128 * b + 64 * c + 63:128 * b + 64 * c + 64]
                            s_ready[4 * h + b] = dve(lambda e, h=h, b=b, kb=kb, cur=cur, nxt=nxt, ecol=ecol: e.scalar_tensor_tensor(
                                out=S[:, nxt, h, b, :], in0=S[:, cur, h, b, :], scalar=ecol,
                                in1=PS[:, kb, 128 * b:128 * b + 128], op0=ALU.mult, op1=ALU.add),
                                a, s_ready[4 * h + b], s_read[4 * h + b])
                        give(kb, s_ready[4 * h + 3])
                        f["ep"] = [s_ready[4 * h + 3], kgr]
                f["kz"], f["v"], f["qg"] = [a], [a], [oend]
                sgr = []
                for b in range(4):
                    kb, fr = take()
                    mm(PS[:, kb, :], xt[0][:, b, :], WG[:, 0, :], True, False, [fr, l_g])
                    a = mm(PS[:, kb, :], xt[1][:, b, :], WG[:, 1, :], False, True)
                    xtfree = a
                    a = act(lambda e, kb=kb, b=b: e.activation(SG[:, b, :], PS[:, kb, :], ACT.Silu), a, f["sg"])
                    give(kb, a)
                    a = pool(lambda e, b=b: e.tensor_tensor(SG[:, b, :], SG[:, b, :], RMS[:], ALU.mult), a, l_rms)
                    sgr.append(a)
                for b in range(4):
                    for hd in range(4):
                        i = 4 * b + hd
                        a = act(lambda e, b=b, hd=hd, i=i, kb=ob[b]: e.activation(
                            SQ[:], PS[:, kb, 128 * hd:128 * hd + 128], ACT.Square, accum_out=SS[:, i:i + 1]),
                            oend, a if i else f["sr"])
                r = rsqrt(SR[:], SS[:], SL[:], 1.0 / 128, 0, a, f["sr"])
                yr = []
                for b in range(4):
                    for hd in range(4):
                        i = 4 * b + hd
                        a = dve(lambda e, b=b, hd=hd, i=i, kb=ob[b]: e.scalar_tensor_tensor(
                            out=Y[:, b, 128 * hd:128 * hd + 128], in0=PS[:, kb, 128 * hd:128 * hd + 128],
                            scalar=SR[:, i:i + 1], in1=SG[:, b, 128 * hd:128 * hd + 128], op0=ALU.mult, op1=ALU.mult),
                            r, sgr[b], f["y"])
                    give(ob[b], a)
                    yr.append(a)
                f["sg"], f["sr"] = [a], [a]
                ytr = []
                for b in range(4):
                    kb, fr = take()
                    for hd in range(4):
                        a = tr(PS[:, kb, 128 * hd:128 * hd + 128], Y[:, b, 128 * hd:128 * hd + 128], [fr, yr[b]])
                    a2 = act(lambda e, b=b, kb=kb: e.activation(YT[:, 4 * b:4 * b + 4, :], PS[:, kb, :].rearrange("p (h s) -> p h s", h=4), ACT.Copy), a, f["yt"])
                    give(kb, a2)
                    ytr.append(a2)
                f["y"] = [a]
                res = []
                for p in range(2):
                    kb, fr = take()
                    for j in range(2):
                        b = 2 * p + j
                        for hd in range(4):
                            a = mm(PS[:, kb, 256 * j:256 * j + 256], YT[:, 4 * b + hd, :], WO[:, hd, :], hd == 0, hd == 3,
                                   [fr, ytr[b], l_o])
                    a2 = dve(lambda e, p=p, kb=kb, t=t: e.tensor_tensor(
                        xv[:, 2 * p:2 * p + 2, t, :], xv[:, 2 * p:2 * p + 2, t, :],
                        PS[:, kb, :].rearrange("p (b d) -> p b d", b=2), ALU.add), a, l_X)
                    give(kb, a2)
                    res.append(a2)
                f["yt"] = [a]
                xs = [xv[:, b, t, :] for b in range(4)]
                n1 = layernorm(xs, xs, res)
                n2 = layernorm(xs, [NR[:, b, :] for b in range(4)], n1, f["nr"])
                a = pool(lambda e: e.tensor_tensor(NR[:], NR[:], GAM[:].unsqueeze(1).to_broadcast([128, 4, 256]), ALU.mult), n2, l_gam)
                a = pool(lambda e: e.tensor_tensor(NR[:], NR[:], BET[:].unsqueeze(1).to_broadcast([128, 4, 256]), ALU.add), a, l_bet)
                for k in range(2):
                    kb, fr = take()
                    for b in range(4):
                        a2 = tr(PS[:, kb, 128 * b:128 * b + 128], NR[:, b, 128 * k:128 * k + 128], [fr, a])
                    a3 = dve(lambda e, k=k, kb=kb, t=t: e.tensor_copy(
                        xtv[:, k, :, 128 * t:128 * t + 128], PS[:, kb, :].rearrange("p (b s) -> p b s", b=4)), a2, xtfree)
                    give(kb, a3)
                f["nr"] = [a2]
            Q.barrier()

        def retile():
            for g in range(8):
                xs = [X[:, 4 * g + i, :] for i in range(4)]
                n1 = layernorm(xs, xs)
                for k in range(2):
                    kb, fr = take()
                    for i in range(4):
                        a = tr(PS[:, kb, 128 * i:128 * i + 128], xs[i][:, 128 * k:128 * k + 128], [fr, n1])
                    a = act(lambda e, k=k, kb=kb, g=g: e.activation(XT[:, k, 512 * g:512 * g + 512], PS[:, kb, :], ACT.Copy), a)
                    give(kb, a)

        def finish():
            o = Q.dma("sp", out, X[:], Q.last())
            Q.q["sp"].append(Op("sp", None, [o]))
            if dbg is not None:
                dd = Q.dma("sp", dbg, XT[:], Q.last())
                Q.q["sp"].append(Op("sp", None, [dd]))
            Q.emit(nc, ctx)

        if stages < 2:
            return finish()
        def router(RW, l_rw, gates, c, *w):
            b3 = [128, 32, 8]
            LG, PB, OH, T8 = (sb(n + str(int(gates)), b3, F32, c) for n in ("LG", "PB", "OH", "T8"))
            M1, M2, R1, R2 = (sb(n + str(int(gates)), [128, 32], F32, c) for n in ("M1", "M2", "R1", "R2"))
            up = lambda m: m.unsqueeze(2).to_broadcast(b3)
            kb, fr = take()
            pl = PS[:, kb, 0:256].rearrange("p (t e) -> p t e", e=8)
            for t in range(32):
                mm(pl[:, t, :], XT[:, 0, 128 * t:128 * t + 128], RW[:, 0, :], True, False, [fr, w, l_rw])
                a = mm(pl[:, t, :], XT[:, 1, 128 * t:128 * t + 128], RW[:, 1, :], False, True)
            tt = lambda o, x, y, op, *w: dve(lambda e: e.tensor_tensor(o, x, y, op), *w)
            red = lambda o, x, op, *w: dve(lambda e: e.tensor_reduce(o, x, AX, op), *w)
            a = red(M1[:], pl, ALU.max, a)
            a = tt(LG[:], pl, up(M1[:]), ALU.subtract, a)
            give(kb, a)
            a = act(lambda e: e.activation(PB[:], LG[:], ACT.Exp), a)
            a = red(M2[:], PB[:], ALU.add, a)
            a = dve(lambda e: e.reciprocal(R1[:], M2[:]), a)
            a = tt(PB[:], PB[:], up(R1[:]), ALU.mult, a)
            def top(m, oh, r, a):
                a = red(m[:], PB[:], ALU.max, a)
                a = tt(T8[:], PB[:], up(m[:]), ALU.is_equal, a)
                a = tt(T8[:], T8[:], IREV[:].unsqueeze(1).to_broadcast(b3), ALU.mult, a, l_irev)
                a = red(r[:], T8[:], ALU.max, a)
                return tt(oh[:], T8[:], up(r[:]), ALU.is_equal, a)
            a = top(M1, OH, R1, a)
            a = dve(lambda e: e.scalar_tensor_tensor(out=PB[:], in0=OH[:], scalar=-2.0, in1=PB[:], op0=ALU.mult, op1=ALU.add), a)
            a = top(M2, LG, R1, a)
            if gates:
                a = tt(R1[:], M2[:], M1[:], ALU.subtract, a)
                a = act(lambda e: e.activation(R1[:], R1[:], ACT.Exp), a)
                a = dve(lambda e: e.tensor_scalar(R2[:], R1[:], 1.0, None, ALU.add), a)
                a = dve(lambda e: e.reciprocal(M1[:], R2[:]), a)
                a = tt(M2[:], R1[:], M1[:], ALU.mult, a)
            a = tt(OH[:], OH[:], up(M1[:]), ALU.mult, a)
            a = tt(LG[:], LG[:], up(M2[:]), ALU.mult, a)
            return tt(COMB[:], OH[:], LG[:], ALU.add, a)

        with ExitStack() as c2:
            s2 = lambda n, s, d=F32: sb(n, s, d, c2)
            RW = s2("RW", [128, 2, 8])
            SGU, SDN = s2("SGU", [128, 2, 512]), s2("SDN", [128, 2, 256])
            WGU = [s2(f"WGU{i}", [128, 2, 1536]) for i in range(2)]
            WDN = [s2(f"WDN{i}", [128, 6, 256]) for i in range(2)]
            H = [s2(f"H{i}", [128, 6, 512]) for i in range(2)]
            SL2 = [s2(f"SLU{i}", [128, 512]) for i in range(3)]
            l_rw = Q.dma("sp", RW[:], A["rw"])
            l_sg, l_sd = Q.dma("sp", SGU[:], A["sgu"]), Q.dma("sp", SDN[:], A["sdn"])

            def load_e(e_, *w):
                i = e_ % 2
                return [Q.dma("sp", WGU[i][:], A["gu"][e_], *w), Q.dma("sp", WDN[i][:], A["dn"][e_], *w)]
            wl = {0: load_e(0), 1: load_e(1)}
            rr = router(RW, l_rw, True, c2)
            hfree, sfree = [[], []], [[], [], []]
            cnt = {"h": 0, "s": 0}

            def hidden(n, nf, W, lw):
                hi = cnt["h"] % 2
                cnt["h"] += 1
                hr = []
                for f_ in range(nf):
                    (kg, fg), (ku, fu) = take(), take()
                    xs = [XT[:, k, 512 * n:512 * n + 512] for k in range(2)]
                    for kb, fr, o in ((kg, fg, 0), (ku, fu, nf)):
                        c0 = 128 * (o + f_)
                        mm(PS[:, kb, :], W[:, 0, c0:c0 + 128], xs[0], True, False, [fr, lw])
                        a = mm(PS[:, kb, :], W[:, 1, c0:c0 + 128], xs[1], False, True)
                        if o == 0:
                            ag = a
                    si = cnt["s"] % 3
                    cnt["s"] += 1
                    a1 = act(lambda e, kg=kg, si=si: e.activation(SL2[si][:], PS[:, kg, :], ACT.Silu), ag, sfree[si])
                    give(kg, a1)
                    a2 = dve(lambda e, ku=ku, si=si, hi=hi, f_=f_: e.tensor_tensor(
                        H[hi][:, f_, :], PS[:, ku, :], SL2[si][:], ALU.mult), a, a1, hfree[hi])
                    give(ku, a2)
                    sfree[si] = [a2]
                    hr.append(a2)
                return hi, hr

            def down(n, hi, hr, nf, W, lw, e_):
                for p in range(2):
                    kb, fr = take()
                    for j in range(2):
                        m = 2 * p + j
                        for f_ in range(nf):
                            a = mm(PS[:, kb, 256 * j:256 * j + 256], H[hi][:, f_, 128 * m:128 * m + 128], W[:, f_, :],
                                   f_ == 0, f_ == nf - 1, [fr, hr, lw])
                    t0 = 4 * n + 2 * p
                    if e_ is None:
                        a2 = dve(lambda e, kb=kb, t0=t0: e.tensor_tensor(
                            X[:, t0:t0 + 2, :], X[:, t0:t0 + 2, :], PS[:, kb, :].rearrange("p (b d) -> p b d", b=2), ALU.add), a)
                    else:
                        for j in range(2):
                            a2 = dve(lambda e, kb=kb, t=t0 + j, j=j: e.scalar_tensor_tensor(
                                out=X[:, t, :], in0=PS[:, kb, 256 * j:256 * j + 256], scalar=COMB[:, t, e_:e_ + 1],
                                in1=X[:, t, :], op0=ALU.mult, op1=ALU.add), a, rr, xacc.get(t, []))
                    for j in range(2):
                        xacc[t0 + j] = [a2]
                    give(kb, a2)
                hfree[hi] = [a]
                return a

            xacc = {}
            todo = None
            jobs = [(None, n) for n in range(8)] + [(e_, n) for e_ in range(8) for n in range(8)]
            for e_, n in jobs:
                if e_ is None:
                    nf, W, D, lw = 2, SGU, SDN, [l_sg, l_sd]
                else:
                    nf, W, D, lw = 6, WGU[e_ % 2], WDN[e_ % 2], wl[e_]
                hi, hr = hidden(n, nf, W, lw)
                if todo:
                    last_pe = down(*todo)
                    if todo[-1] is not None and todo[0] == 7 and todo[-1] + 2 < 8:
                        wl[todo[-1] + 2] = load_e(todo[-1] + 2, last_pe)
                todo = (n, hi, hr, nf, D, lw, e_)
            down(*todo)
            Q.barrier()
            retile()
            Q.barrier()

        if stages < 3:
            return finish()
        PARTS = nc.dram_tensor("parts", (2, 3, 512, 4096), BF16, kind="Internal").ap()
        with ExitStack() as c3:
            s3 = lambda n, s, d=F32: sb(n, s, d, c3)
            WW = [s3(f"WW{i}", [128, 2, 1024]) for i in range(2)]
            BB = s3("BB", [128, 2, 2, 4])
            CS = s3("CS", [128, 2, 1024])
            T1 = [s3(f"TA{i}", [128, 512]) for i in range(3)]
            T2 = [s3(f"TB{i}", [128, 512]) for i in range(3)]
            PP = [s3(f"PP{i}", [128, 3, 512], BF16) for i in range(4)]
            l_bb, l_cs = Q.dma("sp", BB[:], A["bqk"]), Q.dma("sp", CS[:], A["c_cs"])
            l_ww = [Q.dma("sp", WW[i][:], A["wqk"][i]) for i in range(2)]
            tf, pf = [[], [], []], [[], [], [], []]
            pw = {}
            i = 0
            for b in range(4):
                for qi in range(2):
                    for fb in range(4):
                        for hf in range(2):
                            tok = 1024 * b + 512 * hf
                            (ka, fa), (kb, fr) = take(), take()
                            for bank, fx, o in ((ka, fa, 0), (kb, fr, 512)):
                                c0 = o + 128 * fb
                                mm(PS[:, bank, :], WW[qi][:, 0, c0:c0 + 128], XT[:, 0, tok:tok + 512], True, False, [fx, l_ww[qi]])
                                a = mm(PS[:, bank, :], WW[qi][:, 1, c0:c0 + 128], XT[:, 1, tok:tok + 512], False, True)
                                if o == 0:
                                    am = a
                            t1, t2, pp = T1[i % 3], T2[i % 3], PP[i % 4]
                            a1 = dve(lambda e, ka=ka, t1=t1, qi=qi, fb=fb, hf=hf: e.scalar_tensor_tensor(
                                out=t1[:], in0=PS[:, ka, :], scalar=BB[:, qi, 0, fb:fb + 1], in1=CS[:, 0, 512 * hf:512 * hf + 512],
                                op0=ALU.add, op1=ALU.mult), am, l_bb, l_cs, tf[i % 3])
                            a2 = dve(lambda e, kb=kb, t2=t2, qi=qi, fb=fb, hf=hf: e.scalar_tensor_tensor(
                                out=t2[:], in0=PS[:, kb, :], scalar=BB[:, qi, 1, fb:fb + 1], in1=CS[:, 1, 512 * hf:512 * hf + 512],
                                op0=ALU.add, op1=ALU.mult), a)
                            give(ka, a1)
                            give(kb, a2)
                            r = pool(lambda e, t1=t1, t2=t2: e.tensor_tensor(t1[:], t1[:], t2[:], ALU.add), a1, a2)
                            h = act(lambda e, t1=t1, pp=pp: e.activation(pp[:, 0, :], t1[:], ACT.Copy), r, pf[i % 4])
                            d = dve(lambda e, t1=t1, pp=pp: e.tensor_tensor(t1[:], t1[:], pp[:, 0, :], ALU.subtract), h)
                            m = act(lambda e, t1=t1, pp=pp: e.activation(pp[:, 1, :], t1[:], ACT.Copy), d)
                            l = pool(lambda e, t1=t1, pp=pp: e.tensor_tensor(pp[:, 2, :], t1[:], pp[:, 1, :], ALU.subtract), m)
                            tf[i % 3] = [l]
                            w = Q.dma("sp", PARTS[qi, :, 128 * fb:128 * fb + 128, tok:tok + 512].rearrange("c p s -> p c s"), pp[:], l)
                            pf[i % 4] = [w]
                            pw.setdefault((b, fb), []).append(w)
                            i += 1
            Q.barrier()

        with ExitStack() as c4:
            s4 = lambda n, s, d=F32: sb(n, s, d, c4)
            QS = [s4(f"QS{i}", [128, 8, 1024], BF16) for i in range(2)]
            KS = [s4(f"KS{i}", [128, 8, 1024], BF16) for i in range(2)]
            VP = s4("VP", [128, 8, 16, 32])
            E = s4("E", [128, 4, 1024])
            IDB = s4("IDB", [128, 128], BF16)
            MR, MC = s4("MR", [128, 128], BF16), s4("MC", [128, 128], BF16)
            WV1, WO1 = s4("WV1", [128, 2, 256]), s4("WO1", [128, 2, 256])
            BV, BO, HN = s4("BV", [128, 256]), s4("BO", [128, 256]), s4("HN", [128, 256])
            LQ = s4("LQ", [128, 4, 256])
            L1, L2, NL = s4("L1", [128, 16]), s4("L2", [128, 16]), s4("NL", [128, 16])
            NM = s4("NM", [128, 8, 8])
            MP = s4("MP", [64, 3, 128], BF16)
            MT = s4("MT", [64, 128])
            OT = s4("OT", [128, 1024])
            OA = s4("OA", [128, 8, 256])
            OB = s4("OB", [128, 8, 256])
            RC = s4("RC", [128, 8, 4])
            O1, O2 = s4("O1", [128, 8, 2, 16]), s4("O2", [128, 8, 2, 16])
            MS, ML = s4("MS", [128, 128]), s4("ML", [128, 128])

            l_m = Q.dma("sp", E[:, 0, 0:256], A["c_mrc"])
            l_idb = act(lambda e: e.activation(IDB[:], IDN[:], ACT.Copy))
            l_mr = act(lambda e: e.activation(MR[:], E[:, 0, 0:128], ACT.Copy), l_m)
            l_mc = act(lambda e: e.activation(MC[:], E[:, 0, 128:256], ACT.Copy), l_m)
            l_v1, l_o1 = Q.dma("sp", WV1[:], A["wv1"]), Q.dma("sp", WO1[:], A["wo1"])
            l_bv, l_bo, l_hn = (Q.dma("sp", d[:], A[n]) for d, n in ((BV, "bv"), (BO, "bo"), (HN, "hn")))
            l_lq = Q.dma("sp", LQ[:], A["lam"])
            z_k = [dve(lambda e, i=i: e.memset(KS[i][96:128], 1.0)) for i in range(2)]
            z_v = pool(lambda e: e.memset(VP[:], 0.0))
            z_v = pool(lambda e: e.memset(VP[:, :, :, 16:17], 1.0), z_v)
            li = 0.8 - 0.6 * 1.0
            a = dve(lambda e: e.tensor_tensor(LQ[:, 0, :], LQ[:, 0, :], LQ[:, 1, :], ALU.mult), l_lq)
            a2 = dve(lambda e: e.tensor_tensor(LQ[:, 2, :], LQ[:, 2, :], LQ[:, 3, :], ALU.mult), l_lq)
            a = dve(lambda e: e.tensor_reduce(L1[:], LQ[:, 0, :].rearrange("p (h d) -> p h d", d=16), AX, ALU.add), a)
            a2 = dve(lambda e: e.tensor_reduce(L2[:], LQ[:, 2, :].rearrange("p (h d) -> p h d", d=16), AX, ALU.add), a2)
            a = act(lambda e: e.activation(L1[:], L1[:], ACT.Exp), a)
            a = act(lambda e: e.activation(L2[:], L2[:], ACT.Exp), a2)
            a = dve(lambda e: e.scalar_tensor_tensor(out=NL[:], in0=L2[:], scalar=-li, in1=L1[:], op0=ALU.add, op1=ALU.subtract), a)
            nl = a
            hn = dve(lambda e: e.tensor_scalar(HN[:], HN[:], 1.0 - li, None, ALU.mult), l_hn)

            def fetch(u, *w):
                b, fb = u // 4, u % 4
                ops = []
                for qi, D in ((0, QS[u % 2]), (1, KS[u % 2])):
                    for r0, n in ((0, 3), (48, 2), (80, 1)):
                        for c in range(n):
                            part = c if qi == 0 else (0, 1, 2)[(0, 48, 80).index(r0)]
                            src = PARTS[qi, part, 128 * fb:128 * fb + 128, 1024 * b:1024 * b + 1024]
                            ops.append(Q.dma("sp", D[r0 + 16 * c:r0 + 16 * c + 16, :, :],
                                             src.rearrange("(j r) s -> r j s", r=16), *w))
                return ops

            kvread = {}
            fl = {0: fetch(0)}
            vfree, ofree, efree, oafree, nmfree, mpfree, otfree = [z_v], [], [[], [], [], []], [], [], [], []
            rcfree = []
            for b in range(4):
                vr = []
                for i in range(8):
                    if i % 2 == 0:
                        kb, fr = take()
                    o = PS[:, kb, 256 * (i % 2):256 * (i % 2) + 256]
                    tk_ = slice(1024 * b + 128 * i, 1024 * b + 128 * i + 128)
                    mm(o, XT[:, 0, tk_], WV1[:, 0, :], True, False, [fr, l_v1])
                    a = mm(o, XT[:, 1, tk_], WV1[:, 1, :], False, True)
                    if i % 2:
                        a = dve(lambda e, i=i, kb=kb: e.tensor_tensor(
                            VP[:, i - 1:i + 1, :, 0:16], PS[:, kb, :].rearrange("p (i h d) -> p i h d", i=2, d=16),
                            BV[:].rearrange("p (h d) -> p h d", d=16).unsqueeze(1).to_broadcast([128, 2, 16, 16]), ALU.add),
                            a, l_bv, vfree)
                        vr.append(a)
                        give(kb, a)
                oar = []
                for fb in range(4):
                    u = 4 * b + fb
                    Qs, Ks = QS[u % 2], KS[u % 2]
                    if u + 1 < 16:
                        fl[u + 1] = fetch(u + 1, kvread.get(u - 1, []), z_k)
                    nmr = []
                    for j in range(8):
                        for i in range(8):
                            W = 128 * (i + 1)
                            np_ = (W + 511) // 512
                            if np_ == 2:
                                ks = [k for k, _ in banks]
                                k0 = next(k for k in ks if k % 2 == 0 and k + 1 in ks)
                                pair = [x for x in banks if x[0] in (k0, k0 + 1)]
                                banks[:] = [x for x in banks if x[0] not in (k0, k0 + 1)]
                                fr = [x[1] for x in pair]
                            else:
                                k0, fr = take()
                            lhs = Qs[0:96, j, 128 * i:128 * i + 128]
                            for p in range(np_):
                                n = min(512, W - 512 * p)
                                dg = p == np_ - 1
                                a = mm(PS[:, k0 + p, 0:n], lhs, Ks[0:96, j, 512 * p:512 * p + n], True, True, [fr, fl[u]])
                                if dg:
                                    a = mm(PS[:, k0 + p, n - 128:n], IDB[:], MR[:], False, True, [l_idb, l_mr], skip=True)
                            src = PS[:, k0, 0:W] if np_ == 1 else PS[:, k0:k0 + 2, :].rearrange("p k s -> p (k s)")[:, 0:W]
                            a = dve(lambda e, src=src, j=j, i=i: e.tensor_reduce(NM[:, j, i:i + 1], src, AX, ALU.max), a, nmfree)
                            for p in range(np_):
                                give(k0 + p, a)
                    kb, fr = take()
                    tm = tr(PS[0:64, kb, 0:128], NM[:].rearrange("p j i -> p (j i)"), [fr, a])
                    nmfree = [tm]
                    h = act(lambda e, kb=kb: e.activation(MP[:, 0, :], PS[0:64, kb, 0:128], ACT.Copy, scale=-1.0), tm, mpfree)
                    d = dve(lambda e, kb=kb: e.scalar_tensor_tensor(out=MT[:], in0=PS[0:64, kb, 0:128], scalar=-1.0, in1=MP[:, 0, :],
                                                                    op0=ALU.mult, op1=ALU.subtract), h)
                    m = act(lambda e: e.activation(MP[:, 1, :], MT[:], ACT.Copy), d)
                    l = dve(lambda e: e.tensor_tensor(MP[:, 2, :], MT[:], MP[:, 1, :], ALU.subtract), m)
                    give(kb, d)
                    ml = [Q.dma("sp", Qs[96 + p:97 + p, :, :], MP[:, p, :], l) for p in range(3)]
                    mpfree = ml
                    for g in range(2):
                        (o0, f0), (o1, f1) = take(), take()
                        ob = (o0, o1)
                        of = (f0, f1)
                        pend = []
                        def av(kt, reads):
                            for p in range(2):
                                lo = max(128 * kt, 512 * p)
                                if lo >= 512 * p + 512:
                                    continue
                                for jj in range(4):
                                    hd = 4 * fb + 2 * g + jj // 2
                                    a = mm(PS[32 * jj:32 * jj + 32, ob[p], lo - 512 * p:512], VP[:, kt, hd, :],
                                           E[:, jj, lo:512 * p + 512], kt == 0, True, [of[p], reads, vr], skip=True)
                            for jj in range(4):
                                efree[jj] = [a]
                            return a
                        for kt in range(8):
                            ers = []
                            for jj in range(4):
                                j = 4 * g + jj
                                q0 = 128 * kt
                                ks = [k for k, _ in banks]
                                k0 = next(k for k in ks if k % 2 == 0 and k + 1 in ks)
                                fr = [x[1] for x in banks if x[0] in (k0, k0 + 1)]
                                banks[:] = [x for x in banks if x[0] not in (k0, k0 + 1)]
                                lhs = Ks[0:99, j, q0:q0 + 128]
                                for p in range(2):
                                    lo = max(q0, 512 * p)
                                    if lo >= 512 * p + 512:
                                        continue
                                    dg = lo == q0
                                    a = mm(PS[:, k0 + p, lo - 512 * p:512], lhs, Qs[0:99, j, lo:512 * p + 512], True, True, [fr, ml, z_k])
                                    if dg:
                                        a = mm(PS[:, k0 + p, lo - 512 * p:lo - 512 * p + 128], IDB[:], MC[:], False, True, [l_mc], skip=True)
                                a = act(lambda e, k0=k0, q0=q0, jj=jj: e.activation(
                                    E[:, jj, q0:1024], PS[:, k0:k0 + 2, :].rearrange("p k s -> p (k s)")[:, q0:1024], ACT.Exp, scale=0.25),
                                    a, efree[jj])
                                give(k0, a)
                                give(k0 + 1, a)
                                ers.append(a)
                            a = av(kt, ers)
                        kvread[u] = [a]
                        c1_ = act(lambda e, o0=o0: e.activation(OT[:, 0:512], PS[:, o0, :], ACT.Copy), a, otfree)
                        c2_ = dve(lambda e, o1=o1: e.tensor_copy(OT[:, 512:1024], PS[:, o1, :]), a, otfree)
                        give(o0, c1_)
                        give(o1, c2_)
                        ks = [k for k, _ in banks]
                        k0 = next(k for k in ks if k % 2 == 0 and k + 1 in ks)
                        fr = [x[1] for x in banks if x[0] in (k0, k0 + 1)]
                        banks[:] = [x for x in banks if x[0] not in (k0, k0 + 1)]
                        for i in range(8):
                            a = tr(PS[:, k0 + i // 4, 128 * (i % 4):128 * (i % 4) + 128], OT[:, 128 * i:128 * i + 128], [fr, c1_, c2_])
                        otfree = [a]
                        ov = PS[:, k0:k0 + 2, :].rearrange("p k s -> p (k s)").rearrange("p (i h m d) -> p i h m d", i=8, h=2, m=2)
                        h0 = 4 * fb + 2 * g
                        rc4 = RC[:].rearrange("p i (h m) -> p i h m", m=2)
                        a = dve(lambda e, ov=ov: e.reciprocal(rc4, ov[:, :, :, :, 16]), a, rcfree)
                        a = dve(lambda e, h0=h0: e.tensor_tensor(rc4[:, :, :, 1], rc4[:, :, :, 1],
                                NL[:, h0:h0 + 2].unsqueeze(1).to_broadcast([128, 8, 2]), ALU.mult), a, nl)
                        b4 = [128, 8, 2, 16]
                        x1 = dve(lambda e, ov=ov: e.tensor_tensor(O1[:], ov[:, :, :, 0, 0:16], rc4[:, :, :, 0].unsqueeze(3).to_broadcast(b4), ALU.mult), a, rcfree)
                        x2 = dve(lambda e, ov=ov: e.tensor_tensor(O2[:], ov[:, :, :, 1, 0:16], rc4[:, :, :, 1].unsqueeze(3).to_broadcast(b4), ALU.mult), a, rcfree)
                        give(k0, x2)
                        give(k0 + 1, x2)
                        a = pool(lambda e, h0=h0: e.tensor_tensor(
                            OA[:, :, 16 * h0:16 * h0 + 32].rearrange("p i (h d) -> p i h d", d=16), O1[:], O2[:], ALU.add), x1, x2, oafree)
                        rcfree = [a]
                        oar.append(a)
                vfree = kvread[4 * b + 3]
                oh = OA[:].rearrange("p i (h d) -> p (i h) d", d=16)
                a = pool(lambda e: e.tensor_tensor(OB[:], OA[:], OA[:], ALU.mult), oar, oafree)
                a = dve(lambda e: e.tensor_reduce(MS[:], OB[:].rearrange("p i (h d) -> p (i h) d", d=16), AX, ALU.add), a)
                a = rsqrt(MS[:], MS[:], ML[:], 1.0 / 16, 1, a)
                a = dve(lambda e: e.tensor_tensor(oh, oh, MS[:].unsqueeze(2).to_broadcast([128, 128, 16]), ALU.mult), a)
                a = pool(lambda e: e.tensor_tensor(OA[:], OA[:], HN[:].unsqueeze(1).to_broadcast([128, 8, 256]), ALU.mult), a, hn)
                bo = pool(lambda e, b=b: e.tensor_tensor(X[:, 8 * b:8 * b + 8, :], X[:, 8 * b:8 * b + 8, :],
                          BO[:].unsqueeze(1).to_broadcast([128, 8, 256]), ALU.add), l_bo)
                OTT = OB[:].rearrange("p i d -> p (i d)").rearrange("p (k s) -> p k s", k=2)
                tt_ = []
                for k in range(2):
                    for hf in range(2):
                        kb, fr = take()
                        for i in range(4):
                            a2 = tr(PS[:, kb, 128 * i:128 * i + 128], OA[:, 4 * hf + i, 128 * k:128 * k + 128], [fr, a])
                        a3 = act(lambda e, k=k, hf=hf, kb=kb: e.activation(OTT[:, k, 512 * hf:512 * hf + 512], PS[:, kb, :], ACT.Copy), a2)
                        give(kb, a3)
                        tt_.append(a3)
                for i in range(8):
                    if i % 2 == 0:
                        kb, fr = take()
                    o = PS[:, kb, 256 * (i % 2):256 * (i % 2) + 256]
                    mm(o, OTT[:, 0, 128 * i:128 * i + 128], WO1[:, 0, :], True, False, [fr, tt_, l_o1])
                    a3 = mm(o, OTT[:, 1, 128 * i:128 * i + 128], WO1[:, 1, :], False, True)
                    if i % 2:
                        t0 = 8 * b + i - 1
                        a4 = dve(lambda e, kb=kb, t0=t0: e.tensor_tensor(
                            X[:, t0:t0 + 2, :], X[:, t0:t0 + 2, :], PS[:, kb, :].rearrange("p (b d) -> p b d", b=2), ALU.add), a3, bo)
                        give(kb, a4)
                oafree = [a3, a2]
            Q.barrier()
            retile()
            Q.barrier()

        if stages < 4:
            return finish()
        with ExitStack() as c5:
            s5 = lambda n, s, d=F32: sb(n, s, d, c5)
            RW2 = s5("RW2", [128, 2, 8])
            WI = s5("WI", [128, 8, 2, 256])
            WO2 = s5("WO2", [128, 8, 2, 256])
            HH = [s5(f"HH{i}", [128, 2, 512]) for i in range(3)]
            YO = [s5(f"YO{i}", [128, 4, 256]) for i in range(2)]
            l_rw = Q.dma("sp", RW2[:], A["wr2"])
            l_wi, l_wo = [], []
            for e_ in range(8):
                l_wi.append(Q.dma("sp", WI[:, e_], A["wi"][e_]))
                l_wo.append(Q.dma("sp", WO2[:, e_], A["wo2"][e_]))
            rr = router(RW2, l_rw, False, c5)
            hfree = [[], [], []]
            pend = None
            accs = {}

            def second(n, e_, hi, hr):
                for p in range(2):
                    kb, fr = take()
                    for j in range(2):
                        m = 2 * p + j
                        for k in range(2):
                            a = mm(PS[:, kb, 256 * j:256 * j + 256], HH[hi][:, k, 128 * m:128 * m + 128], WO2[:, e_, k, :],
                                   k == 0, k == 1, [fr, hr, l_wo[e_]])
                    for j in range(2):
                        t = 4 * n + 2 * p + j
                        a2 = dve(lambda e, kb=kb, t=t, j=j: e.scalar_tensor_tensor(
                            out=X[:, t, :], in0=PS[:, kb, 256 * j:256 * j + 256], scalar=COMB[:, t, e_:e_ + 1],
                            in1=X[:, t, :], op0=ALU.mult, op1=ALU.add), a, rr, accs.get(t, []))
                        accs[t] = [a2]
                    give(kb, a2)
                hfree[hi] = [a]
                if e_ == 7:
                    xs = [X[:, 4 * n + i, :] for i in range(4)]
                    y = YO[n % 2]
                    n1 = layernorm(xs, [y[:, i, :] for i in range(4)], accs[4 * n + 3], stores[n - 2:n - 1] if n > 1 else [])
                    stores.append(Q.dma("sp", out[:, 4 * n:4 * n + 4, :], y[:], n1))

            stores = []
            i = 0
            for n in range(8):
                for e_ in range(8):
                    hr = []
                    for k in range(2):
                        kb, fr = take()
                        c0 = slice(128 * k, 128 * k + 128)
                        mm(PS[:, kb, :], WI[:, e_, 0, c0], XT[:, 0, 512 * n:512 * n + 512], True, False, [fr, l_wi[e_]])
                        a = mm(PS[:, kb, :], WI[:, e_, 1, c0], XT[:, 1, 512 * n:512 * n + 512], False, True)
                        a = act(lambda e, kb=kb, k=k, hi=i % 3: e.activation(HH[hi][:, k, :], PS[:, kb, :], ACT.Copy), a, hfree[i % 3])
                        give(kb, a)
                        hr.append(a)
                    if pend:
                        second(*pend)
                    pend = (n, e_, i % 3, hr)
                    i += 1
            second(*pend)
            Q.q["sp"].append(Op("sp", None, Q.last()))
        Q.emit(nc, ctx)





def layout(inputs):
    f = lambda n: np.ascontiguousarray(np.asarray(inputs[n]))
    kc = lambda w: np.ascontiguousarray(w.reshape(-1, 128, w.shape[-1]).transpose(1, 0, 2))
    bc = lambda v, n=128: np.ascontiguousarray(np.broadcast_to(v.reshape(1, -1), (n, v.size)))
    a = {}
    x = f("L0_attn_x")
    a["x"] = np.ascontiguousarray(x.reshape(32, 128, 256).transpose(1, 0, 2))
    a["xt"] = np.ascontiguousarray(x.reshape(4, 8, 128, 2, 128).transpose(1, 4, 3, 0, 2).reshape(8, 128, 8, 128))
    a["wq0"], a["wk0"], a["wv0"], a["wg0"] = (kc(f("L0_attn_W" + n)) for n in "qkvg")
    a["wgk1"] = kc(f("L0_attn_Wgk1"))
    a["wgk2"] = f("L0_attn_Wgk2")
    a["bgk2"] = f("L0_attn_bgk2").reshape(1, 256)
    a["wo0"] = kc(f("L0_attn_Wo"))
    a["rms"] = bc(np.tile(f("L0_attn_rms_w"), 4))
    a["gam"], a["bet"] = bc(f("L0_ffn_ln_gamma")), bc(f("L0_ffn_ln_beta"))
    i = np.arange(128)
    same = (i[:, None] // 64) == (i[None, :] // 64)
    up = same & (i[:, None] <= i[None, :])
    a["c_tri"] = up.astype(np.float32) / 16
    a["c_msk"] = up.astype(np.int32)
    a["c_idn"] = np.eye(128, dtype=np.float32)
    a["c_eps"] = np.tile(np.array([1e-5, 1e-6, 1.0, 0.0], np.float32), (128, 1))
    a["c_irev"] = np.tile(np.arange(8, 0, -1).astype(np.float32), (128, 1))
    tk = lambda w: kc(np.ascontiguousarray(w.T))
    a["rw"] = tk(f("L0_ffn_router_w"))
    a["gu"] = np.stack([tk(w) for w in f("L0_ffn_gate_up_w")])
    a["dn"] = np.stack([tk(w) for w in f("L0_ffn_down_w")])
    a["sgu"], a["sdn"] = tk(f("L0_ffn_shared_gate_up_w")), tk(f("L0_ffn_shared_down_w"))
    other = (np.arange(512) // 16) * 16 + (np.arange(512) + 8) % 16
    w, bb = [], []
    for n in "qk":
        W, v = f("L1_attn_W" + n), f("L1_attn_b" + n)
        w.append(tk(np.concatenate([W, W[other]])))
        bb.append(np.stack([v.reshape(4, 128).T, v[other].reshape(4, 128).T], 1))
    a["wqk"] = np.stack(w)
    a["bqk"] = np.ascontiguousarray(np.stack(bb, 1))
    inv = (1.0 / np.float32(10000.0) ** (np.arange(8, dtype=np.float32) / np.float32(8))).astype(np.float32)
    ang = (np.arange(1024, dtype=np.float32)[None, :] * inv[:, None]).astype(np.float32)
    row = np.arange(128) % 16
    sign = np.where(row < 8, -1.0, 1.0).astype(np.float32)[:, None]
    a["c_cs"] = np.ascontiguousarray(np.stack([np.cos(ang)[row % 8], np.sin(ang)[row % 8] * sign], 1).astype(np.float32))
    later = np.where(i[None, :] > i[:, None], -1e30, 0.0).astype(np.float32)
    a["c_mrc"] = np.concatenate([later, later.T], 1)
    a["wv1"], a["wo1"] = tk(f("L1_attn_Wv")), tk(f("L1_attn_Wo"))
    a["bv"], a["bo"], a["hn"] = bc(f("L1_attn_bv")), bc(f("L1_attn_bo")), bc(f("L1_attn_head_norm_w"))
    a["lam"] = np.ascontiguousarray(np.stack([bc(f("L1_attn_" + n)) for n in ("lq1", "lk1", "lq2", "lk2")], 1))
    a["wr2"] = kc(f("L1_ffn_Wr"))
    a["wi"] = np.stack([kc(w) for w in f("L1_ffn_Wi")])
    a["wo2"] = np.stack([kc(w) for w in f("L1_ffn_Wo")])
    return a


def kernel(**inputs):
    import concourse.bacc as bacc
    from concourse.bass_utils import run_bass_kernel_spmd

    a = layout(inputs)
    nc = bacc.Bacc("TRN2", target_bir_lowering=False, num_devices=1)
    aps = {k: nc.dram_tensor("in_" + k, v.shape, mybir.dt.from_np(v.dtype), kind="ExternalInput").ap() for k, v in a.items()}
    out = nc.dram_tensor("out_0_dram", (128, 32, 256), F32, kind="ExternalOutput").ap()
    program(nc, aps, out)
    r = run_bass_kernel_spmd(nc, [{"in_" + k: v for k, v in a.items()}], core_ids=[0])
    got = r.results[0]["out_0_dram"]
    return np.ascontiguousarray(got.transpose(1, 0, 2).reshape(4, 1024, 256))
```

```python
from contextlib import ExitStack

import numpy as np
import concourse.bass as bass
from concourse import mybir

F32 = mybir.dt.float32
BF16 = mybir.dt.bfloat16
I32 = mybir.dt.int32
U32 = mybir.dt.uint32
NT = 71
ALU = mybir.AluOpType
ACT = mybir.ActivationFunctionType
AX = mybir.AxisListType.X


class Op:

    def __init__(self, eng, fn, waits, step=1):
        self.eng, self.fn, self.waits, self.step = eng, fn, waits, step
        self.sem, self.value, self.marked = None, 0, False


def flat(x):
    out = []
    for y in x:
        if isinstance(y, (list, tuple)):
            out += flat(y)
        elif y is not None:
            out.append(y)
    return out


class Queues:

    ENGINES = ("pe", "dve", "act", "pool", "sp")

    def __init__(self, nc, ctx, ndma):
        self.q = {e: [] for e in self.ENGINES}
        self.sem = {e: ctx.enter_context(nc.semaphore(f"done_{e}")) for e in self.ENGINES}
        self.dsem = [ctx.enter_context(nc.semaphore(f"dma{i}")) for i in range(ndma)]
        self.dlast = [None] * ndma
        self.n = 0
        self.isem = [ctx.enter_context(nc.semaphore(f"idma{i}")) for i in range(16)]
        self.ilast = [None] * 16
        self.ni = 0

    def add(self, eng, fn, *waits):
        op = Op(eng, fn, flat(waits))
        op.sem = self.sem[eng]
        for w in op.waits:
            w.marked = True
        self.q[eng].append(op)
        return op

    def dma(self, eng, out, in_, *waits):
        k = self.n % len(self.dsem)
        self.n += 1
        waits = flat(waits) + ([self.dlast[k]] if self.dlast[k] else [])
        op = Op(eng, lambda e: e.dma_start(out, in_), waits, 16)
        op.sem, op.marked = self.dsem[k], True
        op.value = 16 + (self.dlast[k].value if self.dlast[k] else 0)
        for w in waits:
            w.marked = True
        self.dlast[k] = op
        self.q[eng].append(op)
        return op

    def idma(self, out, out_off, in_, in_off, *waits):
        k = self.ni % len(self.isem)
        self.ni += 1
        waits = flat(waits) + ([self.ilast[k]] if self.ilast[k] else [])
        op = Op("pool", lambda e: e.indirect_dma_start(out, out_off, in_, in_off), waits, 16)
        op.sem, op.marked = self.isem[k], True
        op.value = 16 + (self.ilast[k].value if self.ilast[k] else 0)
        for w in waits:
            w.marked = True
        self.ilast[k] = op
        self.q["pool"].append(op)
        return op

    def last(self):
        out = [d for d in self.dlast + self.ilast if d]
        for e in self.ENGINES:
            own = [o for o in self.q[e] if o.step == 1]
            if own:
                out.append(own[-1])
        return out

    def barrier(self):
        end = self.last()
        for e in self.ENGINES:
            self.q[e].append(Op(e, None, [o for o in end]))
        for o in end:
            o.marked = True

    def emit(self, nc, ctx):
        for e in self.ENGINES:
            n = 0
            for o in self.q[e]:
                if o.step == 1 and o.fn and o.marked:
                    n += 1
                    o.value = n
        block = ctx.enter_context(nc.Block())
        heads = dict(pe=block.tensor, dve=block.vector, act=block.scalar, pool=block.gpsimd, sp=block.sync)
        for name in self.ENGINES:
            ops = self.q[name]

            def body(e, ops=ops):
                seen = {}
                for o in ops:
                    for w in o.waits:
                        k = id(w.sem)
                        if seen.get(k, 0) < w.value:
                            e.wait_ge(w.sem, w.value)
                            seen[k] = w.value
                    if o.fn:
                        ins = o.fn(e)
                        if o.marked and o.step:
                            ins.then_inc(o.sem, o.step)

            heads[name](body)


def program(nc, A, out, stages=9, dbg=None):
    with ExitStack() as ctx:
        def sb(name, shape, dt=F32, c=ctx):
            return c.enter_context(nc.sbuf_tensor(name, shape, dt))

        Q = Queues(nc, ctx, 40)
        PS = ctx.enter_context(nc.psum_tensor("PS", [128, 8, 512], F32))

        def pe(fn, *w): return Q.add("pe", fn, *w)
        def dve(fn, *w): return Q.add("dve", fn, *w)
        def act(fn, *w): return Q.add("act", fn, *w)
        def pool(fn, *w): return Q.add("pool", fn, *w)

        def mm(o, l, r, start=True, stop=True, w=(), skip=False):
            return pe(lambda e: e.matmul(o, l, r, start=start, stop=stop, skip_group_check=skip), *w)

        def tr(o, i, w=()):
            n = i.shape[0]
            return pe(lambda e: e.transpose(o, i, IDN[0:n, 0:n]), *w)

        def load(name, dst, src, *w, eng="sp"):
            return Q.dma(eng, dst, src, *w)

        banks = [(k, []) for k in range(8)]

        def take():
            return banks.pop(0)

        def give(k, *ops):
            banks.append((k, flat(ops)))

        IDN = sb("IDN", [128, 128])
        EPS = sb("EPS", [128, 4])
        ST = sb("ST", [128, 4, 6])
        MV = sb("MV", [128, 4, 2])
        LV = sb("LV", [128, 4])
        RS = sb("RS", [128, 4])
        IREV = sb("IREV", [128, 8])
        GT = [sb(f"GT{i}", [128, 32]) for i in range(2)]
        PI = [sb(f"PI{i}", [128, 32], U32) for i in range(2)]
        XS_D = nc.dram_tensor("xs_sorted", (128 * NT, 256), F32, kind="Internal").ap()
        YS_D = nc.dram_tensor("ys_sorted", (128 * NT, 256), F32, kind="Internal").ap()
        XR_D = nc.dram_tensor("x_resid", (128, 32, 256), F32, kind="Internal").ap()
        l_eps = Q.dma("sp", EPS[:], A["c_eps"])
        l_idn = Q.dma("sp", IDN[:], A["c_idn"])
        l_irev = Q.dma("sp", IREV[:], A["c_irev"])

        def rsqrt(dst, src, tmp, scale, epscol, *w):
            a = act(lambda e: e.activation(tmp, src, ACT.Ln, bias=EPS[:, epscol:epscol + 1], scale=scale), l_eps, *w)
            return act(lambda e: e.activation(dst, tmp, ACT.Exp, scale=-0.5), a)

        ln_state = {"free": []}

        def layernorm(tiles, outs, *w):
            ops = []
            for i, t in enumerate(tiles):
                a = dve(lambda e, i=i, t=t: e.bn_stats(ST[:, i, :], t), *w, ln_state["free"])
                ops.append(a)
            for i in range(len(tiles)):
                a = dve(lambda e, i=i: e.bn_aggr(MV[:, i, :], ST[:, i, :]), ops[i])
            n = len(tiles)
            r = rsqrt(RS[:, 0:n], MV[:, 0:n, 1], LV[:, 0:n], 1.0, 0, a)
            res = []
            for i, (t, o) in enumerate(zip(tiles, outs)):
                res.append(dve(lambda e, i=i, t=t, o=o: e.tensor_scalar(
                    o, t, MV[:, i, 0:1], RS[:, i:i + 1], ALU.subtract, ALU.mult), r))
            ln_state["free"] = [res[-1]]
            return res

        cA = ExitStack()
        NALL = sb("NALL", [128, 32, 256], F32, cA)
        LGA = sb("LGA", [128, 32, 8], F32, cA)
        nav = NALL[:].rearrange("p (b t) d -> p b t d", b=4)
        lgv = LGA[:].rearrange("p (b t) e -> p b t e", b=4)
        x_in = A["x"].rearrange("p (b t) d -> p b t d", b=4)
        x_out = XR_D.rearrange("p (b t) d -> p b t d", b=4)
        with ExitStack() as c1:
            s1 = lambda n, s, d=F32: sb(n, s, d, c1)
            WQ, WK = s1("WQ", [128, 2, 256]), s1("WK", [128, 2, 256])
            WV, WG = s1("WV", [128, 2, 512]), s1("WG", [128, 2, 512])
            W1 = s1("W1", [128, 2, 16])
            W2 = s1("W2", [128, 256])
            WO = s1("WO", [128, 4, 256])
            RMS = s1("RMS", [128, 512])
            GAM, BET = s1("GAM", [128, 256]), s1("BET", [128, 256])
            SGU, SDN = s1("SGU", [128, 2, 512]), s1("SDN", [128, 2, 256])
            RW = s1("RW", [128, 2, 8])
            TRI = s1("TRI", [128, 128])
            MSK = s1("MSK", [128, 128], I32)
            XTS = [s1(f"XTS{i}", [128, 2, 4, 128]) for i in range(2)]
            XS = [s1(f"XS{i}", [128, 4, 256]) for i in range(2)]
            NTT = s1("NTT", [128, 2, 4, 128])
            XG = s1("XG", [128, 512])
            GA, GE, GG = s1("GA", [128, 1024]), s1("GE", [128, 1024]), s1("GG", [128, 1024])
            EP, EM = s1("EP", [128, 2, 512]), s1("EM", [128, 2, 512])
            QG = s1("QG", [128, 2, 2, 512])
            KD, KG = s1("KD", [128, 2, 512]), s1("KG", [128, 2, 512])
            KZ = s1("KZ", [128, 2, 4, 256])
            V = s1("V", [128, 4, 512])
            AT = s1("AT", [128, 16, 128])
            SG = s1("SG", [128, 4, 512])
            Y = s1("Y", [128, 4, 512])
            YT = s1("YT", [128, 16, 128])
            S = s1("S", [128, 2, 2, 4, 128])
            SQ = s1("SQ", [128, 128])
            HS = s1("HS", [128, 2, 512])
            SU = s1("SU", [128, 2, 512])
            SS, SL, SR = s1("SS", [128, 16]), s1("SL", [128, 16]), s1("SR", [128, 16])

            lx, lxs = {}, {}

            def load_x(t, *w):
                lx[t] = Q.dma("sp", XTS[t % 2][:].rearrange("p k b s -> p (k b) s"), A["xt"][t], *w)
                lxs[t] = Q.dma("sp", XS[t % 2][:], x_in[:, :, t, :], *w)

            l_w1 = Q.dma("sp", W1[:], A["wgk1"])
            load_x(0)
            l_w2 = Q.dma("sp", W2[:], A["wgk2"])
            l_q = Q.dma("sp", WQ[:], A["wq0"])
            l_k = Q.dma("sp", WK[:], A["wk0"])
            l_v = Q.dma("sp", WV[:], A["wv0"])
            l_g = Q.dma("sp", WG[:], A["wg0"])
            l_tri = Q.dma("sp", TRI[:], A["c_tri"])
            l_msk = Q.dma("sp", MSK[:], A["c_msk"])
            l_rms = Q.dma("sp", RMS[:], A["rms"])
            l_o = Q.dma("sp", WO[:], A["wo0"])
            load_x(1)
            l_gam = Q.dma("sp", GAM[:], A["gam"])
            l_bet = Q.dma("sp", BET[:], A["bet"])
            l_rw, l_sg, l_sd = Q.dma("sp", RW[:], A["rw"]), Q.dma("sp", SGU[:], A["sgu"]), Q.dma("sp", SDN[:], A["sdn"])

            z_xg = pool(lambda e: e.memset(XG[:], 1.0))
            z_qg = pool(lambda e: e.memset(QG[:], 0.0))
            z_kz = pool(lambda e: e.memset(KZ[:], 0.0))
            z_at = pool(lambda e: e.memset(AT[:], 0.0))
            z_s = pool(lambda e: e.memset(S[:], 0.0))
            z_na = pool(lambda e: e.memset(NALL[:], 0.0))
            zx = [Q.dma("sp", XS_D[1024 * c:min(1024 * c + 1024, 128 * NT), :].rearrange("(a p) d -> p a d", p=128),
                        NALL[:, 0:min(8, NT - 8 * c), :], z_na) for c in range((NT + 7) // 8)]

            f = {k: [] for k in "xg ga ge gg ep em qg kd kg kz v at sg y yt sr ntt hs su".split()}
            s_ready = [z_s] * 8
            s_read = [[] for _ in range(8)]
            xts_read = {}
            G = {}

            def explog():
                act(lambda e: e.preload_act_table_set("natural_log_exp_and_others"))

            def a1(t):
                XTt = XTS[t % 2]
                xt = [XTt[:, k] for k in range(2)]
                bt = lambda k: PS[:, k, :].rearrange("p (b s) -> p b s", b=4)
                g_ = G[t] = {}
                kb, fr = take()
                mm(PS[0:16, kb, :].rearrange("p (b s) -> p b s", b=4), W1[:, 0, :], xt[0], True, False, [fr, lx[t], l_w1])
                a = mm(PS[0:16, kb, :].rearrange("p (b s) -> p b s", b=4), W1[:, 1, :], xt[1], False, True)
                xg = act(lambda e, kb=kb: e.activation(XG[0:16, :], PS[0:16, kb, :], ACT.Copy), a, z_xg, f["xg"])
                give(kb, xg)
                qk = []
                for W, l in ((WQ, l_q), (WK, l_k)):
                    for h in range(2):
                        kb, fr = take()
                        mm(bt(kb), W[:, 0, 128 * h:128 * h + 128], xt[0], True, False, [fr, l])
                        qk.append((kb, mm(bt(kb), W[:, 1, 128 * h:128 * h + 128], xt[1], False, True)))
                g2 = []
                explog()
                for p in range(2):
                    kb, fr = take()
                    for j in range(2):
                        b = 2 * p + j
                        a = mm(PS[:, kb, 256 * j:256 * j + 256], XG[:, 128 * b:128 * b + 128], W2[:],
                               True, True, [fr, xg, l_w2])
                    f["xg"] = [a]
                    c0 = 512 * p
                    z1 = act(lambda e, kb=kb, c0=c0: e.activation(GA[:, c0:c0 + 512], PS[:, kb, :], ACT.Abs), a, f["ga"])
                    z2 = act(lambda e, c0=c0: e.activation(GE[:, c0:c0 + 512], GA[:, c0:c0 + 512], ACT.Exp, scale=-1.0), z1, f["ge"])
                    z3 = act(lambda e, c0=c0: e.activation(GA[:, c0:c0 + 512], GE[:, c0:c0 + 512], ACT.Ln, bias=EPS[:, 2:3]), z2, l_eps)
                    z4 = dve(lambda e, kb=kb, c0=c0: e.scalar_tensor_tensor(
                        out=GG[:, c0:c0 + 512], in0=PS[:, kb, :], scalar=0.0, in1=GA[:, c0:c0 + 512],
                        op0=ALU.min, op1=ALU.subtract), z3, f["gg"])
                    give(kb, z4)
                    g2.append(z4)
                f["ga"], f["ge"] = g2, [z3]
                vr = []
                for b in range(4):
                    kb, fr = take()
                    mm(PS[:, kb, :], xt[0][:, b, :], WV[:, 0, :], True, False, [fr, l_v])
                    a = mm(PS[:, kb, :], xt[1][:, b, :], WV[:, 1, :], False, True)
                    a = act(lambda e, kb=kb, b=b: e.activation(V[:, b, :], PS[:, kb, :], ACT.Copy), a, f["v"])
                    give(kb, a)
                    vr.append(a)
                g_.update(qk=qk, g2=g2, vr=vr)

            def a1g(t):
                XTt = XTS[t % 2]
                sgr = []
                for b in range(4):
                    kb, fr = take()
                    mm(PS[:, kb, :], XTt[:, 0, b, :], WG[:, 0, :], True, False, [fr, l_g])
                    a = mm(PS[:, kb, :], XTt[:, 1, b, :], WG[:, 1, :], False, True)
                    xts_read[t] = [a]
                    a = act(lambda e, kb=kb, b=b: e.activation(SG[:, b, :], PS[:, kb, :], ACT.Silu), a, f["sg"])
                    give(kb, a)
                    a = pool(lambda e, b=b: e.tensor_tensor(SG[:, b, :], SG[:, b, :], RMS[:], ALU.mult), a, l_rms)
                    sgr.append(a)
                G[t]["sgr"] = sgr

            def a2(t):
                g_ = G[t]
                qk, g2 = g_["qk"], g_["g2"]
                qgr, kdr, kgr = [], [], []
                for h in range(2):
                    kb, fr = take()
                    for b in range(4):
                        a = mm(PS[:, kb, 128 * b:128 * b + 128], GG[:, 256 * b + 128 * h:256 * b + 128 * h + 128], TRI[:],
                               True, True, [fr, g2, l_tri])
                    e1 = act(lambda e, kb=kb, h=h: e.activation(EP[:, h, :], PS[:, kb, :], ACT.Exp), a, f["ep"])
                    e2 = act(lambda e, kb=kb, h=h: e.activation(EM[:, h, :], PS[:, kb, :], ACT.Exp, scale=-1.0), a, f["em"])
                    give(kb, e2)
                    f["gg"] = [a]
                    kq, mq = qk[h]
                    for hh in range(2):
                        r = slice(64 * hh, 64 * hh + 64)
                        a = dve(lambda e, r=r, h=h, hh=hh, kq=kq: e.scalar_tensor_tensor(
                            out=QG[r, h, hh, :], in0=PS[r, kq, :], scalar=0.125, in1=EP[r, h, :],
                            op0=ALU.mult, op1=ALU.mult), e1, mq, z_qg, f["qg"])
                    give(kq, a)
                    qgr.append(a)
                    kk, mk = qk[2 + h]
                    a = dve(lambda e, h=h, kk=kk: e.tensor_tensor(KD[:, h, :], PS[:, kk, :], EM[:, h, :], ALU.mult), e2, mk, f["kd"])
                    give(kk, a)
                    kdr.append(a)
                    lastc = EP[:, h, :].rearrange("p (c s) -> p c s", s=64)[:, :, 63:64].to_broadcast([128, 8, 64])
                    a = pool(lambda e, h=h, lastc=lastc: e.tensor_tensor(
                        KG[:, h, :].rearrange("p (c s) -> p c s", s=64), KD[:, h, :].rearrange("p (c s) -> p c s", s=64),
                        lastc, ALU.mult), a, e1, f["kg"])
                    kgr.append(a)
                f["em"] = kdr
                g_.update(qgr=qgr, kdr=kdr, kgr=kgr)

            def a3(t):
                g_ = G[t]
                qgr, kdr, kgr = g_["qgr"], g_["kdr"], g_["kgr"]
                atr = []
                for h in range(2):
                    for p in range(2):
                        kb, fr = take()
                        for j in range(2):
                            b = 2 * p + j
                            a = mm(PS[:, kb, 256 * j:256 * j + 256].rearrange("p (h s) -> p h s", h=2),
                                   KD[:, h, 128 * b:128 * b + 128], QG[:, h, :, 128 * b:128 * b + 128],
                                   True, True, [fr, qgr, kdr])
                        dst = AT[:].rearrange("p (b g) s -> p b g s", b=4)[:, 2 * p:2 * p + 2, 2 * h:2 * h + 2, :]
                        for j in range(2):
                            a2_ = dve(lambda e, kb=kb, j=j, dst=dst: e.copy_predicated(
                                dst[:, j], MSK[:].unsqueeze(1).to_broadcast([128, 2, 128]),
                                PS[:, kb, 256 * j:256 * j + 256].rearrange("p (h s) -> p h s", h=2)),
                                a, z_at, l_msk, f["at"])
                        give(kb, a2_)
                        atr.append(a2_)
                f["kd"] = [a, kgr]
                kzr = []
                for p in range(2):
                    kb, fr = take()
                    for j in range(2):
                        for h in range(2):
                            b = 2 * p + j
                            a = tr(PS[:, kb, 256 * j + 128 * h:256 * j + 128 * h + 128], KG[:, h, 128 * b:128 * b + 128],
                                   [fr, kgr, l_idn])
                    for c in range(2):
                        r = slice(64 * c, 64 * c + 64)
                        a2_ = act(lambda e, r=r, c=c, p=p, kb=kb: e.activation(
                            KZ[r, c, 2 * p:2 * p + 2, :], PS[r, kb, :].rearrange("p (b s) -> p b s", b=2), ACT.Copy), a, z_kz, f["kz"])
                    give(kb, a2_)
                    kzr.append(a2_)
                f["kg"] = [a]
                g_.update(atr=atr, kzr=kzr)

            def a4(t):
                g_ = G[t]
                atr, kzr, kgr, vr, sgr = (g_[k] for k in ("atr", "kzr", "kgr", "vr", "sgr"))
                ob = []
                for b in range(4):
                    kb, fr = take()
                    for hd in range(4):
                        a = mm(PS[:, kb, 128 * hd:128 * hd + 128], AT[:, 4 * b + hd, :], V[:, b, 128 * hd:128 * hd + 128],
                               hd == 0, False, [fr, atr, vr], skip=True)
                    ob.append(kb)
                f["at"] = [a]
                sk = {}
                oend = [None] * 4
                for c in range(2):
                    cur, nxt = c, 1 - c
                    for h in range(2):
                        kb, fr = take()
                        for b in range(4):
                            for hh in range(2):
                                hd = 2 * h + hh
                                a = mm(PS[64 * hh:64 * hh + 64, kb, 128 * b:128 * b + 128],
                                       KZ[:, c, b, 64 * hd:64 * hd + 64], V[:, b, 128 * hd:128 * hd + 128],
                                       True, True, [fr, kzr])
                        sk[h] = (kb, a)
                    kzl = a
                    for b in range(4):
                        for h in range(2):
                            for hh in range(2):
                                hd = 2 * h + hh
                                a = mm(PS[64 * c:64 * c + 64, ob[b], 128 * hd:128 * hd + 128],
                                       QG[:, h, hh, 128 * b + 64 * c:128 * b + 64 * c + 64], S[:, cur, h, b, :],
                                       False, c == 1, [s_ready[4 * h + b]], skip=True)
                            s_read[4 * h + b] = [a]
                        oend[b] = a
                    for h in range(2):
                        kb, m_ = sk[h]
                        for b in range(4):
                            ecol = EP[:, h, 128 * b + 64 * c + 63:128 * b + 64 * c + 64]
                            s_ready[4 * h + b] = dve(lambda e, h=h, b=b, kb=kb, cur=cur, nxt=nxt, ecol=ecol: e.scalar_tensor_tensor(
                                out=S[:, nxt, h, b, :], in0=S[:, cur, h, b, :], scalar=ecol,
                                in1=PS[:, kb, 128 * b:128 * b + 128], op0=ALU.mult, op1=ALU.add),
                                m_, s_ready[4 * h + b])
                        give(kb, s_ready[4 * h + 3])
                        f["ep"] = [s_ready[4 * h + 3], kgr]
                f["kz"], f["v"], f["qg"] = [kzl], [kzl], [oend[3]]
                for b in range(4):
                    for hd in range(4):
                        i = 4 * b + hd
                        a = act(lambda e, b=b, hd=hd, i=i, kb=ob[b]: e.activation(
                            SQ[:], PS[:, kb, 128 * hd:128 * hd + 128], ACT.Square, accum_out=SS[:, i:i + 1]),
                            oend[b], a if i else f["sr"])
                r = rsqrt(SR[:], SS[:], SL[:], 1.0 / 128, 0, a, f["sr"])
                yr = []
                for b in range(4):
                    for hd in range(4):
                        i = 4 * b + hd
                        a = dve(lambda e, b=b, hd=hd, i=i, kb=ob[b]: e.scalar_tensor_tensor(
                            out=Y[:, b, 128 * hd:128 * hd + 128], in0=PS[:, kb, 128 * hd:128 * hd + 128],
                            scalar=SR[:, i:i + 1], in1=SG[:, b, 128 * hd:128 * hd + 128], op0=ALU.mult, op1=ALU.mult),
                            r, sgr[b], f["y"])
                    give(ob[b], a)
                    yr.append(a)
                f["sg"], f["sr"] = [a], [a]
                g_["yr"] = yr

            def b1(t):
                g_ = G[t]
                yr = g_["yr"]
                ytr = []
                for b in range(4):
                    kb, fr = take()
                    for hd in range(4):
                        a = tr(PS[:, kb, 128 * hd:128 * hd + 128], Y[:, b, 128 * hd:128 * hd + 128], [fr, yr[b]])
                    a2_ = act(lambda e, b=b, kb=kb: e.activation(YT[:, 4 * b:4 * b + 4, :], PS[:, kb, :].rearrange("p (h s) -> p h s", h=4), ACT.Copy), a, f["yt"])
                    give(kb, a2_)
                    ytr.append(a2_)
                f["y"] = [a]
                g_["ytr"] = ytr

            def b2(t):
                g_ = G[t]
                ytr = g_["ytr"]
                xs_t = XS[t % 2]
                res = []
                for p in range(2):
                    kb, fr = take()
                    for j in range(2):
                        b = 2 * p + j
                        for hd in range(4):
                            a = mm(PS[:, kb, 256 * j:256 * j + 256], YT[:, 4 * b + hd, :], WO[:, hd, :], hd == 0, hd == 3,
                                   [fr, ytr[b], l_o])
                    a2_ = dve(lambda e, p=p, kb=kb: e.tensor_tensor(
                        xs_t[:, 2 * p:2 * p + 2, :], xs_t[:, 2 * p:2 * p + 2, :],
                        PS[:, kb, :].rearrange("p (b d) -> p b d", b=2), ALU.add), a, lxs[t])
                    give(kb, a2_)
                    res.append(a2_)
                f["yt"] = [a]
                xs = [xs_t[:, b, :] for b in range(4)]
                n1 = layernorm(xs, xs, res)
                n2 = layernorm(xs, [nav[:, b, t, :] for b in range(4)], n1, zx)
                a = pool(lambda e: e.tensor_tensor(nav[:, :, t, :], nav[:, :, t, :], GAM[:].unsqueeze(1).to_broadcast([128, 4, 256]), ALU.mult), n2, l_gam)
                a = pool(lambda e: e.tensor_tensor(nav[:, :, t, :], nav[:, :, t, :], BET[:].unsqueeze(1).to_broadcast([128, 4, 256]), ALU.add), a, l_bet)
                g_.update(n1=n1, nr=a)

            def b3(t):
                g_ = G[t]
                ntr = []
                for k in range(2):
                    kb, fr = take()
                    for b in range(4):
                        a = tr(PS[:, kb, 128 * b:128 * b + 128], nav[:, b, t, 128 * k:128 * k + 128], [fr, g_["nr"]])
                    a = dve(lambda e, k=k, kb=kb: e.tensor_copy(NTT[:, k], PS[:, kb, :].rearrange("p (b s) -> p b s", b=4)), a, f["ntt"])
                    give(kb, a)
                    ntr.append(a)
                g_["ntr"] = ntr

            def b4(t):
                g_ = G[t]
                ntr = g_["ntr"]
                kb, fr = take()
                for b in range(4):
                    mm(PS[:, kb, 8 * b:8 * b + 8], NTT[:, 0, b, :], RW[:, 0, :], True, False, [fr, ntr, l_rw])
                    a = mm(PS[:, kb, 8 * b:8 * b + 8], NTT[:, 1, b, :], RW[:, 1, :], False, True)
                a = dve(lambda e, kb=kb: e.tensor_copy(lgv[:, :, t, :], PS[:, kb, 0:32].rearrange("p (b e) -> p b e", b=4)), a)
                give(kb, a)
                hr = []
                for fx in range(2):
                    ks = []
                    for o in range(2):
                        kb, fr = take()
                        c0 = 256 * o + 128 * fx
                        mm(PS[:, kb, :].rearrange("p (b s) -> p b s", b=4), SGU[:, 0, c0:c0 + 128], NTT[:, 0], True, False, [fr, l_sg])
                        ks.append((kb, mm(PS[:, kb, :].rearrange("p (b s) -> p b s", b=4), SGU[:, 1, c0:c0 + 128], NTT[:, 1], False, True)))
                    (kg, mg), (ku, mu) = ks
                    a1_ = act(lambda e, kg=kg, fx=fx: e.activation(SU[:, fx, :], PS[:, kg, :], ACT.Silu), mg, f["su"])
                    give(kg, a1_)
                    a2_ = dve(lambda e, ku=ku, fx=fx: e.tensor_tensor(HS[:, fx, :], PS[:, ku, :], SU[:, fx, :], ALU.mult), mu, a1_, f["hs"])
                    give(ku, a2_)
                    hr.append(a2_)
                f["ntt"], f["su"] = [mu], [a2_]
                g_["hr"] = hr

            def b5(t):
                g_ = G[t]
                xs_t = XS[t % 2]
                for p in range(2):
                    kb, fr = take()
                    for j in range(2):
                        b = 2 * p + j
                        for fx in range(2):
                            a = mm(PS[:, kb, 256 * j:256 * j + 256], HS[:, fx, 128 * b:128 * b + 128], SDN[:, fx, :], fx == 0, fx == 1,
                                   [fr, g_["hr"], l_sd])
                    a2_ = dve(lambda e, p=p, kb=kb: e.tensor_tensor(
                        xs_t[:, 2 * p:2 * p + 2, :], xs_t[:, 2 * p:2 * p + 2, :],
                        PS[:, kb, :].rearrange("p (b d) -> p b d", b=2), ALU.add), a, g_["n1"], g_["nr"])
                    give(kb, a2_)
                f["hs"] = [a]
                st = Q.dma("sp", x_out[:, :, t, :], xs_t[:], a2_)
                if t + 2 < 8:
                    load_x(t + 2, st, xts_read[t])

            for t in range(9):
                if t < 8:
                    a1(t)
                if t > 0:
                    b1(t - 1)
                if t < 8:
                    a2(t)
                    a1g(t)
                if t > 0:
                    b2(t - 1)
                if t < 8:
                    a3(t)
                if t > 0:
                    b3(t - 1)
                if t < 8:
                    a4(t)
                if t > 0:
                    b4(t - 1)
                    b5(t - 1)
            Q.barrier()

        def finish():
            o = Q.dma("sp", out, X[:], Q.last())
            Q.q["sp"].append(Op("sp", None, [o]))
            if dbg is not None:
                dd = Q.dma("sp", dbg, XT[:], Q.last())
                Q.q["sp"].append(Op("sp", None, [dd]))
            Q.emit(nc, ctx)

        if stages < 2:
            return finish()
        def choose(lg, tag, c, *w):
            b3 = [128, 32, 8]
            LG, PB, OH, T8 = (sb(n + tag, b3, F32, c) for n in ("LG", "PB", "OH", "T8"))
            M1, M2, R1 = (sb(n + tag, [128, 32], F32, c) for n in ("M1", "M2", "R1"))
            up = lambda m: m.unsqueeze(2).to_broadcast(b3)
            a = red(M1[:], lg, ALU.max, *w)
            a = tt(LG[:], lg, up(M1[:]), ALU.subtract, a)
            lg_read = a
            a = act(lambda e: e.activation(PB[:], LG[:], ACT.Exp), a)
            a = red(M2[:], PB[:], ALU.add, a)
            a = dve(lambda e: e.reciprocal(R1[:], M2[:]), a)
            a = tt(PB[:], PB[:], up(R1[:]), ALU.mult, a)

            def top(m, oh, r, a):
                a = red(m[:], PB[:], ALU.max, a)
                a = tt(T8[:], PB[:], up(m[:]), ALU.is_equal, a)
                a = tt(T8[:], T8[:], IREV[:].unsqueeze(1).to_broadcast(b3), ALU.mult, a, l_irev)
                a = red(r[:], T8[:], ALU.max, a)
                return tt(oh[:], T8[:], up(r[:]), ALU.is_equal, a)
            a = top(M1, OH, R1, a)
            a = dve(lambda e: e.scalar_tensor_tensor(out=PB[:], in0=OH[:], scalar=-2.0, in1=PB[:], op0=ALU.mult, op1=ALU.add), a)
            a = top(M2, LG, R1, a)
            return OH, LG, M1, M2, R1, T8, lg_read, a

        tt = lambda o, x, y, op, *w: dve(lambda e: e.tensor_tensor(o, x, y, op), *w)
        red = lambda o, x, op, *w: dve(lambda e: e.tensor_reduce(o, x, AX, op), *w)

        with ExitStack() as c2:
            s2 = lambda n, s, d=F32: sb(n, s, d, c2)
            WALL = s2("WALL", [128, 8 * 4608])
            SLT, ONE = s2("SLT", [128, 128]), s2("ONE", [128, 128])
            CNT = s2("CNT", [128, 104])
            INC = s2("INC", [128, 32, 8])
            TL, IT, BT_ = (s2(n, [128, 8]) for n in ("TL", "IT", "BT_"))
            TE = s2("TE", [128, 72])
            TI = s2("TI", [128, 72], I32)
            PF = s2("PF", [128, 32])
            XI = [s2(f"XI{i}", [128, 256]) for i in range(3)]
            XIT = [s2(f"XIT{i}", [128, 2, 128]) for i in range(2)]
            SI = s2("SI", [128, 768])
            HI = s2("HI", [128, 768])
            HT = s2("HT", [128, 6, 128])
            t8 = lambda m: m.rearrange("p (t e) -> p t e", e=8)
            CC, TOT = t8(SI[:, 0:256]), t8(SI[:, 256:512])
            C32 = SI[:, 512:768].rearrange("p (e t) -> p e t", t=32)
            CT = t8(HI[:, 0:576])
            POS = t8(HT[:].rearrange("p i s -> p (i s)")[:, 0:256])
            YI = [s2(f"YI{i}", [128, 256]) for i in range(2)]
            l_slt, l_cnt = Q.dma("sp", SLT[:], A["c_slt"]), Q.dma("sp", CNT[:], A["c_cnt"])
            l_we = [Q.dma("sp", WALL[:, 4608 * e_:4608 * e_ + 4608], A["we"][e_]) for e_ in range(8)]
            z_one = pool(lambda e: e.memset(ONE[:], 1.0))

            OH1, OH2, M1, M2, R1, T8, _, a = choose(LGA[:], "a", c2)
            g_ = tt(R1[:], M2[:], M1[:], ALU.subtract, a)
            g_ = act(lambda e: e.activation(R1[:], R1[:], ACT.Exp), g_)
            c_ = tt(CC, OH1[:], OH2[:], ALU.add, a)
            kb, fr = take()
            mm(PS[:, kb, 0:256], SLT[:], SI[:, 0:256], True, True, [fr, c_, l_slt])
            a = mm(PS[:, kb, 256:512], ONE[:], SI[:, 0:256], True, True, [z_one])
            pre = PS[:, kb, 0:256].rearrange("p (t e) -> p t e", e=8)
            tot = PS[:, kb, 256:512].rearrange("p (t e) -> p t e", e=8)
            a = dve(lambda e: e.tensor_copy(TOT, tot), a)
            for e_ in range(8):
                a2 = dve(lambda e, e_=e_: e.tensor_tensor_scan(INC[:, :, e_], ONE[:, 0:32], TOT[:, :, e_], 0.0, ALU.mult, ALU.add), a)
            a = a2
            cnt_b = INC[:, 31, :].unsqueeze(2).to_broadcast([128, 8, 32])
            a = tt(C32, cnt_b, CNT[:, 0:32].unsqueeze(1).to_broadcast([128, 8, 32]), ALU.is_gt, a, l_cnt)
            a = red(TL[:], C32, ALU.add, a)
            a = dve(lambda e: e.tensor_tensor_scan(IT[:], ONE[:, 0:8], TL[:], 0.0, ALU.mult, ALU.add), a)
            a2 = tt(BT_[:], IT[:], TL[:], ALU.subtract, a)
            a2 = tt(POS, INC[:], TOT, ALU.subtract, a2)
            a2 = tt(POS, pre, POS, ALU.add, a2)
            give(kb, a2)
            a2 = dve(lambda e: e.scalar_tensor_tensor(out=POS, in0=BT_[:].unsqueeze(1).to_broadcast([128, 32, 8]), scalar=128.0,
                                                      in1=POS, op0=ALU.mult, op1=ALU.add), a2)
            pr_ = []
            for k, oh in enumerate((OH1, OH2)):
                a2 = tt(T8[:], oh[:], POS, ALU.mult, a2)
                a2 = red(PF[:], T8[:], ALU.add, a2)
                a2 = dve(lambda e, k=k: e.tensor_copy(PI[k][:], PF[:]), a2)
                pr_.append(a2)
            a = tt(CT, IT[:].unsqueeze(1).to_broadcast([128, 72, 8]), CNT[:, 32:104].unsqueeze(2).to_broadcast([128, 72, 8]), ALU.is_le, a)
            a = red(TE[:], CT, ALU.add, a)
            a = dve(lambda e: e.tensor_scalar(TE[:], TE[:], 7.0, 4608.0, ALU.min, ALU.mult), a)
            te = dve(lambda e: e.tensor_copy(TI[:], TE[:]), a)
            te.marked = True
            g_ = dve(lambda e: e.tensor_scalar(GT[1][:], R1[:], 1.0, None, ALU.add), g_)
            g_ = dve(lambda e: e.reciprocal(GT[0][:], GT[1][:]), g_)
            g_ = tt(GT[1][:], R1[:], GT[0][:], ALU.mult, g_)

            sc = []
            for t in range(32):
                for k in range(2):
                    sc.append(Q.idma(XS_D, bass.IndirectOffsetOnAxis(PI[k][:, t:t + 1], 0), NALL[:, t, :], None, pr_))

            xf, xtf, yf = [[], [], []], [[], []], [[], []]
            set_free = [[[], [], []], [[], [], []]]
            b67 = [[], []]
            hif, htf, sif = [], [], []
            lx2, xtr2, hr2, ht2 = {}, {}, {}, {}

            def load_rows(s):
                lx2[s] = Q.dma("sp", XI[s % 3][:], XS_D[128 * s:128 * s + 128, :], sc, xf[s % 3])

            def turn_rows(s):
                bk = 6 + s % 2
                for k in range(2):
                    a = tr(PS[:, bk, 128 * k:128 * k + 128], XI[s % 3][:, 128 * k:128 * k + 128], [b67[s % 2], lx2[s]])
                xf[s % 3] = [a]
                a = dve(lambda e: e.tensor_copy(XIT[s % 2][:], PS[:, bk, 0:256].rearrange("p (k s) -> p k s", k=2)), a, xtf[s % 2])
                b67[s % 2] = [a]
                xtr2[s] = a

            regs = {}

            def wide(s, off, n):
                return lambda: WALL[:, bass.ds(regs["r"][s % 2] + off, n)]

            def mmr(o, l, get, start, stop, w=()):
                return pe(lambda e: e.matmul(o, l, get(), start=start, stop=stop), *w)

            def expert_of(s):
                def go(e):
                    regs.setdefault("r", {})[s % 2] = e.value_load(TI[0:1, s:s + 1], min_val=0, max_val=7 * 4608)
                    return None
                Q.q["pe"].append(Op("pe", go, [te]))
                Q.q["pe"][-1].step = 0

            def up_piece(s, c):
                bk = 3 * (s % 2) + c
                mmr(PS[:, bk, :], XIT[s % 2][:, 0, :], wide(s, 512 * c, 512), True, False, [set_free[s % 2][c], xtr2[s], l_we])
                return mmr(PS[:, bk, :], XIT[s % 2][:, 1, :], wide(s, 1536 + 512 * c, 512), False, True)

            def hidden(s, a):
                gu = PS[:, 3 * (s % 2):3 * (s % 2) + 3, :].rearrange("p k s -> p (k s)")
                a1_ = act(lambda e: e.activation(SI[:], gu[:, 0:768], ACT.Silu), a, sif)
                a2_ = dve(lambda e: e.tensor_tensor(HI[:], gu[:, 768:1536], SI[:], ALU.mult), a1_, a, hif)
                sif[:] = [a2_]
                for c in range(3):
                    set_free[s % 2][c] = [a2_]
                hr2[s] = a2_

            def turn_hidden(s):
                b0 = 3 * (s % 2)
                for i in range(6):
                    a = tr(PS[:, b0 + i // 4, 128 * (i % 4):128 * (i % 4) + 128], HI[:, 128 * i:128 * i + 128], [set_free[s % 2], hr2[s]])
                hif[:] = [a]
                a = act(lambda e: e.activation(HT[:].rearrange("p i s -> p (i s)"), PS[:, b0:b0 + 2, :].rearrange("p k s -> p (k s)")[:, 0:768], ACT.Copy), a, htf)
                set_free[s % 2][0] = set_free[s % 2][1] = [a]
                ht2[s] = a

            def down(s):
                bk = 3 * (s % 2) + 2
                for i in range(6):
                    a = mmr(PS[:, bk, 0:256], HT[:, i, :], wide(s, 3072 + 256 * i, 256), i == 0, i == 5, [set_free[s % 2][2], ht2[s]])
                htf[:] = [a]
                y = YI[s % 2]
                a = dve(lambda e: e.tensor_copy(y[:], PS[:, bk, 0:256]), a, yf[s % 2])
                set_free[s % 2][2] = [a]
                yf[s % 2] = [Q.dma("sp", YS_D[128 * s:128 * s + 128, :], y[:], a)]

            for s in range(2):
                load_rows(s)
            turn_rows(0)
            for s in range(NT + 1):
                if s < NT:
                    expert_of(s)
                    up_piece(s, 0)
                    if s + 2 < NT:
                        load_rows(s + 2)
                    up_piece(s, 1)
                if s > 0:
                    turn_hidden(s - 1)
                if s < NT:
                    a = up_piece(s, 2)
                    xtf[s % 2] = [a]
                    hidden(s, a)
                if s + 1 < NT:
                    turn_rows(s + 1)
                if s > 0:
                    down(s - 1)
            Q.barrier()
        cA.close()

        if stages < 3:
            return finish()
        PARTS = nc.dram_tensor("parts", (2, 3, 512, 4096), BF16, kind="Internal").ap()
        X = sb("X", [128, 32, 256])
        XT = sb("XT", [128, 2, 4096])
        with ExitStack() as c3:
            s3 = lambda n, s, d=F32: sb(n, s, d, c3)
            XL = [s3(f"XL{i}", [128, 4, 256]) for i in range(2)]
            YG = [s3(f"YG{i}", [128, 256]) for i in range(6)]
            ygf = [[] for _ in range(6)]
            xlf = [[], []]
            xtr = {}
            tt = lambda o, x, y, op, *w: dve(lambda e: e.tensor_tensor(o, x, y, op), *w)

            def combine(b):
                for q in range(2):
                    gI = 2 * b + q
                    xl = XL[gI % 2]
                    l_xl = Q.dma("sp", xl[:], XR_D[:, 4 * gI:4 * gI + 4, :], xlf[gI % 2])
                    for i in range(4):
                        t = 4 * gI + i
                        for k in range(2):
                            z = (2 * t + k) % 6
                            g = Q.idma(YG[z][:], None, YS_D, bass.IndirectOffsetOnAxis(PI[k][:, t:t + 1], 0), ygf[z])
                            src = xl[:, i, :] if k == 0 else X[:, t, :]
                            a = dve(lambda e, t=t, k=k, z=z, src=src: e.scalar_tensor_tensor(
                                out=X[:, t, :], in0=YG[z][:], scalar=GT[k][:, t:t + 1], in1=src, op0=ALU.mult, op1=ALU.add),
                                g, l_xl, a if k else [])
                            ygf[z] = [a]
                    xlf[gI % 2] = [a]
                    xs = [X[:, 4 * gI + i, :] for i in range(4)]
                    n1 = layernorm(xs, xs, a)
                    xr_ = []
                    for k in range(2):
                        kb, fr = take()
                        for i in range(4):
                            a = tr(PS[:, kb, 128 * i:128 * i + 128], xs[i][:, 128 * k:128 * k + 128], [fr, n1])
                        a = act(lambda e, k=k, kb=kb, gI=gI: e.activation(XT[:, k, 512 * gI:512 * gI + 512], PS[:, kb, :], ACT.Copy), a)
                        give(kb, a)
                        xr_.append(a)
                    xtr[gI] = xr_
            WW = [s3(f"WW{i}", [128, 2, 1024]) for i in range(2)]
            BB = s3("BB", [128, 2, 2, 4])
            CS = s3("CS", [128, 2, 1024])
            T1 = [s3(f"TA{i}", [128, 512]) for i in range(3)]
            T2 = [s3(f"TB{i}", [128, 512]) for i in range(3)]
            PP = [s3(f"PP{i}", [128, 3, 512], BF16) for i in range(4)]
            l_bb, l_cs = Q.dma("sp", BB[:], A["bqk"]), Q.dma("sp", CS[:], A["c_cs"])
            l_ww = [Q.dma("sp", WW[i][:], A["wqk"][i]) for i in range(2)]
            tf, pf = [[], [], []], [[], [], [], []]
            pw = {}
            i = 0
            combine(0)
            for b in range(4):
                if b < 3:
                    combine(b + 1)
                for qi in range(2):
                    for fb in range(4):
                        for hf in range(2):
                            tok = 1024 * b + 512 * hf
                            (ka, fa), (kb, fr) = take(), take()
                            for bank, fx, o in ((ka, fa, 0), (kb, fr, 512)):
                                c0 = o + 128 * fb
                                mm(PS[:, bank, :], WW[qi][:, 0, c0:c0 + 128], XT[:, 0, tok:tok + 512], True, False, [fx, l_ww[qi], xtr[2 * b + hf]])
                                a = mm(PS[:, bank, :], WW[qi][:, 1, c0:c0 + 128], XT[:, 1, tok:tok + 512], False, True)
                                if o == 0:
                                    am = a
                            t1, t2, pp = T1[i % 3], T2[i % 3], PP[i % 4]
                            a1 = dve(lambda e, ka=ka, t1=t1, qi=qi, fb=fb, hf=hf: e.scalar_tensor_tensor(
                                out=t1[:], in0=PS[:, ka, :], scalar=BB[:, qi, 0, fb:fb + 1], in1=CS[:, 0, 512 * hf:512 * hf + 512],
                                op0=ALU.add, op1=ALU.mult), am, l_bb, l_cs, tf[i % 3])
                            a2 = dve(lambda e, kb=kb, t2=t2, qi=qi, fb=fb, hf=hf: e.scalar_tensor_tensor(
                                out=t2[:], in0=PS[:, kb, :], scalar=BB[:, qi, 1, fb:fb + 1], in1=CS[:, 1, 512 * hf:512 * hf + 512],
                                op0=ALU.add, op1=ALU.mult), a)
                            give(ka, a1)
                            give(kb, a2)
                            r = pool(lambda e, t1=t1, t2=t2: e.tensor_tensor(t1[:], t1[:], t2[:], ALU.add), a1, a2)
                            h = act(lambda e, t1=t1, pp=pp: e.activation(pp[:, 0, :], t1[:], ACT.Copy), r, pf[i % 4])
                            d = dve(lambda e, t1=t1, pp=pp: e.tensor_tensor(t1[:], t1[:], pp[:, 0, :], ALU.subtract), h)
                            m = act(lambda e, t1=t1, pp=pp: e.activation(pp[:, 1, :], t1[:], ACT.Copy), d)
                            l = pool(lambda e, t1=t1, pp=pp: e.tensor_tensor(pp[:, 2, :], t1[:], pp[:, 1, :], ALU.subtract), m)
                            tf[i % 3] = [l]
                            w = Q.dma("sp", PARTS[qi, :, 128 * fb:128 * fb + 128, tok:tok + 512].rearrange("c p s -> p c s"), pp[:], l)
                            pf[i % 4] = [w]
                            pw.setdefault((b, fb), []).append(w)
                            i += 1
            Q.barrier()

        with ExitStack() as c4:
            s4 = lambda n, s, d=F32: sb(n, s, d, c4)
            QS = [s4(f"QS{i}", [128, 4, 1024], BF16) for i in range(4)]
            KS = [s4(f"KS{i}", [128, 4, 1024], BF16) for i in range(4)]
            VP = [s4(f"VP{i}", [128, 8, 288]) for i in range(2)]
            NE_ = 3
            NACC = 1
            E = s4("E", [128, NE_, 4, 512])
            IDB = s4("IDB", [128, 128], BF16)
            MR, MC = s4("MR", [128, 128], BF16), s4("MC", [128, 128], BF16)
            WV1, WO1 = s4("WV1", [128, 2, 256]), s4("WO1", [128, 2, 256])
            BV, BO, HN = s4("BV", [128, 256]), s4("BO", [128, 256]), s4("HN", [128, 256])
            L1, L2, NL = s4("L1", [128, 16]), s4("L2", [128, 16]), s4("NL", [128, 16])
            NM = [s4(f"NM{i}", [128, 4, 8]) for i in range(2)]
            MP = [s4(f"MP{i}", [32, 3, 128], BF16) for i in range(2)]
            MT = s4("MT", [32, 128])
            OT = s4("OT", [128, 1024])
            OA = [s4("OA", [128, 8, 256])] * 2
            OB = s4("OB", [128, 8, 256])
            RC = s4("RC", [128, 8, 4])
            O1, O2 = s4("O1", [128, 8, 2, 16]), s4("O2", [128, 8, 2, 16])
            MS, ML = s4("MS", [128, 128]), s4("ML", [128, 128])
            LQ = OB[:].rearrange("p i d -> p (i d)").rearrange("p (a d) -> p a d", d=256)

            l_m = Q.dma("sp", E[:, 0, 0, 0:256], A["c_mrc"])
            l_idb = act(lambda e: e.activation(IDB[:], IDN[:], ACT.Copy))
            l_mr = act(lambda e: e.activation(MR[:], E[:, 0, 0, 0:128], ACT.Copy), l_m)
            l_mc = act(lambda e: e.activation(MC[:], E[:, 0, 0, 128:256], ACT.Copy), l_m)
            l_v1, l_o1 = Q.dma("sp", WV1[:], A["wv1"]), Q.dma("sp", WO1[:], A["wo1"])
            l_bv, l_bo, l_hn = (Q.dma("sp", d[:], A[n]) for d, n in ((BV, "bv"), (BO, "bo"), (HN, "hn")))
            l_lq = Q.dma("sp", LQ[:, 0:4, :], A["lam"])
            z_k = [dve(lambda e, i=i: e.memset(KS[i][96:128], 1.0)) for i in range(4)]
            z_v = [pool(lambda e, i=i: e.memset(VP[i][:], 1.0)) for i in range(2)]
            li = 0.8 - 0.6 * 1.0
            a = dve(lambda e: e.tensor_tensor(LQ[:, 0, :], LQ[:, 0, :], LQ[:, 1, :], ALU.mult), l_lq)
            a2 = dve(lambda e: e.tensor_tensor(LQ[:, 2, :], LQ[:, 2, :], LQ[:, 3, :], ALU.mult), l_lq)
            a = dve(lambda e: e.tensor_reduce(L1[:], LQ[:, 0, :].rearrange("p (h d) -> p h d", d=16), AX, ALU.add), a)
            a2 = dve(lambda e: e.tensor_reduce(L2[:], LQ[:, 2, :].rearrange("p (h d) -> p h d", d=16), AX, ALU.add), a2)
            lq_free = a2
            a = act(lambda e: e.activation(L1[:], L1[:], ACT.Exp), a)
            a = act(lambda e: e.activation(L2[:], L2[:], ACT.Exp), a2)
            nl = dve(lambda e: e.scalar_tensor_tensor(out=NL[:], in0=L2[:], scalar=-li, in1=L1[:], op0=ALU.add, op1=ALU.subtract), a)
            hn = dve(lambda e: e.tensor_scalar(HN[:], HN[:], 1.0 - li, None, ALU.mult), l_hn)

            kvread = {}
            fl, ml, vr = {}, {}, {}
            turn = {"n": 0, "free": [[], []]}
            SB = [4, 5, 6] if NACC == 1 else [4, 5]
            single = {"n": 0, "free": [[] for _ in SB]}
            acc_free = [[], []]
            later = []

            def pair():
                k = turn["n"] % 2
                turn["n"] += 1
                return k, turn["free"][k]

            def pv(k):
                return PS[:, 2 * k:2 * k + 2, :]

            def fetch(v):
                b, g = v // 8, v % 8
                ops = []
                for qi, D in ((0, QS[v % 4]), (1, KS[v % 4])):
                    for r0, n, kp in ((0, 3, 0), (48, 2, 1), (80, 1, 2)):
                        for c in range(n):
                            src = PARTS[qi, c if qi == 0 else kp, 64 * g:64 * g + 64, 1024 * b:1024 * b + 1024]
                            ops.append(Q.dma("sp", D[r0 + 16 * c:r0 + 16 * c + 16, :, :],
                                             src.rearrange("(j r) s -> r j s", r=16), kvread.get(v - 4), z_k))
                fl[v] = ops

            nmfree, mpfree, otfree, rcfree = [[], []], [[], []], [[], []], []
            efree = [[] for _ in range(NE_)]
            cnt = {"e": 0, "pend": None}
            vread, oread = {}, [[], []]
            mtfree = []

            def values(b):
                for q in range(2):
                    k, fr = pair()
                    for i in range(4):
                        i_ = 4 * q + i
                        o = PS[:, 2 * k + i // 2, 256 * (i % 2):256 * (i % 2) + 256]
                        tk_ = slice(1024 * b + 128 * i_, 1024 * b + 128 * i_ + 128)
                        mm(o, XT[:, 0, tk_], WV1[:, 0, :], True, False, [fr, l_v1])
                        a = mm(o, XT[:, 1, tk_], WV1[:, 1, :], False, True)
                    a = dve(lambda e, q=q, k=k: e.tensor_tensor(
                        VP[b % 2][:, 4 * q:4 * q + 4, 0:272].rearrange("p i (h d) -> p i h d", d=17)[:, :, :, 0:16],
                        pv(k).rearrange("p k (i h d) -> p (k i) h d", i=2, d=16),
                        BV[:].rearrange("p (h d) -> p h d", d=16).unsqueeze(1).to_broadcast([128, 4, 16, 16]), ALU.add),
                        a, l_bv, vread.get(b - 2, z_v))
                    turn["free"][k] = [a]
                    vr.setdefault(b, []).append(a)

            def maxima(v):
                Qs, Ks, nm = QS[v % 4], KS[v % 4], NM[v % 2]
                jobs = [(i, (2 * p, 2 * p + 1)) for i in range(4) for p in range(2)]
                jobs += [(i, (j,)) for i in range(4, 8) for j in range(4)]

                def step(i, js):
                    k, fr = pair()
                    W = 128 * (i + 1)
                    for n_, j in enumerate(js):
                        lhs = Qs[0:96, j, 128 * i:128 * i + 128]
                        for p in range((W + 511) // 512):
                            n = min(512, W - 512 * p)
                            bank = 2 * k + (n_ if len(js) == 2 else p)
                            a = mm(PS[:, bank, 0:n], lhs, Ks[0:96, j, 512 * p:512 * p + n], True, True, [fr, fl[v]])
                            if 512 * p + n == W:
                                a = mm(PS[:, bank, n - 128:n], IDB[:], MR[:], False, True, [l_idb, l_mr], skip=True)
                    if len(js) == 2:
                        src, dst = pv(k)[:, :, 0:W], nm[:, js[0]:js[0] + 2, i]
                    else:
                        src, dst = pv(k).rearrange("p k s -> p (k s)")[:, 0:W], nm[:, js[0], i:i + 1]
                    a = dve(lambda e: e.tensor_reduce(dst, src, AX, ALU.max), a, nmfree[v % 2])
                    turn["free"][k] = [a]
                    cnt["nm"] = a
                return [lambda i=i, js=js: step(i, js) for i, js in jobs]

            def subtract_rows(v, a):
                k, fr = pair()
                p_ = PS[0:32, 2 * k, 0:128]
                mp = MP[v % 2]
                tm = tr(p_, NM[v % 2][:].rearrange("p j i -> p (j i)"), [fr, a])
                nmfree[v % 2] = [tm]
                h = act(lambda e: e.activation(mp[:, 0, :], p_, ACT.Copy, scale=-1.0), tm, mpfree[v % 2])
                d = dve(lambda e: e.scalar_tensor_tensor(out=MT[:], in0=p_, scalar=-1.0, in1=mp[:, 0, :],
                                                         op0=ALU.mult, op1=ALU.subtract), h, mtfree)
                m = act(lambda e: e.activation(mp[:, 1, :], MT[:], ACT.Copy), d)
                l = dve(lambda e: e.tensor_tensor(mp[:, 2, :], MT[:], mp[:, 1, :], ALU.subtract), m)
                mtfree[:] = [l]
                turn["free"][k] = [d]
                ml[v] = [Q.dma("sp", QS[v % 4][96 + p:97 + p, :, :], mp[:, p, :], l, kvread.get(v - 4)) for p in range(3)]
                mpfree[v % 2] = ml[v]

            def exponentials(v):
                Qs, Ks = QS[v % 4], KS[v % 4]
                b, g = v // 8, v % 8
                steps = []
                for p in range(2):
                    for kt in range(4 * p + 4):
                        q0 = max(128 * kt, 512 * p)
                        n = 512 * p + 512 - q0
                        st = {}
                        for pr in range(2):
                            def step(p=p, kt=kt, q0=q0, n=n, pr=pr, st=st):
                                if pr == 0:
                                    st["e"] = cnt["e"] % NE_
                                    cnt["e"] += 1
                                    st["r"] = []
                                ei = st["e"]
                                for x in range(2):
                                    j = 2 * pr + x
                                    z = single["n"] % len(SB)
                                    single["n"] += 1
                                    fr, bank = single["free"][z], SB[z]
                                    lhs = Ks[0:99, j, 128 * kt:128 * kt + 128]
                                    a = mm(PS[:, bank, 0:n], lhs, Qs[0:99, j, q0:q0 + n], True, True, [fr, fl[v], ml[v], z_k])
                                    if q0 == 128 * kt:
                                        a = mm(PS[:, bank, 0:128], IDB[:], MC[:], False, True, [l_mc], skip=True)
                                    a = act(lambda e, j=j, bank=bank: e.activation(E[:, ei, j, 0:n], PS[:, bank, 0:n], ACT.Exp, scale=0.25),
                                            a, efree[ei], l_mr, l_mc)
                                    single["free"][z] = [a]
                                    st["r"].append(a)
                                if pr == 1:
                                    if cnt["pend"]:
                                        cnt["pend"]()
                                    cnt["pend"] = lambda: st["av"](ei, st["r"])
                            steps.append(step)

                        def av(ei, reads, p=p, kt=kt, q0=q0, n=n):
                            for jj in range(4):
                                hd = 2 * g + jj // 2
                                a = mm(PS[32 * jj:32 * jj + 32, 7 - p * (NACC - 1), 512 - n:512], VP[b % 2][:, kt, 17 * hd:17 * hd + 32],
                                       E[:, ei, jj, 0:n], kt == 0, True, [acc_free[p if NACC == 2 else 0], reads, vr[b]], skip=True)
                            efree[ei] = [a]
                            if kt == 4 * p + 3:
                                o = (lambda e: e.activation(OT[:, 512 * p:512 * p + 512], PS[:, 7 - p * (NACC - 1), :], ACT.Copy)) if p == 0 else \
                                    (lambda e: e.tensor_copy(OT[:, 512 * p:512 * p + 512], PS[:, 7 - p * (NACC - 1), :]))
                                c_ = (act if p == 0 else dve)(o, a, otfree[p])
                                acc_free[p if NACC == 2 else 0] = [c_]
                                cnt.setdefault("ot", {})[p] = c_
                                if p == 1:
                                    kvread[v] = [a]
                                    if g == 7:
                                        vread[b] = [a]
                                    later.append([3, lambda: heads(v)])
                        st["av"] = av
                return steps

            oar = {}

            def heads(v):
                b, g = v // 8, v % 8
                k, fr = pair()
                for i in range(8):
                    a = tr(PS[:, 2 * k + i // 4, 128 * (i % 4):128 * (i % 4) + 128], OT[:, 128 * i:128 * i + 128],
                           [fr, cnt["ot"][0], cnt["ot"][1]])
                otfree[0] = otfree[1] = [a]
                ov = pv(k).rearrange("p k s -> p (k s)").rearrange("p (i h m d) -> p i h m d", i=8, h=2, m=2)
                h0 = 2 * g
                rc4 = RC[:].rearrange("p i (h m) -> p i h m", m=2)
                a = dve(lambda e: e.reciprocal(rc4, ov[:, :, :, :, 16]), a, rcfree)
                a = dve(lambda e: e.tensor_tensor(rc4[:, :, :, 1], rc4[:, :, :, 1],
                        NL[:, h0:h0 + 2].unsqueeze(1).to_broadcast([128, 8, 2]), ALU.mult), a, nl)
                b4 = [128, 8, 2, 16]
                x1 = dve(lambda e: e.tensor_tensor(O1[:], ov[:, :, :, 0, 0:16], rc4[:, :, :, 0].unsqueeze(3).to_broadcast(b4), ALU.mult), a, rcfree)
                x2 = dve(lambda e: e.tensor_tensor(O2[:], ov[:, :, :, 1, 0:16], rc4[:, :, :, 1].unsqueeze(3).to_broadcast(b4), ALU.mult), a, rcfree)
                turn["free"][k] = [x2]
                a = pool(lambda e: e.tensor_tensor(
                    OA[b % 2][:, :, 16 * h0:16 * h0 + 32].rearrange("p i (h d) -> p i h d", d=16), O1[:], O2[:], ALU.add),
                    x1, x2, oread[b % 2])
                rcfree[:] = [a]
                oar.setdefault(b, []).append(a)
                if g == 7:
                    norm(b)

            obfree = [lq_free]

            def norm(b):
                oa = OA[b % 2]
                oh = oa[:].rearrange("p i (h d) -> p (i h) d", d=16)
                a = pool(lambda e: e.tensor_tensor(OB[:], oa[:], oa[:], ALU.mult), oar[b], obfree)
                a = dve(lambda e: e.tensor_reduce(MS[:], OB[:].rearrange("p i (h d) -> p (i h) d", d=16), AX, ALU.add), a)
                ob_read = a
                bo = pool(lambda e: e.tensor_tensor(X[:, 8 * b:8 * b + 8, :], X[:, 8 * b:8 * b + 8, :],
                          BO[:].unsqueeze(1).to_broadcast([128, 8, 256]), ALU.add), l_bo)
                a = rsqrt(MS[:], MS[:], ML[:], 1.0 / 16, 1, a)
                a = pool(lambda e: e.tensor_tensor(oh, oh, MS[:].unsqueeze(2).to_broadcast([128, 128, 16]), ALU.mult), a)
                a = pool(lambda e: e.tensor_tensor(oa[:], oa[:], HN[:].unsqueeze(1).to_broadcast([128, 8, 256]), ALU.mult), a, hn)
                later.append([9, lambda: project(b, a, bo, ob_read)])

            def project(b, a, bo, ob_read):
                oa = OA[b % 2]
                OTT = OB[:].rearrange("p i d -> p (i d)").rearrange("p (k s) -> p k s", k=2)
                tt_ = []
                for kk in range(2):
                    k, fr = pair()
                    for i in range(8):
                        a2 = tr(PS[:, 2 * k + i // 4, 128 * (i % 4):128 * (i % 4) + 128], oa[:, i, 128 * kk:128 * kk + 128], [fr, a])
                    a3 = act(lambda e, kk=kk, k=k: e.activation(OTT[:, kk, :], pv(k).rearrange("p k s -> p (k s)"), ACT.Copy), a2, ob_read)
                    turn["free"][k] = [a3]
                    tt_.append(a3)
                oread[0] = oread[1] = [a2]

                def out_product():
                    for q in range(2):
                        k, fr = pair()
                        for i in range(4):
                            i_ = 4 * q + i
                            o = PS[:, 2 * k + i // 2, 256 * (i % 2):256 * (i % 2) + 256]
                            mm(o, OTT[:, 0, 128 * i_:128 * i_ + 128], WO1[:, 0, :], True, False, [fr, tt_, l_o1])
                            a3 = mm(o, OTT[:, 1, 128 * i_:128 * i_ + 128], WO1[:, 1, :], False, True)
                        t0 = 8 * b + 4 * q
                        a4 = dve(lambda e, k=k, t0=t0: e.tensor_tensor(
                            X[:, t0:t0 + 4, :], X[:, t0:t0 + 4, :], pv(k).rearrange("p k (i d) -> p (k i) d", i=2), ALU.add), a3, bo)
                        turn["free"][k] = [a4]
                        xs = [X[:, t0 + i, :] for i in range(4)]
                        n1 = layernorm(xs, xs, a4)
                        later.append([3 + q, lambda t0=t0, n1=n1, xs=xs: turned(t0, n1, xs)])
                    obfree[:] = [a3]
                later.append([2, out_product])

            def turned(t0, n1, xs):
                k, fr = pair()
                for kk in range(2):
                    for i in range(4):
                        a = tr(PS[:, 2 * k + kk, 128 * i:128 * i + 128], xs[i][:, 128 * kk:128 * kk + 128], [fr, n1])
                a = act(lambda e: e.activation(XT[:, :, 128 * t0:128 * t0 + 512], pv(k), ACT.Copy), a, vr[t0 // 8])
                turn["free"][k] = [a]

            def due():
                now = [x for x in later if x[0] <= 0]
                later[:] = [x for x in later if x[0] > 0]
                for x in later:
                    x[0] -= 1
                for x in now:
                    x[1]()

            for v in range(3):
                fetch(v)
            values(0)
            for v in range(-2, 32):
                xs_ = exponentials(v) if v >= 0 else []
                ms_ = maxima(v + 2) if v + 2 < 32 else []
                for s_ in range(24):
                    if xs_:
                        xs_[s_]()
                    if ms_:
                        ms_[s_]()
                    due()
                    if s_ == 2 and v >= 0 and v + 3 < 32:
                        fetch(v + 3)
                if v + 2 < 32:
                    later.append([2 if v >= 0 else 0, lambda v=v, a=cnt["nm"]: subtract_rows(v + 2, a)])
                if v % 8 == 3 and v // 8 + 1 < 4:
                    values(v // 8 + 1)
                if v < 0:
                    due()
            cnt["pend"]()
            while later:
                due()
            Q.barrier()

        if stages < 4:
            return finish()
        with ExitStack() as c5:
            s5 = lambda n, s, d=F32: sb(n, s, d, c5)
            RW2 = s5("RW2", [128, 2, 8])
            COMB = s5("COMB", [128, 32, 8])
            WI = s5("WI", [128, 8, 2, 256])
            WO2 = s5("WO2", [128, 8, 2, 256])
            HH = [s5(f"HH{i}", [128, 2, 512]) for i in range(3)]
            YO = [s5(f"YO{i}", [128, 4, 256]) for i in range(2)]
            l_rw = Q.dma("sp", RW2[:], A["wr2"])
            l_wi, l_wo = [], []
            for e_ in range(8):
                l_wi.append(Q.dma("sp", WI[:, e_], A["wi"][e_]))
                l_wo.append(Q.dma("sp", WO2[:, e_], A["wo2"][e_]))
            kb, fr = take()
            pl = PS[:, kb, 0:256].rearrange("p (t e) -> p t e", e=8)
            for t in range(32):
                mm(pl[:, t, :], XT[:, 0, 128 * t:128 * t + 128], RW2[:, 0, :], True, False, [fr, l_rw])
                a = mm(pl[:, t, :], XT[:, 1, 128 * t:128 * t + 128], RW2[:, 1, :], False, True)
            OH1b, OH2b, M1b, M2b, _r1, _t8, lg_read, a = choose(pl, "b", c5, a)
            give(kb, lg_read)
            up = lambda m: m.unsqueeze(2).to_broadcast([128, 32, 8])
            a = tt(OH1b[:], OH1b[:], up(M1b[:]), ALU.mult, a)
            a = tt(OH2b[:], OH2b[:], up(M2b[:]), ALU.mult, a)
            rr = tt(COMB[:], OH1b[:], OH2b[:], ALU.add, a)
            hfree = [[], [], []]
            pend = None
            accs = {}

            def second(n, e_, hi, hr):
                for p in range(2):
                    kb, fr = take()
                    for j in range(2):
                        m = 2 * p + j
                        for k in range(2):
                            a = mm(PS[:, kb, 256 * j:256 * j + 256], HH[hi][:, k, 128 * m:128 * m + 128], WO2[:, e_, k, :],
                                   k == 0, k == 1, [fr, hr, l_wo[e_]])
                    for j in range(2):
                        t = 4 * n + 2 * p + j
                        a2 = dve(lambda e, kb=kb, t=t, j=j: e.scalar_tensor_tensor(
                            out=X[:, t, :], in0=PS[:, kb, 256 * j:256 * j + 256], scalar=COMB[:, t, e_:e_ + 1],
                            in1=X[:, t, :], op0=ALU.mult, op1=ALU.add), a, rr, accs.get(t, []))
                        accs[t] = [a2]
                    give(kb, a2)
                hfree[hi] = [a]
                if e_ == 7:
                    xs = [X[:, 4 * n + i, :] for i in range(4)]
                    y = YO[n % 2]
                    n1 = layernorm(xs, [y[:, i, :] for i in range(4)], accs[4 * n + 3], stores[n - 2:n - 1] if n > 1 else [])
                    stores.append(Q.dma("sp", out[:, 4 * n:4 * n + 4, :], y[:], n1))

            stores = []
            i = 0
            for n in range(8):
                for e_ in range(8):
                    hr = []
                    for k in range(2):
                        kb, fr = take()
                        c0 = slice(128 * k, 128 * k + 128)
                        mm(PS[:, kb, :], WI[:, e_, 0, c0], XT[:, 0, 512 * n:512 * n + 512], True, False, [fr, l_wi[e_]])
                        a = mm(PS[:, kb, :], WI[:, e_, 1, c0], XT[:, 1, 512 * n:512 * n + 512], False, True)
                        a = act(lambda e, kb=kb, k=k, hi=i % 3: e.activation(HH[hi][:, k, :], PS[:, kb, :], ACT.Copy), a, hfree[i % 3])
                        give(kb, a)
                        hr.append(a)
                    if pend:
                        second(*pend)
                    pend = (n, e_, i % 3, hr)
                    i += 1
            second(*pend)
            Q.q["sp"].append(Op("sp", None, Q.last()))
        Q.emit(nc, ctx)





def layout(inputs):
    f = lambda n: np.ascontiguousarray(np.asarray(inputs[n]))
    kc = lambda w: np.ascontiguousarray(w.reshape(-1, 128, w.shape[-1]).transpose(1, 0, 2))
    bc = lambda v, n=128: np.ascontiguousarray(np.broadcast_to(v.reshape(1, -1), (n, v.size)))
    a = {}
    x = f("L0_attn_x")
    a["x"] = np.ascontiguousarray(x.reshape(32, 128, 256).transpose(1, 0, 2))
    a["xt"] = np.ascontiguousarray(x.reshape(4, 8, 128, 2, 128).transpose(1, 4, 3, 0, 2).reshape(8, 128, 8, 128))
    a["wq0"], a["wk0"], a["wv0"], a["wg0"] = (kc(f("L0_attn_W" + n)) for n in "qkvg")
    a["wgk1"] = kc(f("L0_attn_Wgk1"))
    a["wgk2"] = np.concatenate([f("L0_attn_Wgk2"), f("L0_attn_bgk2").reshape(1, 256), np.zeros((111, 256), np.float32)])
    a["wo0"] = kc(f("L0_attn_Wo"))
    a["rms"] = bc(np.tile(f("L0_attn_rms_w"), 4))
    a["gam"], a["bet"] = bc(f("L0_ffn_ln_gamma")), bc(f("L0_ffn_ln_beta"))
    i = np.arange(128)
    same = (i[:, None] // 64) == (i[None, :] // 64)
    up = same & (i[:, None] <= i[None, :])
    a["c_tri"] = up.astype(np.float32) / 16
    a["c_msk"] = up.astype(np.int32)
    a["c_idn"] = np.eye(128, dtype=np.float32)
    a["c_eps"] = np.tile(np.array([1e-5, 1e-6, 1.0, 0.0], np.float32), (128, 1))
    a["c_irev"] = np.tile(np.arange(8, 0, -1).astype(np.float32), (128, 1))
    tk = lambda w: kc(np.ascontiguousarray(w.T))
    a["rw"] = tk(f("L0_ffn_router_w"))
    a["we"] = np.stack([np.concatenate([tk(g).reshape(128, -1), tk(d).reshape(128, -1)], 1)
                        for g, d in zip(f("L0_ffn_gate_up_w"), f("L0_ffn_down_w"))])
    a["c_slt"] = (i[:, None] < i[None, :]).astype(np.float32)
    a["c_cnt"] = np.tile(np.concatenate([128.0 * np.arange(32), np.arange(72)]).astype(np.float32), (128, 1))
    a["sgu"], a["sdn"] = tk(f("L0_ffn_shared_gate_up_w")), tk(f("L0_ffn_shared_down_w"))
    other = (np.arange(512) // 16) * 16 + (np.arange(512) + 8) % 16
    w, bb = [], []
    for n in "qk":
        W, v = f("L1_attn_W" + n), f("L1_attn_b" + n)
        w.append(tk(np.concatenate([W, W[other]])))
        bb.append(np.stack([v.reshape(4, 128).T, v[other].reshape(4, 128).T], 1))
    a["wqk"] = np.stack(w)
    a["bqk"] = np.ascontiguousarray(np.stack(bb, 1))
    inv = (1.0 / np.float32(10000.0) ** (np.arange(8, dtype=np.float32) / np.float32(8))).astype(np.float32)
    ang = (np.arange(1024, dtype=np.float32)[None, :] * inv[:, None]).astype(np.float32)
    row = np.arange(128) % 16
    sign = np.where(row < 8, -1.0, 1.0).astype(np.float32)[:, None]
    a["c_cs"] = np.ascontiguousarray(np.stack([np.cos(ang)[row % 8], np.sin(ang)[row % 8] * sign], 1).astype(np.float32))
    later = np.where(i[None, :] > i[:, None], -1e30, 0.0).astype(np.float32)
    a["c_mrc"] = np.concatenate([later, later.T], 1)
    a["wv1"], a["wo1"] = tk(f("L1_attn_Wv")), tk(f("L1_attn_Wo"))
    a["bv"], a["bo"], a["hn"] = bc(f("L1_attn_bv")), bc(f("L1_attn_bo")), bc(f("L1_attn_head_norm_w"))
    a["lam"] = np.ascontiguousarray(np.stack([bc(f("L1_attn_" + n)) for n in ("lq1", "lk1", "lq2", "lk2")], 1))
    a["wr2"] = kc(f("L1_ffn_Wr"))
    a["wi"] = np.stack([kc(w) for w in f("L1_ffn_Wi")])
    a["wo2"] = np.stack([kc(w) for w in f("L1_ffn_Wo")])
    return a


def kernel(**inputs):
    import concourse.bacc as bacc
    from concourse.bass_utils import run_bass_kernel_spmd

    a = layout(inputs)
    nc = bacc.Bacc("TRN2", target_bir_lowering=False, num_devices=1)
    aps = {k: nc.dram_tensor("in_" + k, v.shape, mybir.dt.from_np(v.dtype), kind="ExternalInput").ap() for k, v in a.items()}
    out = nc.dram_tensor("out_0_dram", (128, 32, 256), F32, kind="ExternalOutput").ap()
    program(nc, aps, out)
    r = run_bass_kernel_spmd(nc, [{"in_" + k: v for k, v in a.items()}], core_ids=[0])
    got = r.results[0]["out_0_dram"]
    return np.ascontiguousarray(got.transpose(1, 0, 2).reshape(4, 1024, 256))
```

```python
from contextlib import ExitStack

import numpy as np
import concourse.bass as bass
from concourse import mybir

F32 = mybir.dt.float32
BF16 = mybir.dt.bfloat16
F32R = mybir.dt.float32r
I32 = mybir.dt.int32
U32 = mybir.dt.uint32
NT = 71
ALU = mybir.AluOpType
ACT = mybir.ActivationFunctionType
AX = mybir.AxisListType.X


class Op:

    def __init__(self, eng, fn, waits, step=1):
        self.eng, self.fn, self.waits, self.step = eng, fn, waits, step
        self.sem, self.value, self.marked = None, 0, False


def flat(x):
    out = []
    for y in x:
        if isinstance(y, (list, tuple)):
            out += flat(y)
        elif y is not None:
            out.append(y)
    return out


class Queues:

    ENGINES = ("pe", "dve", "act", "pool", "sp")

    def __init__(self, nc, ctx, ndma):
        self.q = {e: [] for e in self.ENGINES}
        self.sem = {e: ctx.enter_context(nc.semaphore(f"done_{e}")) for e in self.ENGINES}
        self.dsem = [ctx.enter_context(nc.semaphore(f"dma{i}")) for i in range(ndma)]
        self.dlast = [None] * ndma
        self.n = 0
        self.isem = [ctx.enter_context(nc.semaphore(f"idma{i}")) for i in range(64)]
        self.ilast = [None] * 64
        self.ni = 0

    def add(self, eng, fn, *waits):
        op = Op(eng, fn, flat(waits))
        op.sem = self.sem[eng]
        for w in op.waits:
            w.marked = True
        self.q[eng].append(op)
        return op

    def dma(self, eng, out, in_, *waits):
        k = self.n % len(self.dsem)
        self.n += 1
        waits = flat(waits) + ([self.dlast[k]] if self.dlast[k] else [])
        op = Op(eng, lambda e: e.dma_start(out, in_), waits, 16)
        op.sem, op.marked = self.dsem[k], True
        op.value = 16 + (self.dlast[k].value if self.dlast[k] else 0)
        for w in waits:
            w.marked = True
        self.dlast[k] = op
        self.q[eng].append(op)
        return op

    def idma(self, out, out_off, in_, in_off, *waits):
        k = self.ni % len(self.isem)
        self.ni += 1
        waits = flat(waits) + ([self.ilast[k]] if self.ilast[k] else [])
        op = Op("pool", lambda e: e.indirect_dma_start(out, out_off, in_, in_off), waits, 16)
        op.sem, op.marked = self.isem[k], True
        op.value = 16 + (self.ilast[k].value if self.ilast[k] else 0)
        for w in waits:
            w.marked = True
        self.ilast[k] = op
        self.q["pool"].append(op)
        return op

    def last(self):
        out = [d for d in self.dlast + self.ilast if d]
        for e in self.ENGINES:
            own = [o for o in self.q[e] if o.step == 1]
            if own:
                out.append(own[-1])
        return out

    def barrier(self):
        end = self.last()
        for e in self.ENGINES:
            self.q[e].append(Op(e, None, [o for o in end]))
        for o in end:
            o.marked = True

    def emit(self, nc, ctx):
        for e in self.ENGINES:
            n = 0
            for o in self.q[e]:
                if o.step == 1 and o.fn and o.marked:
                    n += 1
                    o.value = n
        block = ctx.enter_context(nc.Block())
        heads = dict(pe=block.tensor, dve=block.vector, act=block.scalar, pool=block.gpsimd, sp=block.sync)
        for name in self.ENGINES:
            ops = self.q[name]

            def body(e, ops=ops):
                seen = {}
                for o in ops:
                    for w in o.waits:
                        k = id(w.sem)
                        if seen.get(k, 0) < w.value:
                            e.wait_ge(w.sem, w.value)
                            seen[k] = w.value
                    if o.fn:
                        ins = o.fn(e)
                        if o.marked and o.step:
                            ins.then_inc(o.sem, o.step)

            heads[name](body)


def program(nc, A, out):
    with ExitStack() as ctx:
        def sb(name, shape, dt=F32, c=ctx):
            return c.enter_context(nc.sbuf_tensor(name, shape, dt))

        Q = Queues(nc, ctx, 40)
        PS = ctx.enter_context(nc.psum_tensor("PS", [128, 8, 512], F32))

        def pe(fn, *w): return Q.add("pe", fn, *w)
        def dve(fn, *w): return Q.add("dve", fn, *w)
        def act(fn, *w): return Q.add("act", fn, *w)
        def pool(fn, *w): return Q.add("pool", fn, *w)

        def mm(o, l, r, start=True, stop=True, w=(), skip=False):
            return pe(lambda e: e.matmul(o, l, r, start=start, stop=stop, skip_group_check=skip), *w)

        def tr(o, i, w=()):
            n = i.shape[0]
            return pe(lambda e: e.transpose(o, i, IDN[0:n, 0:n]), *w)

        def split(hi, lo, src, e1, e2, *w):
            a = e1(lambda e: e.activation(hi, src, ACT.Copy) if e1 is act else e.tensor_copy(hi, src), *w)
            return [a, e2(lambda e: e.tensor_tensor(lo, src, hi.bitcast(F32), ALU.subtract), a, *w)]

        def mm3(o, lh, ll, rh, rl, start, stop, w=()):
            mm(o, lh, rh, start, False, w)
            mm(o, lh, rl, False, False)
            return mm(o, ll, rh, False, stop)

        banks = [(k, []) for k in range(8)]

        def take():
            return banks.pop(0)

        def give(k, *ops):
            banks.append((k, flat(ops)))

        IDN = sb("IDN", [128, 128])
        EPS = sb("EPS", [128, 4])
        ST = sb("ST", [128, 4, 6])
        MV = sb("MV", [128, 4, 2])
        LV = sb("LV", [128, 4])
        RS = sb("RS", [128, 4])
        IREV = sb("IREV", [128, 8])
        GT = [sb(f"GT{i}", [128, 32]) for i in range(2)]
        PI = [sb(f"PI{i}", [128, 32], U32) for i in range(2)]
        XS_D = nc.dram_tensor("xs_sorted", (128 * NT, 256), F32, kind="Internal").ap()
        YS_D = nc.dram_tensor("ys_sorted", (128 * NT, 256), F32, kind="Internal").ap()
        XR_D = nc.dram_tensor("x_resid", (128, 32, 256), F32, kind="Internal").ap()
        l_eps = Q.dma("sp", EPS[:], A["c_eps"])
        l_idn = Q.dma("sp", IDN[:], A["c_idn"])
        l_irev = Q.dma("sp", IREV[:], A["c_irev"])

        def rsqrt(dst, src, tmp, scale, epscol, *w):
            a = act(lambda e: e.activation(tmp, src, ACT.Ln, bias=EPS[:, epscol:epscol + 1], scale=scale), l_eps, *w)
            return act(lambda e: e.activation(dst, tmp, ACT.Exp, scale=-0.5), a)

        def explog():
            act(lambda e: e.preload_act_table_set("natural_log_exp_and_others")).step = 0

        ln_state = {"free": []}

        def ln_stats(tiles, *w):
            ops = []
            for i, t in enumerate(tiles):
                a = dve(lambda e, i=i, t=t: e.bn_stats(ST[:, i, :], t), *w, ln_state["free"])
                ops.append(a)
            for i in range(len(tiles)):
                a = dve(lambda e, i=i: e.bn_aggr(MV[:, i, :], ST[:, i, :]), ops[i])
            return a

        def ln_rstd(n, a):
            return rsqrt(RS[:, 0:n], MV[:, 0:n, 1], LV[:, 0:n], 1.0, 0, a)

        def ln_apply(tiles, outs, r, *w):
            res = []
            for i, (t, o) in enumerate(zip(tiles, outs)):
                res.append(dve(lambda e, i=i, t=t, o=o: e.tensor_scalar(
                    o, t, MV[:, i, 0:1], RS[:, i:i + 1], ALU.subtract, ALU.mult), r, *w))
            ln_state["free"] = [res[-1]]
            return res

        def layernorm(tiles, outs, *w):
            return ln_apply(tiles, outs, ln_rstd(len(tiles), ln_stats(tiles, *w)), *w)

        cA = ExitStack()
        NALL = sb("NALL", [128, 32, 256], F32, cA)
        LGA = sb("LGA", [128, 32, 8], F32, cA)
        nav = NALL[:].rearrange("p (b t) d -> p b t d", b=4)
        lgv = LGA[:].rearrange("p (b t) e -> p b t e", b=4)
        x_in = A["x"].rearrange("p (b t) d -> p b t d", b=4)
        x_out = XR_D.rearrange("p (b t) d -> p b t d", b=4)
        with ExitStack() as c1:
            s1 = lambda n, s, d=F32: sb(n, s, d, c1)
            WH = {n: (s1(f"W{n}H", [128, 2, c], F32R), s1(f"W{n}L", [128, 2, c], F32R)) for n, c in (("q", 256), ("k", 256), ("v", 512), ("g", 512))}
            XTH, XTL = s1("XTH", [128, 2, 4, 128], F32R), s1("XTL", [128, 2, 4, 128], F32R)
            W1 = s1("W1", [128, 2, 16])
            W2 = s1("W2", [128, 256])
            WO = s1("WO", [128, 4, 256])
            RMS = s1("RMS", [128, 512])
            GAM, BET = s1("GAM", [128, 256]), s1("BET", [128, 256])
            RW = s1("RW", [128, 2, 8])
            TRI = s1("TRI", [128, 128])
            MSK = s1("MSK", [128, 128], I32)
            XTS = [s1(f"XTS{i}", [128, 2, 4, 128]) for i in range(2)]
            XS = [s1(f"XS{i}", [128, 4, 256]) for i in range(2)]
            NTT = s1("NTT", [128, 2, 4, 128])
            XG = s1("XG", [128, 512])
            GA, GE, GG = s1("GA", [128, 1024]), s1("GE", [128, 1024]), s1("GG", [128, 1024])
            EP, EM = s1("EP", [128, 2, 512]), s1("EM", [128, 2, 512])
            QG = s1("QG", [128, 2, 2, 512])
            KD, KG = s1("KD", [128, 2, 512]), s1("KG", [128, 2, 512])
            KZ = s1("KZ", [128, 2, 4, 256])
            V = s1("V", [128, 4, 512])
            AT = s1("AT", [128, 16, 128])
            SG = s1("SG", [128, 4, 512])
            Y = s1("Y", [128, 4, 512])
            YT = s1("YT", [128, 16, 128])
            S = s1("S", [128, 2, 2, 4, 128])
            SQ = s1("SQ", [128, 128])
            SS, SL, SR = s1("SS", [128, 16]), s1("SL", [128, 16]), s1("SR", [128, 16])

            lx, lxs = {}, {}

            def load_xt(t, *w):
                lx[t] = Q.dma("sp", XTS[t % 2][:].rearrange("p k b s -> p (k b) s"), A["xt"][t], *w)

            def load_xs(t, *w):
                lxs[t] = Q.dma("sp", XS[t % 2][:], x_in[:, :, t, :], *w)

            l_w1 = Q.dma("sp", W1[:], A["wgk1"])
            load_xt(0)
            l_w2 = Q.dma("sp", W2[:], A["wgk2"])
            raw = {n: (Y if n in "qv" else YT)[:].rearrange("p a b -> p (a b)")[:, c:c + 2 * w].rearrange("p (k w) -> p k w", k=2)
                   for n, c, w in (("q", 0, 256), ("k", 0, 256), ("v", 1024, 512), ("g", 1024, 512))}
            l_raw = {n: Q.dma("sp", raw[n], A[f"w{n}0"]) for n in "qkvg"}
            l_tri = Q.dma("sp", TRI[:], A["c_tri"])
            l_msk = Q.dma("sp", MSK[:], A["c_msk"])
            l_rms = Q.dma("sp", RMS[:], A["rms"])
            l_o = Q.dma("sp", WO[:], A["wo0"])
            load_xt(1)
            load_xs(0)
            load_xs(1)
            l_gam = Q.dma("sp", GAM[:], A["gam"])
            l_bet = Q.dma("sp", BET[:], A["bet"])
            l_rw = Q.dma("sp", RW[:], A["rw"])

            z_xg = pool(lambda e: e.memset(XG[:], 1.0))
            z_qg = pool(lambda e: e.memset(QG[:], 0.0))
            z_kz = pool(lambda e: e.memset(KZ[:], 0.0))
            z_at = pool(lambda e: e.memset(AT[:], 0.0))
            z_s = pool(lambda e: e.memset(S[:], 0.0))
            z_na = pool(lambda e: e.memset(NALL[:], 0.0))
            zx = [Q.dma("sp", XS_D[1024 * c:min(1024 * c + 1024, 128 * NT), :].rearrange("(a p) d -> p a d", p=128),
                        NALL[:, 0:min(8, NT - 8 * c), :], z_na) for c in range((NT + 7) // 8)]

            f = {k: [] for k in "xg ga ge gg ep em qg kd kg kz v at sg y yt sr ntt hs su".split()}
            s_ready = [z_s] * 8
            s_read = [[] for _ in range(8)]
            xts_read = {}
            G = {}

            l_q, l_k, l_v, l_g = ([] for _ in range(4))
            xsp = {}

            def split_x(t):
                xsp[t] = split(XTH[:], XTL[:], XTS[t % 2][:], act, dve, lx[t], xts_read.get(t - 1, []))

            def a1(t):
                if t == 0:
                    split_x(0)
                    for n, l in zip("qkvg", (l_q, l_k, l_v, l_g)):
                        l += split(WH[n][0][:], WH[n][1][:], raw[n], act, dve, l_raw[n])
                    f["y"], f["yt"] = [l_q, l_v], [l_k, l_g]
                XTt = XTS[t % 2]
                xt = [XTt[:, k] for k in range(2)]
                bt = lambda k: PS[:, k, :].rearrange("p (b s) -> p b s", b=4)
                g_ = G[t] = {}
                kb, fr = take()
                mm(PS[0:16, kb, :].rearrange("p (b s) -> p b s", b=4), W1[:, 0, :], xt[0], True, False, [fr, lx[t], l_w1])
                a = mm(PS[0:16, kb, :].rearrange("p (b s) -> p b s", b=4), W1[:, 1, :], xt[1], False, True)
                f["x1"] = [a]
                xg = act(lambda e, kb=kb: e.activation(XG[0:16, :], PS[0:16, kb, :], ACT.Copy), a, z_xg, f["xg"])
                give(kb, xg)
                qk = []
                for n, l in (("q", l_q), ("k", l_k)):
                    for h in range(2):
                        kb, fr = take()
                        for k in range(2):
                            c_ = slice(128 * h, 128 * h + 128)
                            a = mm3(bt(kb), WH[n][0][:, k, c_], WH[n][1][:, k, c_], XTH[:, k], XTL[:, k], k == 0, k == 1,
                                    [fr, l, xsp[t]])
                        qk.append((kb, a))
                g2 = []
                explog()
                for p in range(2):
                    kb, fr = take()
                    for j in range(2):
                        b = 2 * p + j
                        a = mm(PS[:, kb, 256 * j:256 * j + 256], XG[:, 128 * b:128 * b + 128], W2[:],
                               True, True, [fr, xg, l_w2])
                    f["xg"] = [a]
                    c0 = 512 * p
                    z1 = act(lambda e, kb=kb, c0=c0: e.activation(GA[:, c0:c0 + 512], PS[:, kb, :], ACT.Abs), a, f["ga"])
                    z2 = act(lambda e, c0=c0: e.activation(GE[:, c0:c0 + 512], GA[:, c0:c0 + 512], ACT.Exp, scale=-1.0), z1, f["ge"])
                    z3 = act(lambda e, c0=c0: e.activation(GA[:, c0:c0 + 512], GE[:, c0:c0 + 512], ACT.Ln, bias=EPS[:, 2:3]), z2, l_eps)
                    z4 = dve(lambda e, kb=kb, c0=c0: e.scalar_tensor_tensor(
                        out=GG[:, c0:c0 + 512], in0=PS[:, kb, :], scalar=0.0, in1=GA[:, c0:c0 + 512],
                        op0=ALU.min, op1=ALU.subtract), z3, f["gg"])
                    give(kb, z4)
                    g2.append(z4)
                f["ga"], f["ge"] = g2, [z3]
                g_.update(qk=qk, g2=g2)

            def a1v(t):
                vr = []
                for b in range(4):
                    kb, fr = take()
                    for k in range(2):
                        a = mm3(PS[:, kb, :], XTH[:, k, b, :], XTL[:, k, b, :], WH["v"][0][:, k, :], WH["v"][1][:, k, :],
                                k == 0, k == 1, [fr, l_v])
                    a = act(lambda e, kb=kb, b=b: e.activation(V[:, b, :], PS[:, kb, :], ACT.Copy), a, f["v"])
                    give(kb, a)
                    vr.append(a)
                G[t]["vr"] = vr

            def a1g(t):
                sgr = []
                for b in range(4):
                    kb, fr = take()
                    for k in range(2):
                        a = mm3(PS[:, kb, :], XTH[:, k, b, :], XTL[:, k, b, :], WH["g"][0][:, k, :], WH["g"][1][:, k, :],
                                k == 0, k == 1, [fr, l_g])
                    xts_read[t] = [a]
                    a = act(lambda e, kb=kb, b=b: e.activation(SG[:, b, :], PS[:, kb, :], ACT.Silu), a, f["sg"])
                    give(kb, a)
                    a = pool(lambda e, b=b: e.tensor_tensor(SG[:, b, :], SG[:, b, :], RMS[:], ALU.mult), a, l_rms)
                    sgr.append(a)
                explog()
                if t < 7:
                    split_x(t + 1)
                if t + 2 < 8:
                    load_xt(t + 2, xsp[t], f["x1"])
                G[t]["sgr"] = sgr

            def a2(t):
                g_ = G[t]
                qk, g2 = g_["qk"], g_["g2"]
                qgr, kdr, kgr = [], [], []
                for h in range(2):
                    kb, fr = take()
                    for b in range(4):
                        a = mm(PS[:, kb, 128 * b:128 * b + 128], GG[:, 256 * b + 128 * h:256 * b + 128 * h + 128], TRI[:],
                               True, True, [fr, g2, l_tri])
                    e1 = act(lambda e, kb=kb, h=h: e.activation(EP[:, h, :], PS[:, kb, :], ACT.Exp), a, f["ep"])
                    e2 = act(lambda e, kb=kb, h=h: e.activation(EM[:, h, :], PS[:, kb, :], ACT.Exp, scale=-1.0), a, f["em"])
                    give(kb, e2)
                    f["gg"] = [a]
                    kq, mq = qk[h]
                    for hh in range(2):
                        r = slice(64 * hh, 64 * hh + 64)
                        a = dve(lambda e, r=r, h=h, hh=hh, kq=kq: e.scalar_tensor_tensor(
                            out=QG[r, h, hh, :], in0=PS[r, kq, :], scalar=0.125, in1=EP[r, h, :],
                            op0=ALU.mult, op1=ALU.mult), e1, mq, z_qg, f["qg"])
                    give(kq, a)
                    qgr.append(a)
                    kk, mk = qk[2 + h]
                    a = dve(lambda e, h=h, kk=kk: e.tensor_tensor(KD[:, h, :], PS[:, kk, :], EM[:, h, :], ALU.mult), e2, mk, f["kd"])
                    give(kk, a)
                    kdr.append(a)
                    lastc = EP[:, h, :].rearrange("p (c s) -> p c s", s=64)[:, :, 63:64].to_broadcast([128, 8, 64])
                    a = pool(lambda e, h=h, lastc=lastc: e.tensor_tensor(
                        KG[:, h, :].rearrange("p (c s) -> p c s", s=64), KD[:, h, :].rearrange("p (c s) -> p c s", s=64),
                        lastc, ALU.mult), a, e1, f["kg"])
                    kgr.append(a)
                f["em"] = kdr
                g_.update(qgr=qgr, kdr=kdr, kgr=kgr)

            def a3(t):
                g_ = G[t]
                qgr, kdr, kgr = g_["qgr"], g_["kdr"], g_["kgr"]
                atr = []
                for h in range(2):
                    for p in range(2):
                        kb, fr = take()
                        for j in range(2):
                            b = 2 * p + j
                            a = mm(PS[:, kb, 256 * j:256 * j + 256].rearrange("p (h s) -> p h s", h=2),
                                   KD[:, h, 128 * b:128 * b + 128], QG[:, h, :, 128 * b:128 * b + 128],
                                   True, True, [fr, qgr, kdr])
                        dst = AT[:].rearrange("p (b g) s -> p b g s", b=4)[:, 2 * p:2 * p + 2, 2 * h:2 * h + 2, :]
                        for j in range(2):
                            a2_ = dve(lambda e, kb=kb, j=j, dst=dst: e.copy_predicated(
                                dst[:, j], MSK[:].unsqueeze(1).to_broadcast([128, 2, 128]),
                                PS[:, kb, 256 * j:256 * j + 256].rearrange("p (h s) -> p h s", h=2)),
                                a, z_at, l_msk, f["at"])
                        give(kb, a2_)
                        atr.append(a2_)
                f["kd"] = [a, kgr]
                kzr = []
                for p in range(2):
                    kb, fr = take()
                    for j in range(2):
                        for h in range(2):
                            b = 2 * p + j
                            a = tr(PS[:, kb, 256 * j + 128 * h:256 * j + 128 * h + 128], KG[:, h, 128 * b:128 * b + 128],
                                   [fr, kgr, l_idn])
                    for c in range(2):
                        r = slice(64 * c, 64 * c + 64)
                        a2_ = act(lambda e, r=r, c=c, p=p, kb=kb: e.activation(
                            KZ[r, c, 2 * p:2 * p + 2, :], PS[r, kb, :].rearrange("p (b s) -> p b s", b=2), ACT.Copy), a, z_kz, f["kz"])
                    give(kb, a2_)
                    kzr.append(a2_)
                f["kg"] = [a]
                g_.update(atr=atr, kzr=kzr)

            def a4(t, between):
                g_ = G[t]
                atr, kzr, kgr, vr, sgr = (g_[k] for k in ("atr", "kzr", "kgr", "vr", "sgr"))
                ob = []
                for b in range(4):
                    kb, fr = take()
                    for hd in range(4):
                        a = mm(PS[:, kb, 128 * hd:128 * hd + 128], AT[:, 4 * b + hd, :], V[:, b, 128 * hd:128 * hd + 128],
                               hd == 0, False, [fr, atr, vr], skip=True)
                    ob.append(kb)
                f["at"] = [a]
                sk = {}
                oend = [None] * 4
                for c in range(2):
                    if c == 1:
                        between()
                    cur, nxt = c, 1 - c
                    for h in range(2):
                        kb, fr = take()
                        for b in range(4):
                            for hh in range(2):
                                hd = 2 * h + hh
                                a = mm(PS[64 * hh:64 * hh + 64, kb, 128 * b:128 * b + 128],
                                       KZ[:, c, b, 64 * hd:64 * hd + 64], V[:, b, 128 * hd:128 * hd + 128],
                                       True, True, [fr, kzr])
                        sk[h] = (kb, a)
                    kzl = a
                    for b in range(4):
                        for h in range(2):
                            for hh in range(2):
                                hd = 2 * h + hh
                                a = mm(PS[64 * c:64 * c + 64, ob[b], 128 * hd:128 * hd + 128],
                                       QG[:, h, hh, 128 * b + 64 * c:128 * b + 64 * c + 64], S[:, cur, h, b, :],
                                       False, c == 1, [s_ready[4 * h + b]], skip=True)
                            s_read[4 * h + b] = [a]
                        oend[b] = a
                    for h in range(2):
                        kb, m_ = sk[h]
                        for b in range(4):
                            ecol = EP[:, h, 128 * b + 64 * c + 63:128 * b + 64 * c + 64]
                            s_ready[4 * h + b] = dve(lambda e, h=h, b=b, kb=kb, cur=cur, nxt=nxt, ecol=ecol: e.scalar_tensor_tensor(
                                out=S[:, nxt, h, b, :], in0=S[:, cur, h, b, :], scalar=ecol,
                                in1=PS[:, kb, 128 * b:128 * b + 128], op0=ALU.mult, op1=ALU.add),
                                m_, s_ready[4 * h + b])
                        give(kb, s_ready[4 * h + 3])
                        f["ep"] = [s_ready[4 * h + 3], kgr]
                f["kz"], f["v"], f["qg"] = [kzl], [kzl], [oend[3]]
                for b in range(4):
                    for hd in range(4):
                        i = 4 * b + hd
                        a = act(lambda e, b=b, hd=hd, i=i, kb=ob[b]: e.activation(
                            SQ[:], PS[:, kb, 128 * hd:128 * hd + 128], ACT.Square, accum_out=SS[:, i:i + 1]),
                            oend[b], a if i else f["sr"])
                r = rsqrt(SR[:], SS[:], SL[:], 1.0 / 128, 0, a, f["sr"])
                yr = []
                for b in range(4):
                    for hd in range(4):
                        i = 4 * b + hd
                        a = dve(lambda e, b=b, hd=hd, i=i, kb=ob[b]: e.scalar_tensor_tensor(
                            out=Y[:, b, 128 * hd:128 * hd + 128], in0=PS[:, kb, 128 * hd:128 * hd + 128],
                            scalar=SR[:, i:i + 1], in1=SG[:, b, 128 * hd:128 * hd + 128], op0=ALU.mult, op1=ALU.mult),
                            r, sgr[b], f["y"])
                    give(ob[b], a)
                    yr.append(a)
                f["sg"], f["sr"] = [a], [a]
                g_["yr"] = yr

            def b1(t):
                g_ = G[t]
                yr = g_["yr"]
                ytr = []
                for b in range(4):
                    kb, fr = take()
                    for hd in range(4):
                        a = tr(PS[:, kb, 128 * hd:128 * hd + 128], Y[:, b, 128 * hd:128 * hd + 128], [fr, yr[b]])
                    a2_ = act(lambda e, b=b, kb=kb: e.activation(YT[:, 4 * b:4 * b + 4, :], PS[:, kb, :].rearrange("p (h s) -> p h s", h=4), ACT.Copy), a, f["yt"])
                    give(kb, a2_)
                    ytr.append(a2_)
                f["y"] = [a]
                g_["ytr"] = ytr

            def b2(t):
                g_ = G[t]
                ytr = g_["ytr"]
                xs_t = XS[t % 2]
                res = []
                for p in range(2):
                    kb, fr = take()
                    for j in range(2):
                        b = 2 * p + j
                        for hd in range(4):
                            a = mm(PS[:, kb, 256 * j:256 * j + 256], YT[:, 4 * b + hd, :], WO[:, hd, :], hd == 0, hd == 3,
                                   [fr, ytr[b], l_o])
                    a2_ = dve(lambda e, p=p, kb=kb: e.tensor_tensor(
                        xs_t[:, 2 * p:2 * p + 2, :], xs_t[:, 2 * p:2 * p + 2, :],
                        PS[:, kb, :].rearrange("p (b d) -> p b d", b=2), ALU.add), a, lxs[t])
                    give(kb, a2_)
                    res.append(a2_)
                f["yt"] = [a]
                g_["st"] = ln_stats([xs_t[:, b, :] for b in range(4)], res)

            def b2b(t):
                g_ = G[t]
                xs = [XS[t % 2][:, b, :] for b in range(4)]
                n1 = ln_apply(xs, xs, ln_rstd(4, g_["st"]))
                g_["st"] = ln_stats(xs, n1)

            def b2c(t):
                g_ = G[t]
                xs = [XS[t % 2][:, b, :] for b in range(4)]
                n2 = ln_apply(xs, [nav[:, b, t, :] for b in range(4)], ln_rstd(4, g_["st"]), zx)
                st = Q.dma("sp", x_out[:, :, t, :], XS[t % 2][:], g_["st"])
                if t + 2 < 8:
                    load_xs(t + 2, st, n2)
                a = pool(lambda e: e.tensor_tensor(nav[:, :, t, :], nav[:, :, t, :], GAM[:].unsqueeze(1).to_broadcast([128, 4, 256]), ALU.mult), n2, l_gam)
                a = pool(lambda e: e.tensor_tensor(nav[:, :, t, :], nav[:, :, t, :], BET[:].unsqueeze(1).to_broadcast([128, 4, 256]), ALU.add), a, l_bet)
                g_["nr"] = a

            def b3(t):
                g_ = G[t]
                ntr = []
                for k in range(2):
                    kb, fr = take()
                    for b in range(4):
                        a = tr(PS[:, kb, 128 * b:128 * b + 128], nav[:, b, t, 128 * k:128 * k + 128], [fr, g_["nr"]])
                    a = dve(lambda e, k=k, kb=kb: e.tensor_copy(NTT[:, k], PS[:, kb, :].rearrange("p (b s) -> p b s", b=4)), a, f["ntt"])
                    give(kb, a)
                    ntr.append(a)
                g_["ntr"] = ntr

            def b4(t):
                g_ = G[t]
                ntr = g_["ntr"]
                kb, fr = take()
                for b in range(4):
                    mm(PS[:, kb, 8 * b:8 * b + 8], NTT[:, 0, b, :], RW[:, 0, :], True, False, [fr, ntr, l_rw])
                    ml_ = mm(PS[:, kb, 8 * b:8 * b + 8], NTT[:, 1, b, :], RW[:, 1, :], False, True)
                a = dve(lambda e, kb=kb: e.tensor_copy(lgv[:, :, t, :], PS[:, kb, 0:32].rearrange("p (b e) -> p b e", b=4)), ml_)
                give(kb, a)
                f["ntt"] = [ml_]

            for t in range(9):
                now, before = t < 8, t > 0
                if now:
                    a1(t)
                    a1v(t)
                if before:
                    b1(t - 1)
                if now:
                    a2(t)
                if before:
                    b2(t - 1)
                if now:
                    a3(t)
                if before:
                    b2b(t - 1)
                if now:
                    a1g(t)
                if before:
                    b2c(t - 1)
                if now:
                    a4(t, lambda: b3(t - 1) if t > 0 else None)
                else:
                    b3(t - 1)
                if before:
                    b4(t - 1)
            Q.barrier()

        def choose(lg, tag, c, *w):
            b3 = [128, 32, 8]
            LG, PB, OH, T8 = (sb(n + tag, b3, F32, c) for n in ("LG", "PB", "OH", "T8"))
            M1, M2, R1 = (sb(n + tag, [128, 32], F32, c) for n in ("M1", "M2", "R1"))
            up = lambda m: m.unsqueeze(2).to_broadcast(b3)
            a = red(M1[:], lg, ALU.max, *w)
            a = tt(LG[:], lg, up(M1[:]), ALU.subtract, a)
            lg_read = a
            a = act(lambda e: e.activation(PB[:], LG[:], ACT.Exp), a)
            a = red(M2[:], PB[:], ALU.add, a)
            a = dve(lambda e: e.reciprocal(R1[:], M2[:]), a)
            a = tt(PB[:], PB[:], up(R1[:]), ALU.mult, a)

            def top(m, oh, r, a):
                a = red(m[:], PB[:], ALU.max, a)
                a = tt(T8[:], PB[:], up(m[:]), ALU.is_equal, a)
                a = tt(T8[:], T8[:], IREV[:].unsqueeze(1).to_broadcast(b3), ALU.mult, a, l_irev)
                a = red(r[:], T8[:], ALU.max, a)
                return tt(oh[:], T8[:], up(r[:]), ALU.is_equal, a)
            a = top(M1, OH, R1, a)
            a = dve(lambda e: e.scalar_tensor_tensor(out=PB[:], in0=OH[:], scalar=-2.0, in1=PB[:], op0=ALU.mult, op1=ALU.add), a)
            a = top(M2, LG, R1, a)
            return OH, LG, M1, M2, R1, T8, lg_read, a

        tt = lambda o, x, y, op, *w: dve(lambda e: e.tensor_tensor(o, x, y, op), *w)
        red = lambda o, x, op, *w: dve(lambda e: e.tensor_reduce(o, x, AX, op), *w)

        with ExitStack() as c2:
            s2 = lambda n, s, d=F32: sb(n, s, d, c2)
            WALL = s2("WALL", [128, 8 * 4608])
            SLT, ONE = s2("SLT", [128, 128]), s2("ONE", [128, 128])
            CNT = s2("CNT", [128, 104])
            INC = s2("INC", [128, 32, 8])
            TL, IT, BT_ = (s2(n, [128, 8]) for n in ("TL", "IT", "BT_"))
            TE = s2("TE", [128, 72])
            TI = s2("TI", [128, 72], I32)
            PF = s2("PF", [128, 32])
            XB = s2("XB", [128, 3, 256])
            XI = [XB[:, i, :] for i in range(3)]
            XIT = [s2(f"XIT{i}", [128, 2, 128]) for i in range(2)]
            SI = s2("SI", [128, 768])
            HB = s2("HB", [128, 1536])
            HI = HB[:, 0:768]
            HT = HB[:, 768:1536].rearrange("p (i s) -> p i s", s=128)
            t8 = lambda m: m.rearrange("p (t e) -> p t e", e=8)
            CC, TOT = t8(SI[:, 0:256]), t8(SI[:, 256:512])
            C32 = SI[:, 512:768].rearrange("p (e t) -> p e t", t=32)
            CT = t8(HI[:, 0:576])
            POS = t8(HB[:, 768:1024])
            YI = [s2(f"YI{i}", [128, 256]) for i in range(2)]
            l_slt, l_cnt = Q.dma("sp", SLT[:], A["c_slt"]), Q.dma("sp", CNT[:], A["c_cnt"])
            z_one = pool(lambda e: e.memset(ONE[:], 1.0))

            at = lambda c, n, k: WALL[:, 7 * 4608 + c:7 * 4608 + c + n].rearrange("p (k n) -> p k n", k=k)
            SGU, NT_, SDN, HS, XR0 = at(0, 1024, 2), at(1024, 1024, 2), at(2048, 512, 2), at(2560, 1024, 2), at(3584, 1024, 4)
            XR = [XR0, HB[:, 0:1024].rearrange("p (k n) -> p k n", k=4)]
            SU = XB[:].rearrange("p i d -> p (i d)")[:, 0:512]
            l_sg, l_sd = Q.dma("sp", SGU, A["sgu"]), Q.dma("sp", SDN, A["sdn"])
            sf = {k: [] for k in ("nt", "hs", "su", "xr")}
            sh, l_we = {}, []

            def load_expert(e_, c0, c1, *w):
                l_we.append(Q.dma("sp", WALL[:, 4608 * e_ + c0:4608 * e_ + c1], A["we"][e_][:, c0:c1], *w))

            def load_xr(t, *w):
                sh["xr", t] = Q.dma("sp", XR[t % 2], x_out[:, :, t, :], *w)

            def shared_turn(t):
                if t == 0:
                    load_xr(0)
                ntr = []
                for k in range(2):
                    kb, fr = take()
                    for b in range(4):
                        a = tr(PS[:, kb, 128 * b:128 * b + 128], nav[:, b, t, 128 * k:128 * k + 128], [fr])
                    a = act(lambda e, k=k, kb=kb: e.activation(NT_[:, k, :], PS[:, kb, :], ACT.Copy), a, sf["nt"])
                    give(kb, a)
                    ntr.append(a)
                sh["nt", t] = ntr

            def shared_up(t):
                ks = []
                for fx in range(2):
                    for o in range(2):
                        kb, fr = take()
                        c0 = 256 * o + 128 * fx
                        mm(PS[:, kb, :], SGU[:, 0, c0:c0 + 128], NT_[:, 0, :], True, False, [fr, sh["nt", t], l_sg])
                        a = mm(PS[:, kb, :], SGU[:, 1, c0:c0 + 128], NT_[:, 1, :], False, True)
                        ks.append((kb, a))
                sf["nt"] = [a]
                sh["up", t] = ks

            def shared_hidden(t):
                hr = []
                for fx in range(2):
                    (kg, mg), (ku, mu) = sh["up", t][2 * fx:2 * fx + 2]
                    a1_ = act(lambda e, kg=kg: e.activation(SU, PS[:, kg, :], ACT.Silu), mg, sf["su"])
                    give(kg, a1_)
                    a2_ = dve(lambda e, ku=ku, fx=fx: e.tensor_tensor(HS[:, fx, :], PS[:, ku, :], SU, ALU.mult), mu, a1_, sf["hs"])
                    give(ku, a2_)
                    sf["su"] = [a2_]
                    hr.append(a2_)
                sh["h", t] = hr

            def shared_down(t):
                ad = []
                for p in range(2):
                    kb, fr = take()
                    for j in range(2):
                        b = 2 * p + j
                        for fx in range(2):
                            a = mm(PS[:, kb, 256 * j:256 * j + 256], HS[:, fx, 128 * b:128 * b + 128], SDN[:, fx, :], fx == 0, fx == 1,
                                   [fr, sh["h", t], l_sd])
                    a2_ = dve(lambda e, p=p, kb=kb: e.tensor_tensor(
                        XR[t % 2][:, 2 * p:2 * p + 2, :], XR[t % 2][:, 2 * p:2 * p + 2, :],
                        PS[:, kb, :].rearrange("p (b d) -> p b d", b=2), ALU.add), a, sh["xr", t])
                    give(kb, a2_)
                    ad.append(a2_)
                sf["hs"] = [a]
                if t == 7:
                    load_expert(7, 2048, 3584, a)
                st = sh["st", t] = Q.dma("sp", x_out[:, :, t, :], XR[t % 2], ad)
                if 0 < t < 6:
                    load_xr(t + 2, st)
                for e_ in {1: (2, 3), 2: (4,), 3: (5,), 4: (6,)}.get(t, ()):
                    load_expert(e_, 0, 4608)

            shared_turn(0)
            load_expert(0, 0, 4608)
            shared_up(0)
            explog()
            OH1, OH2, M1, M2, R1, T8, _, a = choose(LGA[:], "a", c2)
            g_ = tt(R1[:], M2[:], M1[:], ALU.subtract, a)
            g_ = act(lambda e: e.activation(R1[:], R1[:], ACT.Exp), g_)
            c_ = tt(CC, OH1[:], OH2[:], ALU.add, a)
            shared_hidden(0)
            shared_turn(1)
            kb, fr = take()
            mm(PS[:, kb, 0:256], SLT[:], SI[:, 0:256], True, True, [fr, c_, l_slt])
            a = mm(PS[:, kb, 256:512], ONE[:], SI[:, 0:256], True, True, [z_one])
            load_expert(1, 0, 4608)
            shared_down(0)
            shared_up(1)
            pre = PS[:, kb, 0:256].rearrange("p (t e) -> p t e", e=8)
            tot = PS[:, kb, 256:512].rearrange("p (t e) -> p t e", e=8)
            a = dve(lambda e: e.tensor_copy(TOT, tot), a)
            for e_ in range(8):
                a2 = dve(lambda e, e_=e_: e.tensor_tensor_scan(INC[:, :, e_], ONE[:, 0:32], TOT[:, :, e_], 0.0, ALU.mult, ALU.add), a)
            a = a2
            cnt_b = INC[:, 31, :].unsqueeze(2).to_broadcast([128, 8, 32])
            a = tt(C32, cnt_b, CNT[:, 0:32].unsqueeze(1).to_broadcast([128, 8, 32]), ALU.is_gt, a, l_cnt)
            a = red(TL[:], C32, ALU.add, a)
            a = dve(lambda e: e.tensor_tensor_scan(IT[:], ONE[:, 0:8], TL[:], 0.0, ALU.mult, ALU.add), a)
            a2 = tt(BT_[:], IT[:], TL[:], ALU.subtract, a)
            a2 = tt(POS, INC[:], TOT, ALU.subtract, a2)
            a2 = tt(POS, pre, POS, ALU.add, a2)
            give(kb, a2)
            a2 = dve(lambda e: e.scalar_tensor_tensor(out=POS, in0=BT_[:].unsqueeze(1).to_broadcast([128, 32, 8]), scalar=128.0,
                                                      in1=POS, op0=ALU.mult, op1=ALU.add), a2)
            pr_ = []
            for k, oh in enumerate((OH1, OH2)):
                a2 = tt(T8[:], oh[:], POS, ALU.mult, a2)
                a2 = red(PF[:], T8[:], ALU.add, a2)
                a2 = dve(lambda e, k=k: e.tensor_copy(PI[k][:], PF[:]), a2)
                pr_.append(a2)
            a = tt(CT, IT[:].unsqueeze(1).to_broadcast([128, 72, 8]), CNT[:, 32:104].unsqueeze(2).to_broadcast([128, 72, 8]), ALU.is_le, a)
            a = red(TE[:], CT, ALU.add, a)
            a = dve(lambda e: e.tensor_scalar(TE[:], TE[:], 7.0, 4608.0, ALU.min, ALU.mult), a)
            te = dve(lambda e: e.tensor_copy(TI[:], TE[:]), a)
            te.marked = True
            g_ = dve(lambda e: e.tensor_scalar(GT[1][:], R1[:], 1.0, None, ALU.add), g_)
            g_ = dve(lambda e: e.reciprocal(GT[0][:], GT[1][:]), g_)
            g_ = tt(GT[1][:], R1[:], GT[0][:], ALU.mult, g_)

            sc = []
            for t in range(32):
                for k in range(2):
                    sc.append(Q.idma(XS_D, bass.IndirectOffsetOnAxis(PI[k][:, t:t + 1], 0), NALL[:, t, :], None, pr_))

            xf, lx2 = [[], [], []], {}

            def load_rows(s):
                lx2[s] = Q.dma("sp", XI[(s + 2) % 3], XS_D[128 * s:128 * s + 128, :], sc, xf[(s + 2) % 3])

            load_xr(1, te)
            load_xr(2, sh["st", 0])
            shared_hidden(1)
            for t in range(1, 8):
                if t < 7:
                    shared_turn(t + 1)
                else:
                    load_rows(0)
                    load_expert(7, 3584, 4608, sh["st", 6])
                    xf[0], xf[1] = [sf["su"]], [sf["su"]]
                shared_down(t)
                if t < 7:
                    shared_up(t + 1)
                    if t == 6:
                        load_expert(7, 0, 2048, sf["nt"])
                    shared_hidden(t + 1)
            xtf, yf = [[], []], [[], []]
            bank_read = [o for _, o in banks]
            set_free = [[[bank_read] for _ in range(3)] for _ in range(2)]
            b67 = [[bank_read], [bank_read]]
            hif, htf, sif = [sh["st", 7]], [], []
            xtr2, hr2, ht2 = {}, {}, {}

            def turn_rows(s):
                bk = 6 + s % 2
                for k in range(2):
                    a = tr(PS[:, bk, 128 * k:128 * k + 128], XI[(s + 2) % 3][:, 128 * k:128 * k + 128], [b67[s % 2], lx2[s]])
                xf[(s + 2) % 3] = [a]
                a = dve(lambda e: e.tensor_copy(XIT[s % 2][:], PS[:, bk, 0:256].rearrange("p (k s) -> p k s", k=2)), a, xtf[s % 2])
                b67[s % 2] = [a]
                xtr2[s] = a

            regs = {}

            def wide(s, off, n):
                return lambda: WALL[:, bass.ds(regs["r"][s % 2] + off, n)]

            def mmr(o, l, get, start, stop, w=()):
                return pe(lambda e: e.matmul(o, l, get(), start=start, stop=stop), *w)

            def expert_of(s):
                def go(e):
                    regs.setdefault("r", {})[s % 2] = e.value_load(TI[0:1, s:s + 1], min_val=0, max_val=7 * 4608)
                    return None
                Q.q["pe"].append(Op("pe", go, [te]))
                Q.q["pe"][-1].step = 0

            def up_piece(s, c):
                bk = 3 * (s % 2) + c
                mmr(PS[:, bk, :], XIT[s % 2][:, 0, :], wide(s, 512 * c, 512), True, False, [set_free[s % 2][c], xtr2[s], l_we])
                return mmr(PS[:, bk, :], XIT[s % 2][:, 1, :], wide(s, 1536 + 512 * c, 512), False, True)

            def hidden(s, a):
                gu = PS[:, 3 * (s % 2):3 * (s % 2) + 3, :].rearrange("p k s -> p (k s)")
                a1_ = act(lambda e: e.activation(SI[:], gu[:, 0:768], ACT.Silu), a, sif)
                a2_ = dve(lambda e: e.tensor_tensor(HI, gu[:, 768:1536], SI[:], ALU.mult), a1_, a, hif)
                sif[:] = [a2_]
                for c in range(3):
                    set_free[s % 2][c] = [a2_]
                hr2[s] = a2_

            def turn_hidden(s):
                b0 = 3 * (s % 2)
                for i in range(6):
                    a = tr(PS[:, b0 + i // 4, 128 * (i % 4):128 * (i % 4) + 128], HI[:, 128 * i:128 * i + 128], [set_free[s % 2], hr2[s]])
                hif[:] = [a]
                a = act(lambda e: e.activation(HB[:, 768:1536], PS[:, b0:b0 + 2, :].rearrange("p k s -> p (k s)")[:, 0:768], ACT.Copy), a, htf)
                set_free[s % 2][0] = set_free[s % 2][1] = [a]
                ht2[s] = a

            def down(s):
                bk = 3 * (s % 2) + 2
                for i in range(6):
                    a = mmr(PS[:, bk, 0:256], HT[:, i, :], wide(s, 3072 + 256 * i, 256), i == 0, i == 5, [set_free[s % 2][2], ht2[s]])
                htf[:] = [a]
                y = YI[s % 2]
                a = dve(lambda e: e.tensor_copy(y[:], PS[:, bk, 0:256]), a, yf[s % 2])
                set_free[s % 2][2] = [a]
                yf[s % 2] = [Q.dma("sp", YS_D[128 * s:128 * s + 128, :], y[:], a)]

            load_rows(1)
            turn_rows(0)
            for s in range(NT + 1):
                if s < NT:
                    expert_of(s)
                    up_piece(s, 0)
                    if s + 2 < NT:
                        load_rows(s + 2)
                    up_piece(s, 1)
                if s > 0:
                    turn_hidden(s - 1)
                if s < NT:
                    a = up_piece(s, 2)
                    xtf[s % 2] = [a]
                    hidden(s, a)
                if s + 1 < NT:
                    turn_rows(s + 1)
                if s > 0:
                    down(s - 1)
            Q.barrier()
        cA.close()

        PARTS = nc.dram_tensor("parts", (2, 3, 512, 4096), BF16, kind="Internal").ap()
        X = sb("X", [128, 32, 256])
        VP_D = nc.dram_tensor("values", (4, 128, 8, 288), F32, kind="Internal").ap()
        with ExitStack() as c3:
            s3 = lambda n, s, d=F32: sb(n, s, d, c3)
            XH, XO = s3("XH", [128, 2, 4096], F32R), s3("XO", [128, 2, 4096], F32R)
            XL = [s3(f"XL{i}", [128, 4, 256]) for i in range(2)]
            YG = [s3(f"YG{i}", [128, 256]) for i in range(16)]
            ygf = [[] for _ in range(16)]
            xlf = [[], []]
            xtr = {}
            tt = lambda o, x, y, op, *w: dve(lambda e: e.tensor_tensor(o, x, y, op), *w)

            def combine(gI, i):
                xl = XL[gI % 2]
                if i == 0 and gI < 7:
                    load_xl(gI + 1)
                if i < 4:
                    t = 4 * gI + i
                    a = []
                    for k in range(2):
                        z = (2 * t + k) % len(YG)
                        g = gathered.pop(0)
                        src = xl[:, i, :] if k == 0 else X[:, t, :]
                        a = dve(lambda e, t=t, k=k, z=z, src=src: e.scalar_tensor_tensor(
                            out=X[:, t, :], in0=YG[z][:], scalar=GT[k][:, t:t + 1], in1=src, op0=ALU.mult, op1=ALU.add),
                            g, lxl[gI], a, r_ww if gI > 3 else [])
                        ygf[z] = [a]
                    last_x[0] = a
                    return
                xlf[gI % 2] = [last_x[0]]
                xs = [X[:, 4 * gI + i, :] for i in range(4)]
                ln = {"s": ln_stats(xs, last_x[0])}

                def rstd():
                    ln["r"] = ln_rstd(4, ln["s"])

                def apply():
                    ln["n"] = ln_apply(xs, xs, ln["r"])

                def turn_x():
                    xr_ = []
                    for k in range(2):
                        kb, fr = take()
                        for i in range(4):
                            a = tr(PS[:, kb, 128 * i:128 * i + 128], xs[i][:, 128 * k:128 * k + 128], [fr, ln["n"]])
                        c_ = slice(512 * gI, 512 * gI + 512)
                        h = split(XH[:, k, c_], XO[:, k, c_], PS[:, kb, :], act, dve, a)
                        give(kb, h)
                        xr_ += h
                    xtr[gI] = xr_
                return rstd, apply, turn_x

            def load_xl(gI):
                lxl[gI] = Q.dma("sp", XL[gI % 2][:], XR_D[:, 4 * gI:4 * gI + 4, :], xlf[gI % 2])

            def gather(t):
                for k in range(2):
                    z = (2 * t + k) % len(YG)
                    gathered.append(Q.idma(YG[z][:], None, YS_D, bass.IndirectOffsetOnAxis(PI[k][:, t:t + 1], 0), ygf[z]))
            gathered, lxl, last_x = [], {}, [None]
            load_xl(0)

            WWH = [s3(f"WWH{i}", [128, 2, 1024], F32R) for i in range(2)]
            WWL = [s3(f"WWL{i}", [128, 2, 1024], F32R) for i in range(2)]
            WV1, BV = s3("WV1", [128, 2, 256]), s3("BV", [128, 256])
            WVH, WVL = s3("WVH", [128, 2, 256], F32R), s3("WVL", [128, 2, 256], F32R)
            VS = [s3(f"VS{i}", [128, 4, 288]) for i in range(2)]
            BB = s3("BB", [128, 2, 2, 4])
            CS = s3("CS", [128, 2, 1024])
            NP = 4
            T1 = [s3(f"TA{i}", [128, 512]) for i in range(NP)]
            T2 = [s3(f"TB{i}", [128, 512]) for i in range(NP)]
            PP = [s3(f"PP{i}", [128, 3, 512], BF16) for i in range(NP)]
            for t in range(6):
                gather(t)
            explog()
            l_v1, l_bv = Q.dma("sp", WV1[:], A["wv1"]), Q.dma("sp", BV[:], A["bv"])
            l_bb, l_cs = Q.dma("sp", BB[:], A["bqk"]), Q.dma("sp", CS[:], A["c_cs"])
            r_ww = []
            WW = [X[:, 16 + 8 * k:24 + 8 * k, :].rearrange("p t d -> p (t d)").rearrange("p (a c) -> p a c", a=2) for k in range(2)]
            l_ww = [Q.dma("sp", WW[i], A["wqk"][i]) for i in range(2)]
            tf, pf = [[] for _ in range(NP)], [[] for _ in range(NP)]

            def rotate(i, b, qi, fb, hf):
                tok = 1024 * b + 512 * hf
                ts = slice(tok, tok + 512)
                (ka, fa), (kb, fr) = take(), take()
                for bank, fx, o in ((ka, fa, 0), (kb, fr, 512)):
                    c = slice(o + 128 * fb, o + 128 * fb + 128)
                    for k in range(2):
                        a = mm3(PS[:, bank, :], WWH[qi][:, k, c], WWL[qi][:, k, c], XH[:, k, ts], XO[:, k, ts],
                                k == 0, k == 1, [fx, r_ww[qi], xtr[2 * b + hf]])
                    if o == 0:
                        am = a
                t1, t2, pp = T1[i % NP], T2[i % NP], PP[i % NP]
                a1 = dve(lambda e: e.scalar_tensor_tensor(
                    out=t1[:], in0=PS[:, ka, :], scalar=BB[:, qi, 0, fb:fb + 1], in1=CS[:, 0, 512 * hf:512 * hf + 512],
                    op0=ALU.add, op1=ALU.mult), am, l_bb, l_cs, tf[i % NP])
                a2 = dve(lambda e: e.scalar_tensor_tensor(
                    out=t2[:], in0=PS[:, kb, :], scalar=BB[:, qi, 1, fb:fb + 1], in1=CS[:, 1, 512 * hf:512 * hf + 512],
                    op0=ALU.add, op1=ALU.mult), a)
                give(ka, a1)
                give(kb, a2)
                r = pool(lambda e: e.tensor_tensor(t1[:], t1[:], t2[:], ALU.add), a1, a2)

                def first():
                    h = act(lambda e: e.activation(pp[:, 0, :], t1[:], ACT.Copy), r, pf[i % NP])
                    return dve(lambda e: e.tensor_tensor(t1[:], t1[:], pp[:, 0, :], ALU.subtract), h)

                def second(d):
                    m = act(lambda e: e.activation(pp[:, 1, :], t1[:], ACT.Copy), d)
                    l = pool(lambda e: e.tensor_tensor(pp[:, 2, :], t1[:], pp[:, 1, :], ALU.subtract), m)
                    tf[i % NP] = [l]
                    w = Q.dma("sp", PARTS[qi, :, 128 * fb:128 * fb + 128, tok:tok + 512].rearrange("c p s -> p c s"), pp[:], l)
                    pf[i % NP] = [w]
                return first, second

            def values(b, q):
                ends = []
                for h in range(2):
                    kb, fr = take()
                    for i in range(2):
                        t0 = 1024 * b + 512 * q + 256 * h + 128 * i
                        for k in range(2):
                            ts = slice(t0, t0 + 128)
                            mmo = PS[:, kb, 256 * i:256 * i + 256]
                            a = mm3(mmo, XH[:, k, ts], XO[:, k, ts], WVH[:, k, :], WVL[:, k, :], k == 0, k == 1,
                                    [fr, r_wv, xtr[2 * b + q]])
                    a = dve(lambda e, h=h, kb=kb: e.tensor_tensor(
                        VS[q][:, 2 * h:2 * h + 2, 0:272].rearrange("p i (h d) -> p i h d", d=17)[:, :, :, 0:16],
                        PS[:, kb, :].rearrange("p (i h d) -> p i h d", i=2, d=16),
                        BV[:].rearrange("p (h d) -> p h d", d=16).unsqueeze(1).to_broadcast([128, 2, 16, 16]), ALU.add),
                        a, l_bv, vsf[q])
                    give(kb, a)
                    ends.append(a)
                vsf[q] = [Q.dma("sp", VP_D[b][:, 4 * q:4 * q + 4, :], VS[q][:], ends)]

            def feeder():
                turn_before = None
                for gI in range(8):
                    box = []
                    for i in range(4):
                        t = 4 * gI + i

                        def go(t=t, gI=gI, i=i, box=box):
                            combine(gI, i)
                            if t + 6 < 32:
                                gather(t + 6)
                            if i == 3:
                                box += combine(gI, 4)
                        yield go
                        if i == 1 and turn_before is not None:
                            yield lambda box=turn_before: box[2]()
                    yield lambda box=box: box[0]()
                    yield lambda box=box: box[1]()
                    turn_before = box
                yield lambda box=turn_before: box[2]()
            feed = list(feeder())
            for _ in range(4):
                feed.pop(0)()
            r_ww.append(split(WWH[0][:], WWL[0][:], WW[0], act, dve, l_ww[0]))
            for _ in range(5):
                feed.pop(0)()
            r_ww.append(split(WWH[1][:], WWL[1][:], WW[1], act, dve, l_ww[1]))
            r_wv = split(WVH[:], WVL[:], WV1[:], act, dve, l_v1)
            vsf = [dve(lambda e, q=q: e.memset(VS[q][:], 1.0)) for q in range(2)]
            i, ends = 0, []
            for b in range(4):
                for hf in range(2):
                    for qi in range(2):
                        for fb in range(4):
                            ends.append([rotate(i, b, qi, fb, hf), None])
                            if i > 0:
                                ends[i - 1][1] = ends[i - 1][0][0]()
                            if i > 1:
                                ends[i - 2][0][1](ends[i - 2][1])
                            i += 1
                            if feed:
                                feed.pop(0)()
                    values(b, hf)
            ends[i - 1][1] = ends[i - 1][0][0]()
            for e_ in ends[i - 2:]:
                e_[0][1](e_[1])
            Q.barrier()

        with ExitStack() as c4:
            s4 = lambda n, s, d=F32: sb(n, s, d, c4)
            NE_ = 4
            LAG = 2
            IDB = s4("IDB", [128, 128], BF16)
            MR = s4("MR", [128, 128], BF16)
            WO1 = s4("WO1", [128, 2, 256])
            BO, HN = s4("BO", [128, 256]), s4("HN", [128, 2])
            L1, L2, NL = s4("L1", [128, 16]), s4("L2", [128, 16]), s4("NL", [128, 16])
            NM = [s4(f"NM{i}", [128, 4, 8]) for i in range(2)]
            MP = [s4(f"MP{i}", [32, 3, 128], BF16) for i in range(2)]
            MT = s4("MT", [32, 128])
            OT = s4("OT", [128, 1024])
            OA = [s4(f"OA{i}", [128, 8, 256]) for i in range(2)]
            OB = s4("OB", [128, 8, 256])
            RC = s4("RC", [128, 8, 4])
            O1, O2 = s4("O1", [128, 8, 2, 16]), s4("O2", [128, 8, 2, 16])
            MS, ML = s4("MS", [128, 128]), s4("ML", [128, 128])
            c4b = ExitStack()
            QS = [sb(f"QS{i}", [128, 4, 1024], BF16, c4b) for i in range(4)]
            KS = [sb(f"KS{i}", [128, 4, 1024], BF16, c4b) for i in range(4)]
            VP = [sb(f"VP{i}", [128, 8, 288], F32, c4b) for i in range(2)]
            E = sb("E", [128, NE_, 4, 512], F32, c4b)
            LQ = OB[:].rearrange("p i d -> p (i d)").rearrange("p (a d) -> p a d", d=256)

            explog()
            l_m = Q.dma("sp", E[:, 0, 0, 0:128], A["c_mrc"])
            l_idb = act(lambda e: e.activation(IDB[:], IDN[:], ACT.Copy))
            l_mr = act(lambda e: e.activation(MR[:], E[:, 0, 0, 0:128], ACT.Copy), l_m)
            l_o1 = Q.dma("sp", WO1[:], A["wo1"])
            l_bo, l_hn = (Q.dma("sp", d[:], A[n]) for d, n in ((BO, "bo"), (HN, "hn")))
            l_lq = Q.dma("sp", LQ[:, 0:4, :], A["lam"])
            z_k = [(pool if i % 2 else dve)(lambda e, i=i: e.memset(KS[i][96:128], 1.0)) for i in range(4)]
            li = 0.8 - 0.6 * 1.0
            a = dve(lambda e: e.tensor_tensor(LQ[:, 0, :], LQ[:, 0, :], LQ[:, 1, :], ALU.mult), l_lq)
            a2 = dve(lambda e: e.tensor_tensor(LQ[:, 2, :], LQ[:, 2, :], LQ[:, 3, :], ALU.mult), l_lq)
            a = dve(lambda e: e.tensor_reduce(L1[:], LQ[:, 0, :].rearrange("p (h d) -> p h d", d=16), AX, ALU.add), a)
            a2 = dve(lambda e: e.tensor_reduce(L2[:], LQ[:, 2, :].rearrange("p (h d) -> p h d", d=16), AX, ALU.add), a2)
            lq_free = a2
            a = act(lambda e: e.activation(L1[:], L1[:], ACT.Exp), a)
            a = act(lambda e: e.activation(L2[:], L2[:], ACT.Exp), a2)
            nl = dve(lambda e: e.scalar_tensor_tensor(out=NL[:], in0=L2[:], scalar=-li, in1=L1[:], op0=ALU.add, op1=ALU.subtract), a)
            hn = [dve(lambda e, k=k: e.tensor_scalar(WO1[:, k, :], WO1[:, k, :], HN[:, k:k + 1], 1.0 - li, ALU.mult, ALU.mult), l_hn, l_o1)
                  for k in range(2)]
            bo = [pool(lambda e, b=b: e.tensor_tensor(X[:, 8 * b:8 * b + 8, :], X[:, 8 * b:8 * b + 8, :],
                  BO[:].unsqueeze(1).to_broadcast([128, 8, 256]), ALU.add), l_bo, z_k) for b in range(4)]

            kvread = {}
            fl, ml, vr = {}, {}, {}
            turn = {"n": 0, "free": [[], []]}
            SB = [4, 5, 6]
            single = {"n": 0, "free": [[] for _ in SB]}
            acc_free = [[]]
            later = []

            def pair():
                k = turn["n"] % 2
                turn["n"] += 1
                return k, turn["free"][k]

            def pv(k):
                return PS[:, 2 * k:2 * k + 2, :]

            def fetch(v):
                b, g = v // 8, v % 8
                ops = []
                for qi, D in ((0, QS[v % 4]), (1, KS[v % 4])):
                    for r0, n, kp in ((0, 3, 0), (48, 2, 1), (80, 1, 2)):
                        for c in range(n):
                            src = PARTS[qi, c if qi == 0 else kp, 64 * g:64 * g + 64, 1024 * b:1024 * b + 1024]
                            ops.append(Q.dma("sp", D[r0 + 16 * c:r0 + 16 * c + 16, :, :],
                                             src.rearrange("(j r) s -> r j s", r=16), kvread.get(v - 4)))
                fl[v] = ops

            nmfree, mpfree, otfree, rcfree = [[], []], [[], []], [[], []], []
            efree = [[] for _ in range(NE_)]
            cnt = {"e": 0, "pend": []}
            vread, oread = {}, [[], []]
            mtfree = []

            def load_values(b):
                vr[b] = [Q.dma("sp", VP[b % 2][:], VP_D[b], vread.get(b - 2))]

            def maxima(v):
                Qs, Ks, nm = QS[v % 4], KS[v % 4], NM[v % 2]
                jobs = [(i, (2 * p, 2 * p + 1)) for i in range(4) for p in range(2)]
                jobs += [(i, (j,)) for i in range(4, 8) for j in range(4)]

                def step(i, js):
                    k, fr = pair()
                    W = 128 * (i + 1)
                    for n_, j in enumerate(js):
                        lhs = Qs[0:96, j, 128 * i:128 * i + 128]
                        for p in range((W + 511) // 512):
                            n = min(512, W - 512 * p)
                            bank = 2 * k + (n_ if len(js) == 2 else p)
                            a = mm(PS[:, bank, 0:n], lhs, Ks[0:96, j, 512 * p:512 * p + n], True, True, [fr, fl[v]])
                            if 512 * p + n == W:
                                a = mm(PS[:, bank, n - 128:n], IDB[:], MR[:], False, True, [l_idb, l_mr], skip=True)
                    if len(js) == 2:
                        src, dst = pv(k)[:, :, 0:W], nm[:, js[0]:js[0] + 2, i]
                    else:
                        src, dst = pv(k).rearrange("p k s -> p (k s)")[:, 0:W], nm[:, js[0], i:i + 1]
                    a = dve(lambda e: e.tensor_reduce(dst, src, AX, ALU.max), a, nmfree[v % 2])
                    turn["free"][k] = [a]
                    cnt["nm"] = a
                return [lambda i=i, js=js: step(i, js) for i, js in jobs]

            def subtract_rows(v, a):
                k, fr = pair()
                p_ = PS[0:32, 2 * k, 0:128]
                mp = MP[v % 2]
                tm = tr(p_, NM[v % 2][:].rearrange("p j i -> p (j i)"), [fr, a])
                nmfree[v % 2] = [tm]
                h = act(lambda e: e.activation(mp[:, 0, :], p_, ACT.Copy, scale=-1.0), tm, mpfree[v % 2])
                d = dve(lambda e: e.scalar_tensor_tensor(out=MT[:], in0=p_, scalar=-1.0, in1=mp[:, 0, :],
                                                         op0=ALU.mult, op1=ALU.subtract), h, mtfree)
                m = act(lambda e: e.activation(mp[:, 1, :], MT[:], ACT.Copy), d)
                l = dve(lambda e: e.tensor_tensor(mp[:, 2, :], MT[:], mp[:, 1, :], ALU.subtract), m)
                mtfree[:] = [l]
                turn["free"][k] = [d]
                ml[v] = [Q.dma("sp", QS[v % 4][96 + p:97 + p, :, :], mp[:, p, :], l, kvread.get(v - 4)) for p in range(3)]
                mpfree[v % 2] = ml[v]

            def exponentials(v):
                Qs, Ks = QS[v % 4], KS[v % 4]
                b, g = v // 8, v % 8
                steps = []
                for p in range(2):
                    for kt in range(4 * p + 4):
                        q0 = max(128 * kt, 512 * p)
                        n = 512 * p + 512 - q0
                        st = {}
                        for pr in range(2):
                            def step(p=p, kt=kt, q0=q0, n=n, pr=pr, st=st):
                                if pr == 0:
                                    st["e"] = cnt["e"] % NE_
                                    cnt["e"] += 1
                                    st["r"] = []
                                ei = st["e"]
                                for x in range(2):
                                    j = 2 * pr + x
                                    z = single["n"] % len(SB)
                                    single["n"] += 1
                                    fr, bank = single["free"][z], SB[z]
                                    lhs = Ks[0:99, j, 128 * kt:128 * kt + 128]
                                    a = mm(PS[:, bank, 0:n], lhs, Qs[0:99, j, q0:q0 + n], True, True, [fr, fl[v], ml[v], z_k])
                                    a = act(lambda e, j=j, bank=bank: e.activation(E[:, ei, j, 0:n], PS[:, bank, 0:n], ACT.Exp, scale=0.25),
                                            a, efree[ei], l_mr)
                                    single["free"][z] = [a]
                                    st["r"].append(a)
                                if pr == 1:
                                    if q0 == 128 * kt:
                                        st["r"] = [pool(lambda e: e.affine_select(
                                            out=E[:, ei, :, 0:128], in_=E[:, ei, :, 0:128], pattern=[[0, 4], [1, 128]],
                                            compare_op=ALU.is_ge, fill=0.0, base=0, channel_multiplier=-1), st["r"])]
                                    cnt["pend"].append(lambda: st["av"](ei, st["r"]))
                                    if len(cnt["pend"]) > LAG:
                                        cnt["pend"].pop(0)()
                            steps.append(step)

                        def av(ei, reads, p=p, kt=kt, q0=q0, n=n):
                            for jj in range(4):
                                hd = 2 * g + jj // 2
                                a = mm(PS[32 * jj:32 * jj + 32, 7, 512 - n:512], VP[b % 2][:, kt, 17 * hd:17 * hd + 32],
                                       E[:, ei, jj, 0:n], kt == 0, True, [acc_free[0], reads, vr[b]], skip=True)
                            efree[ei] = [a]
                            if kt == 4 * p + 3:
                                o = (lambda e: e.activation(OT[:, 512 * p:512 * p + 512], PS[:, 7, :], ACT.Copy)) if p == 0 else \
                                    (lambda e: e.tensor_copy(OT[:, 512 * p:512 * p + 512], PS[:, 7, :]))
                                c_ = (act if p == 0 else dve)(o, a, otfree[p])
                                acc_free[0] = [c_]
                                cnt.setdefault("ot", {})[p] = c_
                                if p == 1:
                                    kvread[v] = [a]
                                    if g == 7:
                                        vread[b] = [a]
                                    later.append([3, lambda: heads(v)])
                        st["av"] = av
                return steps

            oar = {}

            def heads(v):
                b, g = v // 8, v % 8
                k, fr = pair()
                for i in range(8):
                    a = tr(PS[:, 2 * k + i // 4, 128 * (i % 4):128 * (i % 4) + 128], OT[:, 128 * i:128 * i + 128],
                           [fr, cnt["ot"][0], cnt["ot"][1]])
                otfree[0] = otfree[1] = [a]
                ov = pv(k).rearrange("p k s -> p (k s)").rearrange("p (i h m d) -> p i h m d", i=8, h=2, m=2)
                h0 = 2 * g
                rc4 = RC[:].rearrange("p i (h m) -> p i h m", m=2)
                a = dve(lambda e: e.reciprocal(rc4, ov[:, :, :, :, 16]), a, rcfree)
                a = dve(lambda e: e.tensor_tensor(rc4[:, :, :, 1], rc4[:, :, :, 1],
                        NL[:, h0:h0 + 2].unsqueeze(1).to_broadcast([128, 8, 2]), ALU.mult), a, nl)
                b4 = [128, 8, 2, 16]
                x1 = dve(lambda e: e.tensor_tensor(O1[:], ov[:, :, :, 0, 0:16], rc4[:, :, :, 0].unsqueeze(3).to_broadcast(b4), ALU.mult), a, rcfree)
                x2 = dve(lambda e: e.tensor_tensor(O2[:], ov[:, :, :, 1, 0:16], rc4[:, :, :, 1].unsqueeze(3).to_broadcast(b4), ALU.mult), a, rcfree)
                turn["free"][k] = [x2]
                a = pool(lambda e: e.tensor_tensor(
                    OA[b % 2][:, :, 16 * h0:16 * h0 + 32].rearrange("p i (h d) -> p i h d", d=16), O1[:], O2[:], ALU.add),
                    x1, x2, oread[b % 2])
                rcfree[:] = [a]
                oar.setdefault(b, []).append(a)
                if g == 7:
                    norm(b)

            obfree = [lq_free]

            def norm(b):
                oa = OA[b % 2]
                oh = oa[:].rearrange("p i (h d) -> p (i h) d", d=16)
                sq, ml_ = [], []

                def turns(i):
                    return dve if b == 3 and i % 2 else pool

                def square(i):
                    sq.append(turns(i)(lambda e: e.tensor_tensor(OB[:, i, :], oa[:, i, :], oa[:, i, :], ALU.mult), oar[b], obfree))

                def means():
                    a = dve(lambda e: e.tensor_reduce(MS[:], OB[:].rearrange("p i (h d) -> p (i h) d", d=16), AX, ALU.add), sq)
                    later.append([1, lambda: roots(a)])

                def roots(ob_read):
                    r = rsqrt(MS[:], MS[:], ML[:], 1.0 / 16, 1, ob_read)
                    for i in range(8):
                        later.append([1 + i, lambda i=i: scale(i, r)])
                    later.append([10, lambda: project(b, ml_, bo[b], ob_read)])

                def scale(i, r):
                    ml_.append(turns(i)(lambda e: e.tensor_tensor(oh[:, 16 * i:16 * i + 16, :], oh[:, 16 * i:16 * i + 16, :],
                                    MS[:, 16 * i:16 * i + 16].unsqueeze(2).to_broadcast([128, 16, 16]), ALU.mult), r))
                for i in range(8):
                    later.append([i, lambda i=i: square(i)])
                later.append([9, means])

            def project(b, a, bo, ob_read):
                oa = OA[b % 2]
                OTT = OB[:].rearrange("p i d -> p (i d)").rearrange("p (k s) -> p k s", k=2)
                tt_ = []
                for kk in range(2):
                    k, fr = pair()
                    for i in range(8):
                        a2 = tr(PS[:, 2 * k + i // 4, 128 * (i % 4):128 * (i % 4) + 128], oa[:, i, 128 * kk:128 * kk + 128], [fr, a])
                    a3 = act(lambda e, kk=kk, k=k: e.activation(OTT[:, kk, :], pv(k).rearrange("p k s -> p (k s)"), ACT.Copy), a2, ob_read)
                    turn["free"][k] = [a3]
                    tt_.append(a3)
                oread[b % 2] = [a2]

                def out_product(q):
                    k, fr = pair()
                    for i in range(4):
                        i_ = 4 * q + i
                        o = PS[:, 2 * k + i // 2, 256 * (i % 2):256 * (i % 2) + 256]
                        mm(o, OTT[:, 0, 128 * i_:128 * i_ + 128], WO1[:, 0, :], True, False, [fr, tt_, hn])
                        a3 = mm(o, OTT[:, 1, 128 * i_:128 * i_ + 128], WO1[:, 1, :], False, True)
                    t0 = 8 * b + 4 * q
                    a4 = dve(lambda e: e.tensor_tensor(
                        X[:, t0:t0 + 4, :], X[:, t0:t0 + 4, :], pv(k).rearrange("p k (i d) -> p (k i) d", i=2), ALU.add), a3, bo)
                    turn["free"][k] = [a4]
                    obfree[:] = [a3]
                    xs = [X[:, t0 + i, :] for i in range(4)]
                    st = ln_stats(xs, a4)

                    def rstd():
                        r = ln_rstd(4, st)
                        later.append([1, lambda: apply(r)])

                    def apply(r):
                        xdone[2 * b + q] = ln_apply(xs, xs, r)
                        if q == 0:
                            later.append([0, lambda: out_product(1)])
                    later.append([1, rstd])
                later.append([2, lambda: out_product(0)])

            xdone = {}

            def due():
                now = [x for x in later if x[0] <= 0]
                later[:] = [x for x in later if x[0] > 0]
                for x in later:
                    x[0] -= 1
                for x in now:
                    x[1]()

            for v in range(3):
                fetch(v)
            load_values(0)
            for v in range(-2, 32):
                xs_ = exponentials(v) if v >= 0 else []
                ms_ = maxima(v + 2) if v + 2 < 32 else []
                for s_ in range(24):
                    if xs_:
                        xs_[s_]()
                    if ms_:
                        ms_[s_]()
                    due()
                    if s_ == 2 and v >= 0 and v + 3 < 32:
                        fetch(v + 3)
                if v + 2 < 32:
                    later.append([2 if v >= 0 else 0, lambda v=v, a=cnt["nm"]: subtract_rows(v + 2, a)])
                if v % 8 == 3 and v // 8 + 1 < 4:
                    load_values(v // 8 + 1)
                if v < 0:
                    due()
            for av_ in cnt["pend"]:
                av_()
            pe_end = Q.q["pe"][-1]
            banks[:] = [(SB[z], single["free"][z]) for z in range(3)] + [(7, acc_free[0])]
            c4b.close()

            s5 = s4
            RW2 = s5("RW2", [128, 2, 8])
            COMB = s5("COMB", [128, 32, 8])
            WI = s5("WI", [128, 8, 2, 256])
            WO2 = s5("WO2", [128, 8, 2, 256])
            CH, CL = s5("CH", [128, 2, 8, 256], F32R), s5("CL", [128, 2, 8, 256], F32R)
            XF = [OA[0][:, 4 * i:4 * i + 4, :].rearrange("p i d -> p (i d)").rearrange("p (k s) -> p k s", k=2) for i in range(2)]
            ZH, ZL = s5("ZH", [128, 2, 4096], F32R), s5("ZL", [128, 2, 4096], F32R)
            YO = [OB[:, 4 * i:4 * i + 4, :] for i in range(2)]
            l_rw = Q.dma("sp", RW2[:], A["wr2"], pe_end)
            l_w = [(Q.dma("sp", WI[:, e_], A["wi"][e_], pe_end), Q.dma("sp", WO2[:, e_], A["wo2"][e_], pe_end)) for e_ in range(8)]
            kl, frl = take()
            pl = PS[:, kl, 0:256].rearrange("p (t e) -> p t e", e=8)
            zr, xff, cr = [], [[], []], []

            evs = {}

            def turn_x4(n, k):
                xf = XF[n % 2]
                ev = evs.setdefault(n, [])
                kb, fr = take()
                for i in range(4):
                    a = tr(PS[:, kb, 128 * i:128 * i + 128], X[:, 4 * n + i, 128 * k:128 * k + 128], [fr, xdone[n]])
                a = act(lambda e: e.activation(xf[:, k, :], PS[:, kb, :], ACT.Copy), a, xff[n % 2] if k == 0 else [], oread[0])
                give(kb, a)
                ev.append(a)
                if k == 1:
                    c_ = slice(512 * n, 512 * n + 512)
                    sp_ = split(ZH[:, :, c_], ZL[:, :, c_], xf, act, dve, ev)
                    zr.append(sp_)
                    xff[n % 2] = [sp_]

            def logits(n):
                ev = evs[n]
                for i in range(4):
                    t = 4 * n + i
                    mm(pl[:, t, :], XF[n % 2][:, 0, 128 * i:128 * i + 128], RW2[:, 0, :], True, False, [frl, l_rw, ev])
                    a = mm(pl[:, t, :], XF[n % 2][:, 1, 128 * i:128 * i + 128], RW2[:, 1, :], False, True)
                xff[n % 2].append(a)
                return a

            def join(e_):
                kb, fr = take()
                for m in range(2):
                    for k in range(2):
                        a = mm(PS[:, kb, 256 * m:256 * m + 256], WI[:, e_, k, 128 * m:128 * m + 128], WO2[:, e_, k, :],
                               k == 0, k == 1, [fr, l_w[e_]])
                c_ = split(CH[:, :, e_, :], CL[:, :, e_, :], PS[:, kb, :].rearrange("p (m o) -> p m o", m=2), act, dve, a)
                give(kb, c_)
                cr.append(c_)

            chunks = []
            for n in range(6):
                chunks += [lambda n=n: turn_x4(n, 0), lambda n=n: turn_x4(n, 1), lambda n=n: join(n), lambda n=n: logits(n)]
            chunks += [lambda: join(6), lambda: join(7)]
            for c_ in chunks:
                due()
                c_()
            while later:
                due()
            for k in range(2):
                give(2 * k, turn["free"][k])
                give(2 * k + 1, turn["free"][k])
            for n in (6, 7):
                turn_x4(n, 0)
                turn_x4(n, 1)
            for n in (6, 7):
                a = logits(n)
            OH1b, OH2b, M1b, M2b, _r1, _t8, lg_read, a = choose(pl, "b", c4, a)
            give(kl, lg_read)
            up = lambda m: m.unsqueeze(2).to_broadcast([128, 32, 8])
            a = tt(OH1b[:], OH1b[:], up(M1b[:]), ALU.mult, a)
            a = tt(OH2b[:], OH2b[:], up(M2b[:]), ALU.mult, a)
            rr = tt(COMB[:], OH1b[:], OH2b[:], ALU.add, a)
            stores = []
            for n in range(8):
                for i in range(4):
                    t = 4 * n + i
                    ts = slice(128 * t, 128 * t + 128)
                    a2 = []
                    for ep in range(4):
                        kb, fr = take()
                        for k in range(2):
                            a = mm3(PS[:, kb, :].rearrange("p (e o) -> p e o", e=2), ZH[:, k, ts], ZL[:, k, ts],
                                    CH[:, k, 2 * ep:2 * ep + 2, :], CL[:, k, 2 * ep:2 * ep + 2, :], k == 0, k == 1,
                                    [fr, zr[n], cr[2 * ep], cr[2 * ep + 1]])
                        for j in range(2):
                            e_ = 2 * ep + j
                            a2 = dve(lambda e, kb=kb, t=t, j=j, e_=e_: e.scalar_tensor_tensor(
                                out=X[:, t, :], in0=PS[:, kb, 256 * j:256 * j + 256], scalar=COMB[:, t, e_:e_ + 1],
                                in1=X[:, t, :], op0=ALU.mult, op1=ALU.add), a, rr, a2)
                        give(kb, a2)
                xs = [X[:, 4 * n + i, :] for i in range(4)]
                y = YO[n % 2]
                y_free = stores[n - 2:n - 1] if n > 1 else obfree
                n1 = layernorm(xs, [y[:, i, :] for i in range(4)], a2, y_free)
                stores.append(Q.dma("sp", out[:, 4 * n:4 * n + 4, :], y[:], n1))
            Q.q["sp"].append(Op("sp", None, Q.last()))
        Q.emit(nc, ctx)





def layout(inputs):
    f = lambda n: np.ascontiguousarray(np.asarray(inputs[n]))
    kc = lambda w: np.ascontiguousarray(w.reshape(-1, 128, w.shape[-1]).transpose(1, 0, 2))
    bc = lambda v, n=128: np.ascontiguousarray(np.broadcast_to(v.reshape(1, -1), (n, v.size)))
    a = {}
    x = f("L0_attn_x")
    a["x"] = np.ascontiguousarray(x.reshape(32, 128, 256).transpose(1, 0, 2))
    a["xt"] = np.ascontiguousarray(x.reshape(4, 8, 128, 2, 128).transpose(1, 4, 3, 0, 2).reshape(8, 128, 8, 128))
    a["wq0"], a["wk0"], a["wv0"], a["wg0"] = (kc(f("L0_attn_W" + n)) for n in "qkvg")
    a["wgk1"] = kc(f("L0_attn_Wgk1"))
    a["wgk2"] = np.concatenate([f("L0_attn_Wgk2"), f("L0_attn_bgk2").reshape(1, 256), np.zeros((111, 256), np.float32)])
    a["wo0"] = kc(f("L0_attn_Wo"))
    a["rms"] = bc(np.tile(f("L0_attn_rms_w"), 4))
    a["gam"], a["bet"] = bc(f("L0_ffn_ln_gamma")), bc(f("L0_ffn_ln_beta"))
    i = np.arange(128)
    same = (i[:, None] // 64) == (i[None, :] // 64)
    up = same & (i[:, None] <= i[None, :])
    a["c_tri"] = up.astype(np.float32) / 16
    a["c_msk"] = up.astype(np.int32)
    a["c_idn"] = np.eye(128, dtype=np.float32)
    a["c_eps"] = np.tile(np.array([1e-5, 1e-6, 1.0, 0.0], np.float32), (128, 1))
    a["c_irev"] = np.tile(np.arange(8, 0, -1).astype(np.float32), (128, 1))
    tk = lambda w: kc(np.ascontiguousarray(w.T))
    a["rw"] = tk(f("L0_ffn_router_w"))
    a["we"] = np.stack([np.concatenate([tk(g).reshape(128, -1), tk(d).reshape(128, -1)], 1)
                        for g, d in zip(f("L0_ffn_gate_up_w"), f("L0_ffn_down_w"))])
    a["c_slt"] = (i[:, None] < i[None, :]).astype(np.float32)
    a["c_cnt"] = np.tile(np.concatenate([128.0 * np.arange(32), np.arange(72)]).astype(np.float32), (128, 1))
    a["sgu"], a["sdn"] = tk(f("L0_ffn_shared_gate_up_w")), tk(f("L0_ffn_shared_down_w"))
    other = (np.arange(512) // 16) * 16 + (np.arange(512) + 8) % 16
    w, bb = [], []
    for n in "qk":
        W, v = f("L1_attn_W" + n), f("L1_attn_b" + n)
        w.append(tk(np.concatenate([W, W[other]])))
        bb.append(np.stack([v.reshape(4, 128).T, v[other].reshape(4, 128).T], 1))
    a["wqk"] = np.stack(w)
    a["bqk"] = np.ascontiguousarray(np.stack(bb, 1))
    inv = (1.0 / np.float32(10000.0) ** (np.arange(8, dtype=np.float32) / np.float32(8))).astype(np.float32)
    ang = (np.arange(1024, dtype=np.float32)[None, :] * inv[:, None]).astype(np.float32)
    row = np.arange(128) % 16
    sign = np.where(row < 8, -1.0, 1.0).astype(np.float32)[:, None]
    a["c_cs"] = np.ascontiguousarray(np.stack([np.cos(ang)[row % 8], np.sin(ang)[row % 8] * sign], 1).astype(np.float32))
    later = np.where(i[None, :] > i[:, None], -1e30, 0.0).astype(np.float32)
    a["c_mrc"] = later
    a["wv1"], a["wo1"] = tk(f("L1_attn_Wv")), tk(f("L1_attn_Wo"))
    a["bv"], a["bo"] = bc(f("L1_attn_bv")), bc(f("L1_attn_bo"))
    a["hn"] = np.ascontiguousarray(f("L1_attn_head_norm_w").reshape(2, 128).T)
    a["lam"] = np.ascontiguousarray(np.stack([bc(f("L1_attn_" + n)) for n in ("lq1", "lk1", "lq2", "lk2")], 1))
    a["wr2"] = kc(f("L1_ffn_Wr"))
    a["wi"] = np.stack([tk(w) for w in f("L1_ffn_Wi")])
    a["wo2"] = np.stack([kc(w) for w in f("L1_ffn_Wo")])
    return a


def kernel(**inputs):
    import concourse.bacc as bacc
    from concourse.bass_utils import run_bass_kernel_spmd

    a = layout(inputs)
    nc = bacc.Bacc("TRN2", target_bir_lowering=False, num_devices=1)
    aps = {k: nc.dram_tensor("in_" + k, v.shape, mybir.dt.from_np(v.dtype), kind="ExternalInput").ap() for k, v in a.items()}
    out = nc.dram_tensor("out_0_dram", (128, 32, 256), F32, kind="ExternalOutput").ap()
    program(nc, aps, out)
    r = run_bass_kernel_spmd(nc, [{"in_" + k: v for k, v in a.items()}], core_ids=[0])
    got = r.results[0]["out_0_dram"]
    return np.ascontiguousarray(got.transpose(1, 0, 2).reshape(4, 1024, 256))
```
